# Optimizing a Trainium2 kernel written in Bass

```python
import numpy as np
import jax
import jax.numpy as jnp

def _softmax(x, axis=-1):
    return jax.nn.softmax(x, axis=axis)

def _gelu(x):
    return jax.nn.gelu(x, approximate=True)

def _silu(x):
    return jax.nn.silu(x)

def _sigmoid(x):
    return jax.nn.sigmoid(x)

def _layernorm(x, axis=-1, eps=1e-05):
    m = jnp.mean(x, axis=axis, keepdims=True)
    v = jnp.var(x, axis=axis, keepdims=True)
    return (x - m) / jnp.sqrt(v + eps)

def _scatter_add(tgt, idx, src, axis=0):
    return tgt.at[idx].add(src)

def _segment_sum(src, seg, n):
    return jax.ops.segment_sum(src, seg, n)
kernel_name = 'mk_audio_tower_d4_tok_audfeat256_r4_f5f5a6'

def setup_inputs(seed: int=0):
    np.random.seed(seed)
    _w = jnp.asarray

    def _rec_inputs():
        import jax
        import jax.numpy as jnp
        _rk = jax.random.key(seed)
        x = -0.000520686 + 1.00062 * jax.random.normal(jax.random.fold_in(_rk, 1), (16, 750, 64), jnp.float32)
        return x
    x = _rec_inputs()

    def _L0_tok_setup():
        import jax, jax.numpy as jnp
        import numpy as np
        BATCH = 2
        SEQ = 1024
        D_MODEL = 64
        N_STATE = 64
        DT_RANK = 1
        NUM_LAYERS = 3

        def _ssm_layer(x, A_log, Dp, W_dbc, W_dt, b_dt):
            A = -jnp.exp(A_log)
            dbc = jnp.einsum('ble,ce->blc', x, W_dbc)
            delta, Bm, Cm = jnp.split(dbc, [DT_RANK, DT_RANK + N_STATE], axis=-1)
            delta = jax.nn.softplus(jnp.einsum('blr,er->ble', delta, W_dt) + b_dt)
            dA = jnp.exp(delta[..., None] * A)
            dBx = (delta * x)[..., None] * Bm[:, :, None, :]

            def combine(c1, c2):
                a1, h1 = c1
                a2, h2 = c2
                return (a1 * a2, h1 * a2 + h2)
            _, hs = jax.lax.associative_scan(combine, (dA, dBx), axis=1)
            y = jnp.einsum('blen,bln->ble', hs, Cm)
            return y + Dp * x
        key = jax.random.key(seed)
        kx, kw1, kw2 = jax.random.split(key, 3)
        x = jax.random.normal(kx, (BATCH, SEQ, D_MODEL), dtype=jnp.float32)
        A_log = jnp.broadcast_to(jnp.log(jnp.arange(1, N_STATE + 1, dtype=jnp.float32)), (NUM_LAYERS, D_MODEL, N_STATE)).copy()
        D = jnp.ones((NUM_LAYERS, D_MODEL), dtype=jnp.float32)
        W_dbc = 0.02 * jax.random.normal(kw1, (NUM_LAYERS, DT_RANK + 2 * N_STATE, D_MODEL), dtype=jnp.float32)
        W_dt = 0.02 * jax.random.normal(kw2, (NUM_LAYERS, D_MODEL, DT_RANK), dtype=jnp.float32)
        b_dt = jnp.zeros((NUM_LAYERS, D_MODEL), dtype=jnp.float32)
        return {'x': x, 'A_log': A_log, 'D': D, 'W_dbc': W_dbc, 'W_dt': W_dt, 'b_dt': b_dt}
    _L0_tok_all = _L0_tok_setup()
    _L0_tok_in = {k: v for k, v in _L0_tok_all.items() if k in ('A_log', 'D', 'W_dbc', 'W_dt', 'b_dt')}
    del _L0_tok_all

    def _L0_attn_setup():
        import jax, jax.numpy as jnp
        import numpy as np
        DIM = 64
        HEADS = 4
        HEAD_DIM = DIM // HEADS
        SCALE = HEAD_DIM ** (-0.5)
        key = jax.random.key(seed)
        k_x, k_wqkv, k_bqkv, k_wp, k_bp = jax.random.split(key, 5)
        B, N = (8, 512)
        x = jax.random.normal(k_x, (B, N, DIM), dtype=jnp.float32)
        W_qkv = jax.random.normal(k_wqkv, (3 * DIM, DIM), dtype=jnp.float32) * DIM ** (-0.5)
        b_qkv = jax.random.normal(k_bqkv, (3 * DIM,), dtype=jnp.float32) * 0.02
        W_proj = jax.random.normal(k_wp, (DIM, DIM), dtype=jnp.float32) * DIM ** (-0.5)
        b_proj = jax.random.normal(k_bp, (DIM,), dtype=jnp.float32) * 0.02
        return {'x': x, 'W_qkv': W_qkv, 'b_qkv': b_qkv, 'W_proj': W_proj, 'b_proj': b_proj}
    _L0_attn_all = _L0_attn_setup()
    _L0_attn_in = {k: v for k, v in _L0_attn_all.items() if k in ('W_qkv', 'b_qkv', 'W_proj', 'b_proj')}
    del _L0_attn_all

    def _L0_ffn_setup():
        import jax, jax.numpy as jnp
        import numpy as np
        E = 8
        K = 2
        D = 64
        H = 128
        DOUT = 64
        EPS = 1e-05
        key = jax.random.key(seed)
        ks = jax.random.split(key, 9)
        s = 0.02
        return {'x': jax.random.normal(ks[0], (4, 2048, D), jnp.float32), 'gamma': 1.0 + 0.05 * jax.random.normal(ks[1], (D,), jnp.float32), 'beta': 0.05 * jax.random.normal(ks[2], (D,), jnp.float32), 'Wr': 0.01 * jax.random.normal(ks[3], (D, E), jnp.float32), 'br': jnp.zeros((E,), jnp.float32), 'W1': s * jax.random.normal(ks[4], (E, D, H), jnp.float32), 'b1': s * jax.random.normal(ks[5], (E, H), jnp.float32), 'W2': s * jax.random.normal(ks[6], (E, H, DOUT), jnp.float32), 'b2': s * jax.random.normal(ks[7], (E, DOUT), jnp.float32)}
    _L0_ffn_all = _L0_ffn_setup()
    _L0_ffn_in = {k: v for k, v in _L0_ffn_all.items() if k in ('gamma', 'beta', 'Wr', 'br', 'W1', 'b1', 'W2', 'b2')}
    del _L0_ffn_all

    def _L1_attn_setup():
        import jax, jax.numpy as jnp
        import numpy as np
        B, N, D = (4, 1024, 64)
        key = jax.random.key(seed)
        ks = jax.random.split(key, 7)

        def xavier(k, shape):
            fan_in, fan_out = (shape[1], shape[0])
            a = jnp.sqrt(6.0 / (fan_in + fan_out))
            return jax.random.uniform(k, shape, jnp.float32, -a, a)
        return {'x': jax.random.normal(ks[0], (B, N, D), jnp.float32), 'Wq': xavier(ks[1], (D, D)), 'bq': jnp.zeros((D,), jnp.float32), 'Wk': xavier(ks[2], (D, D)), 'bk': jnp.zeros((D,), jnp.float32), 'Wv': xavier(ks[3], (D, D)), 'bv': jnp.zeros((D,), jnp.float32), 'scale': jnp.asarray([jnp.sqrt(jnp.float32(D))])}
    _L1_attn_all = _L1_attn_setup()
    _L1_attn_in = {k: v for k, v in _L1_attn_all.items() if k in ('Wq', 'bq', 'Wk', 'bk', 'Wv', 'bv', 'scale')}
    del _L1_attn_all

    def _L1_ffn_setup():
        import jax, jax.numpy as jnp
        import numpy as np
        D_MODEL = 64
        EXPERT_DIM = 128
        NUM_EXPERTS = 8
        TOP_K = 2
        SEQ_LEN = 512
        BATCH = 2
        key = jax.random.key(seed)
        ks = jax.random.split(key, 8)
        s = 0.02
        x = jax.random.normal(ks[0], (SEQ_LEN, BATCH, D_MODEL), dtype=jnp.float32)
        Wg = jax.random.normal(ks[1], (D_MODEL, NUM_EXPERTS), dtype=jnp.float32) * s
        bg = jax.random.normal(ks[2], (NUM_EXPERTS,), dtype=jnp.float32) * s
        bias = jnp.zeros((NUM_EXPERTS,), dtype=jnp.float32)
        W1 = jax.random.normal(ks[3], (NUM_EXPERTS, D_MODEL, EXPERT_DIM), dtype=jnp.float32) * s
        b1 = jax.random.normal(ks[4], (NUM_EXPERTS, EXPERT_DIM), dtype=jnp.float32) * s
        W2 = jax.random.normal(ks[5], (NUM_EXPERTS, EXPERT_DIM, D_MODEL), dtype=jnp.float32) * s
        b2 = jax.random.normal(ks[6], (NUM_EXPERTS, D_MODEL), dtype=jnp.float32) * s
        return {'x': x, 'Wg': Wg, 'bg': bg, 'bias': bias, 'W1': W1, 'b1': b1, 'W2': W2, 'b2': b2}
    _L1_ffn_all = _L1_ffn_setup()
    _L1_ffn_in = {k: v for k, v in _L1_ffn_all.items() if k in ('Wg', 'bg', 'bias', 'W1', 'b1', 'W2', 'b2')}
    del _L1_ffn_all

    def _L2_attn_setup():
        import jax, jax.numpy as jnp
        import numpy as np
        NUM_HEADS = 4
        LN_EPS = 1e-05

        def positional_encoding(length, d_model):
            pos = jnp.arange(length, dtype=jnp.float32)[:, None]
            div = jnp.exp(jnp.arange(0, d_model, 2, dtype=jnp.float32) * (-np.log(10000.0) / d_model))
            pe = jnp.zeros((length, d_model), dtype=jnp.float32)
            pe = pe.at[:, 0::2].set(jnp.sin(pos * div))
            pe = pe.at[:, 1::2].set(jnp.cos(pos * div))
            return pe

        def rel_shift(pos_score):
            B, H, S, _ = pos_score.shape
            padded = jnp.pad(pos_score, ((0, 0), (0, 0), (0, 0), (1, 0)))
            padded = padded.reshape(B, H, S + 1, S)
            return padded[:, :, 1:].reshape(B, H, S, S)
        key = jax.random.key(seed)
        ks = jax.random.split(key, 8)
        B, S, D, H = (8, 512, 64, NUM_HEADS)
        dh = D // H
        s = 0.02
        return {'inputs': jax.random.normal(ks[0], (B, S, D), dtype=jnp.float32), 'ln_gamma': jnp.ones((D,), jnp.float32), 'ln_beta': jnp.zeros((D,), jnp.float32), 'Wq': jax.random.normal(ks[1], (D, D), jnp.float32) * s, 'bq': jnp.zeros((D,), jnp.float32), 'Wk': jax.random.normal(ks[2], (D, D), jnp.float32) * s, 'bk': jnp.zeros((D,), jnp.float32), 'Wv': jax.random.normal(ks[3], (D, D), jnp.float32) * s, 'bv': jnp.zeros((D,), jnp.float32), 'Wpos': jax.random.normal(ks[4], (D, D), jnp.float32) * s, 'u_bias': jax.random.normal(ks[5], (H, dh), jnp.float32) * s, 'v_bias': jax.random.normal(ks[6], (H, dh), jnp.float32) * s, 'Wout': jax.random.normal(ks[7], (D, D), jnp.float32) * s, 'bout': jnp.zeros((D,), jnp.float32)}
    _L2_attn_all = _L2_attn_setup()
    _L2_attn_in = {k: v for k, v in _L2_attn_all.items() if k in ('ln_gamma', 'ln_beta', 'Wq', 'bq', 'Wk', 'bk', 'Wv', 'bv', 'Wpos', 'u_bias', 'v_bias', 'Wout', 'bout')}
    del _L2_attn_all

    def _L2_ffn_setup():
        import jax, jax.numpy as jnp
        import numpy as np
        B, S, D, F, E, K = (8, 512, 64, 256, 8, 2)
        key = jax.random.key(seed)
        ks = jax.random.split(key, 10)
        s = 0.02
        return {'x': jax.random.normal(ks[0], (B, S, D), dtype=jnp.float32), 'Wr': jax.random.normal(ks[1], (D, E), dtype=jnp.float32) * s, 'W1s': jax.random.normal(ks[2], (D, F), dtype=jnp.float32) * s, 'b1s': jnp.zeros((F,), dtype=jnp.float32), 'W2s': jax.random.normal(ks[3], (F, D), dtype=jnp.float32) * s, 'b2s': jnp.zeros((D,), dtype=jnp.float32), 'W1p': jax.random.normal(ks[4], (E, D, F), dtype=jnp.float32) * s, 'b1p': jnp.zeros((E, F), dtype=jnp.float32), 'W2p': jax.random.normal(ks[5], (E, F, D), dtype=jnp.float32) * s, 'b2p': jnp.zeros((E, D), dtype=jnp.float32)}
    _L2_ffn_all = _L2_ffn_setup()
    _L2_ffn_in = {k: v for k, v in _L2_ffn_all.items() if k in ('Wr', 'W1s', 'b1s', 'W2s', 'b2s', 'W1p', 'b1p', 'W2p', 'b2p')}
    del _L2_ffn_all

    def _L3_attn_setup():
        import jax, jax.numpy as jnp
        import numpy as np
        D_IN = 64
        D_OUT = 64
        key = jax.random.key(seed)
        kx, kq, kk, kv = jax.random.split(key, 4)
        scale = 1.0 / np.sqrt(D_IN)
        x = jax.random.normal(kx, (4, 1024, D_IN), dtype=jnp.float32)
        Wq = jax.random.uniform(kq, (D_OUT, D_IN), dtype=jnp.float32, minval=-scale, maxval=scale)
        Wk = jax.random.uniform(kk, (D_OUT, D_IN), dtype=jnp.float32, minval=-scale, maxval=scale)
        Wv = jax.random.uniform(kv, (D_OUT, D_IN), dtype=jnp.float32, minval=-scale, maxval=scale)
        return {'x': x, 'Wq': Wq, 'Wk': Wk, 'Wv': Wv}
    _L3_attn_all = _L3_attn_setup()
    _L3_attn_in = {k: v for k, v in _L3_attn_all.items() if k in ('Wq', 'Wk', 'Wv')}
    del _L3_attn_all

    def _L3_ffn_setup():
        import jax, jax.numpy as jnp
        import numpy as np
        B, S, H, F, E, K = (8, 1024, 64, 128, 16, 2)
        EPS = 1e-05
        key = jax.random.key(seed)
        ks = jax.random.split(key, 9)
        sc = 0.02
        return {'x': jax.random.normal(ks[0], (B, S, H), dtype=jnp.float32), 'gate_w': jax.random.normal(ks[1], (H, E), dtype=jnp.float32) * sc, 'gate_b': jnp.zeros((E,), dtype=jnp.float32), 'w1': jax.random.normal(ks[2], (E, H, F), dtype=jnp.float32) * sc, 'b1': jnp.zeros((E, F), dtype=jnp.float32), 'w2': jax.random.normal(ks[3], (E, F, H), dtype=jnp.float32) * sc, 'b2': jnp.zeros((E, H), dtype=jnp.float32), 'gamma': jnp.ones((H,), dtype=jnp.float32), 'beta': jnp.zeros((H,), dtype=jnp.float32)}
    _L3_ffn_all = _L3_ffn_setup()
    _L3_ffn_in = {k: v for k, v in _L3_ffn_all.items() if k in ('gate_w', 'gate_b', 'w1', 'b1', 'w2', 'b2', 'gamma', 'beta')}
    del _L3_ffn_all
    return {'x': x, 'L0_tok_A_log': _L0_tok_in['A_log'], 'L0_tok_D': _L0_tok_in['D'], 'L0_tok_W_dbc': _L0_tok_in['W_dbc'], 'L0_tok_W_dt': _L0_tok_in['W_dt'], 'L0_tok_b_dt': _L0_tok_in['b_dt'], 'L0_attn_W_qkv': _L0_attn_in['W_qkv'], 'L0_attn_b_qkv': _L0_attn_in['b_qkv'], 'L0_attn_W_proj': _L0_attn_in['W_proj'], 'L0_attn_b_proj': _L0_attn_in['b_proj'], 'L0_ffn_gamma': _L0_ffn_in['gamma'], 'L0_ffn_beta': _L0_ffn_in['beta'], 'L0_ffn_Wr': _L0_ffn_in['Wr'], 'L0_ffn_br': _L0_ffn_in['br'], 'L0_ffn_W1': _L0_ffn_in['W1'], 'L0_ffn_b1': _L0_ffn_in['b1'], 'L0_ffn_W2': _L0_ffn_in['W2'], 'L0_ffn_b2': _L0_ffn_in['b2'], 'L1_attn_Wq': _L1_attn_in['Wq'], 'L1_attn_bq': _L1_attn_in['bq'], 'L1_attn_Wk': _L1_attn_in['Wk'], 'L1_attn_bk': _L1_attn_in['bk'], 'L1_attn_Wv': _L1_attn_in['Wv'], 'L1_attn_bv': _L1_attn_in['bv'], 'L1_attn_scale': _L1_attn_in['scale'], 'L1_ffn_Wg': _L1_ffn_in['Wg'], 'L1_ffn_bg': _L1_ffn_in['bg'], 'L1_ffn_bias': _L1_ffn_in['bias'], 'L1_ffn_W1': _L1_ffn_in['W1'], 'L1_ffn_b1': _L1_ffn_in['b1'], 'L1_ffn_W2': _L1_ffn_in['W2'], 'L1_ffn_b2': _L1_ffn_in['b2'], 'L2_attn_ln_gamma': _L2_attn_in['ln_gamma'], 'L2_attn_ln_beta': _L2_attn_in['ln_beta'], 'L2_attn_Wq': _L2_attn_in['Wq'], 'L2_attn_bq': _L2_attn_in['bq'], 'L2_attn_Wk': _L2_attn_in['Wk'], 'L2_attn_bk': _L2_attn_in['bk'], 'L2_attn_Wv': _L2_attn_in['Wv'], 'L2_attn_bv': _L2_attn_in['bv'], 'L2_attn_Wpos': _L2_attn_in['Wpos'], 'L2_attn_u_bias': _L2_attn_in['u_bias'], 'L2_attn_v_bias': _L2_attn_in['v_bias'], 'L2_attn_Wout': _L2_attn_in['Wout'], 'L2_attn_bout': _L2_attn_in['bout'], 'L2_ffn_Wr': _L2_ffn_in['Wr'], 'L2_ffn_W1s': _L2_ffn_in['W1s'], 'L2_ffn_b1s': _L2_ffn_in['b1s'], 'L2_ffn_W2s': _L2_ffn_in['W2s'], 'L2_ffn_b2s': _L2_ffn_in['b2s'], 'L2_ffn_W1p': _L2_ffn_in['W1p'], 'L2_ffn_b1p': _L2_ffn_in['b1p'], 'L2_ffn_W2p': _L2_ffn_in['W2p'], 'L2_ffn_b2p': _L2_ffn_in['b2p'], 'L3_attn_Wq': _L3_attn_in['Wq'], 'L3_attn_Wk': _L3_attn_in['Wk'], 'L3_attn_Wv': _L3_attn_in['Wv'], 'L3_ffn_gate_w': _L3_ffn_in['gate_w'], 'L3_ffn_gate_b': _L3_ffn_in['gate_b'], 'L3_ffn_w1': _L3_ffn_in['w1'], 'L3_ffn_b1': _L3_ffn_in['b1'], 'L3_ffn_w2': _L3_ffn_in['w2'], 'L3_ffn_b2': _L3_ffn_in['b2'], 'L3_ffn_gamma': _L3_ffn_in['gamma'], 'L3_ffn_beta': _L3_ffn_in['beta']}

def reference(x, L0_tok_A_log, L0_tok_D, L0_tok_W_dbc, L0_tok_W_dt, L0_tok_b_dt, L0_attn_W_qkv, L0_attn_b_qkv, L0_attn_W_proj, L0_attn_b_proj, L0_ffn_gamma, L0_ffn_beta, L0_ffn_Wr, L0_ffn_br, L0_ffn_W1, L0_ffn_b1, L0_ffn_W2, L0_ffn_b2, L1_attn_Wq, L1_attn_bq, L1_attn_Wk, L1_attn_bk, L1_attn_Wv, L1_attn_bv, L1_attn_scale, L1_ffn_Wg, L1_ffn_bg, L1_ffn_bias, L1_ffn_W1, L1_ffn_b1, L1_ffn_W2, L1_ffn_b2, L2_attn_ln_gamma, L2_attn_ln_beta, L2_attn_Wq, L2_attn_bq, L2_attn_Wk, L2_attn_bk, L2_attn_Wv, L2_attn_bv, L2_attn_Wpos, L2_attn_u_bias, L2_attn_v_bias, L2_attn_Wout, L2_attn_bout, L2_ffn_Wr, L2_ffn_W1s, L2_ffn_b1s, L2_ffn_W2s, L2_ffn_b2s, L2_ffn_W1p, L2_ffn_b1p, L2_ffn_W2p, L2_ffn_b2p, L3_attn_Wq, L3_attn_Wk, L3_attn_Wv, L3_ffn_gate_w, L3_ffn_gate_b, L3_ffn_w1, L3_ffn_b1, L3_ffn_w2, L3_ffn_b2, L3_ffn_gamma, L3_ffn_beta):
    import jax
    import jax.numpy as jnp

    def _L0_tok_ref(x, A_log, D, W_dbc, W_dt, b_dt):
        import jax, jax.numpy as jnp
        import numpy as np
        BATCH = 2
        SEQ = 1024
        D_MODEL = 64
        N_STATE = 64
        DT_RANK = 1
        NUM_LAYERS = 3

        def _ssm_layer(x, A_log, Dp, W_dbc, W_dt, b_dt):
            A = -jnp.exp(A_log)
            dbc = jnp.einsum('ble,ce->blc', x, W_dbc)
            delta, Bm, Cm = jnp.split(dbc, [DT_RANK, DT_RANK + N_STATE], axis=-1)
            delta = jax.nn.softplus(jnp.einsum('blr,er->ble', delta, W_dt) + b_dt)
            dA = jnp.exp(delta[..., None] * A)
            dBx = (delta * x)[..., None] * Bm[:, :, None, :]

            def combine(c1, c2):
                a1, h1 = c1
                a2, h2 = c2
                return (a1 * a2, h1 * a2 + h2)
            _, hs = jax.lax.associative_scan(combine, (dA, dBx), axis=1)
            y = jnp.einsum('blen,bln->ble', hs, Cm)
            return y + Dp * x
        for i in range(NUM_LAYERS):
            x = _ssm_layer(x, A_log[i], D[i], W_dbc[i], W_dt[i], b_dt[i])
            if i < NUM_LAYERS - 1:
                b, l, d = x.shape
                x = x[:, :l // 2 * 2].reshape(b, l // 2, 2, d).mean(axis=2)
        return x

    def _L0_attn_ref(x, W_qkv, b_qkv, W_proj, b_proj):
        import jax, jax.numpy as jnp
        import numpy as np
        DIM = 64
        HEADS = 4
        HEAD_DIM = DIM // HEADS
        SCALE = HEAD_DIM ** (-0.5)
        B, N, C = x.shape
        h, d = (HEADS, HEAD_DIM)
        qkv = jnp.einsum('bnc,oc->bno', x, W_qkv) + b_qkv
        qkv = qkv.reshape(B, N, 3, h, d).transpose(2, 0, 3, 1, 4)
        q, k, v = (qkv[0], qkv[1], qkv[2])
        attn = jnp.einsum('bhnd,bhmd->bhnm', q, k) * SCALE
        attn = jax.nn.softmax(attn, axis=-1)
        out = jnp.einsum('bhnm,bhmd->bhnd', attn, v)
        out = out.transpose(0, 2, 1, 3).reshape(B, N, C)
        return jnp.einsum('bnc,oc->bno', out, W_proj) + b_proj

    def _L0_ffn_ref(x, gamma, beta, Wr, br, W1, b1, W2, b2):
        import jax, jax.numpy as jnp
        import numpy as np
        E = 8
        K = 2
        D = 64
        H = 128
        DOUT = 64
        EPS = 1e-05
        mu = jnp.mean(x, axis=-1, keepdims=True)
        var = jnp.mean(jnp.square(x - mu), axis=-1, keepdims=True)
        xn = (x - mu) * jax.lax.rsqrt(var + EPS) * gamma + beta
        logits = jnp.einsum('bsd,de->bse', xn, Wr) + br
        top_vals, top_idx = jax.lax.top_k(logits, K)
        w = jax.nn.softmax(top_vals, axis=-1)
        w_full = jnp.einsum('bsk,bske->bse', w, jax.nn.one_hot(top_idx, E, dtype=w.dtype))
        y = jnp.zeros(x.shape[:-1] + (DOUT,), x.dtype)
        for e in range(E):
            h = jax.nn.gelu(jnp.einsum('bsd,dh->bsh', xn, W1[e]) + b1[e], approximate=False)
            y_e = jnp.einsum('bsh,hd->bsd', h, W2[e]) + b2[e]
            y = y + y_e * w_full[..., e, None]
        return y

    def _L1_attn_ref(x, Wq, bq, Wk, bk, Wv, bv, scale):
        import jax, jax.numpy as jnp
        import numpy as np
        B, N, D = (4, 1024, 64)
        q = jnp.einsum('bnd,ed->bne', x, Wq) + bq
        k = jnp.einsum('bnd,ed->bne', x, Wk) + bk
        v = jnp.einsum('bnd,ed->bne', x, Wv) + bv
        scores = jnp.einsum('bqd,bkd->bqk', q, k) / scale[0]
        attn = jax.nn.softmax(scores, axis=-1)
        out = jnp.einsum('bqk,bkd->bqd', attn, v)
        return out

    def _L1_ffn_ref(x, Wg, bg, bias, W1, b1, W2, b2):
        import jax, jax.numpy as jnp
        import numpy as np
        D_MODEL = 64
        EXPERT_DIM = 128
        NUM_EXPERTS = 8
        TOP_K = 2
        SEQ_LEN = 512
        BATCH = 2
        x_flat = x.reshape(-1, D_MODEL)
        gate_logits = x_flat @ Wg + bg + bias
        topk_vals, topk_idx = jax.lax.top_k(gate_logits, TOP_K)
        topk_w = jax.nn.softmax(topk_vals, axis=-1)
        combine = (jax.nn.one_hot(topk_idx, NUM_EXPERTS, dtype=x.dtype) * topk_w[..., None]).sum(axis=1)
        h = jax.nn.relu(jnp.einsum('td,edh->teh', x_flat, W1) + b1)
        y = jnp.einsum('teh,ehd->ted', h, W2) + b2
        out = jnp.einsum('ted,te->td', y, combine)
        return out.reshape(x.shape)

    def _L2_attn_ref(inputs, ln_gamma, ln_beta, Wq, bq, Wk, bk, Wv, bv, Wpos, u_bias, v_bias, Wout, bout):
        import jax, jax.numpy as jnp
        import numpy as np
        NUM_HEADS = 4
        LN_EPS = 1e-05

        def positional_encoding(length, d_model):
            pos = jnp.arange(length, dtype=jnp.float32)[:, None]
            div = jnp.exp(jnp.arange(0, d_model, 2, dtype=jnp.float32) * (-np.log(10000.0) / d_model))
            pe = jnp.zeros((length, d_model), dtype=jnp.float32)
            pe = pe.at[:, 0::2].set(jnp.sin(pos * div))
            pe = pe.at[:, 1::2].set(jnp.cos(pos * div))
            return pe

        def rel_shift(pos_score):
            B, H, S, _ = pos_score.shape
            padded = jnp.pad(pos_score, ((0, 0), (0, 0), (0, 0), (1, 0)))
            padded = padded.reshape(B, H, S + 1, S)
            return padded[:, :, 1:].reshape(B, H, S, S)
        B, S, D = inputs.shape
        H = NUM_HEADS
        dh = D // H
        mu = jnp.mean(inputs, axis=-1, keepdims=True)
        var = jnp.mean(jnp.square(inputs - mu), axis=-1, keepdims=True)
        x = (inputs - mu) / jnp.sqrt(var + LN_EPS) * ln_gamma + ln_beta
        pe = positional_encoding(S, D)
        q = (x @ Wq + bq).reshape(B, S, H, dh)
        k = (x @ Wk + bk).reshape(B, S, H, dh)
        v = (x @ Wv + bv).reshape(B, S, H, dh)
        p = (pe @ Wpos).reshape(S, H, dh)
        content_score = jnp.einsum('bshd,bthd->bhst', q + u_bias, k)
        pos_score = jnp.einsum('bshd,thd->bhst', q + v_bias, p)
        pos_score = rel_shift(pos_score)
        score = (content_score + pos_score) / np.sqrt(D).astype(np.float32)
        attn = jax.nn.softmax(score, axis=-1)
        ctx = jnp.einsum('bhst,bthd->bshd', attn, v).reshape(B, S, D)
        return ctx @ Wout + bout

    def _L2_ffn_ref(x, Wr, W1s, b1s, W2s, b2s, W1p, b1p, W2p, b2p):
        import jax, jax.numpy as jnp
        import numpy as np
        B, S, D, F, E, K = (8, 512, 64, 256, 8, 2)
        gelu = lambda t: jax.nn.gelu(t, approximate=False)
        shared = gelu(x @ W1s + b1s) @ W2s + b2s
        rw = jax.nn.softmax(x @ Wr, axis=-1)
        topw, topi = jax.lax.top_k(rw, K)
        topw = topw / jnp.sum(topw, axis=-1, keepdims=True)
        mask = jnp.sum(jax.nn.one_hot(topi, E, dtype=topw.dtype) * topw[..., None], axis=-2)
        h = gelu(jnp.einsum('bsd,edf->bsef', x, W1p) + b1p)
        priv = jnp.einsum('bsef,efd->bsed', h, W2p) + b2p
        routed = jnp.einsum('bsed,bse->bsd', priv, mask)
        return shared + routed

    def _L3_attn_ref(x, Wq, Wk, Wv):
        import jax, jax.numpy as jnp
        import numpy as np
        D_IN = 64
        D_OUT = 64
        q = jnp.einsum('bsi,oi->bso', x, Wq)
        k = jnp.einsum('bsi,oi->bso', x, Wk)
        v = jnp.einsum('bsi,oi->bso', x, Wv)
        d_k = k.shape[-1]
        scores = jnp.einsum('bqd,bkd->bqk', q, k) / jnp.sqrt(jnp.asarray(d_k, q.dtype))
        weights = jax.nn.softmax(scores, axis=-1)
        return jnp.einsum('bqk,bkd->bqd', weights, v)

    def _L3_ffn_ref(x, gate_w, gate_b, w1, b1, w2, b2, gamma, beta):
        import jax, jax.numpy as jnp
        import numpy as np
        B, S, H, F, E, K = (8, 1024, 64, 128, 16, 2)
        EPS = 1e-05
        gate_logits = x @ gate_w + gate_b
        topk_vals, topk_idx = jax.lax.top_k(gate_logits, K)
        topk_w = jax.nn.softmax(topk_vals, axis=-1)
        h = jax.nn.relu(jnp.einsum('bsh,ehf->bsef', x, w1) + b1)
        expert_out = jnp.einsum('bsef,efh->bseh', h, w2) + b2
        sel = jnp.take_along_axis(expert_out, topk_idx[:, :, :, None], axis=2)
        moe = jnp.sum(topk_w[..., None] * sel, axis=2)
        y = x + moe
        mu = jnp.mean(y, axis=-1, keepdims=True)
        var = jnp.var(y, axis=-1, keepdims=True)
        return (y - mu) / jnp.sqrt(var + EPS) * gamma + beta
    h = _L0_tok_ref(x, L0_tok_A_log, L0_tok_D, L0_tok_W_dbc, L0_tok_W_dt, L0_tok_b_dt)
    h = h + _L0_attn_ref(_layernorm(h, axis=-1), L0_attn_W_qkv, L0_attn_b_qkv, L0_attn_W_proj, L0_attn_b_proj)
    h = h + _L0_ffn_ref(_layernorm(h, axis=-1), L0_ffn_gamma, L0_ffn_beta, L0_ffn_Wr, L0_ffn_br, L0_ffn_W1, L0_ffn_b1, L0_ffn_W2, L0_ffn_b2)
    h = h + _L1_attn_ref(_layernorm(h, axis=-1), L1_attn_Wq, L1_attn_bq, L1_attn_Wk, L1_attn_bk, L1_attn_Wv, L1_attn_bv, L1_attn_scale)
    h = h + _L1_ffn_ref(_layernorm(h, axis=-1), L1_ffn_Wg, L1_ffn_bg, L1_ffn_bias, L1_ffn_W1, L1_ffn_b1, L1_ffn_W2, L1_ffn_b2)
    h = h + _L2_attn_ref(_layernorm(h, axis=-1), L2_attn_ln_gamma, L2_attn_ln_beta, L2_attn_Wq, L2_attn_bq, L2_attn_Wk, L2_attn_bk, L2_attn_Wv, L2_attn_bv, L2_attn_Wpos, L2_attn_u_bias, L2_attn_v_bias, L2_attn_Wout, L2_attn_bout)
    h = h + _L2_ffn_ref(_layernorm(h, axis=-1), L2_ffn_Wr, L2_ffn_W1s, L2_ffn_b1s, L2_ffn_W2s, L2_ffn_b2s, L2_ffn_W1p, L2_ffn_b1p, L2_ffn_W2p, L2_ffn_b2p)
    h = h + _L3_attn_ref(_layernorm(h, axis=-1), L3_attn_Wq, L3_attn_Wk, L3_attn_Wv)
    h = h + _L3_ffn_ref(_layernorm(h, axis=-1), L3_ffn_gate_w, L3_ffn_gate_b, L3_ffn_w1, L3_ffn_b1, L3_ffn_w2, L3_ffn_b2, L3_ffn_gamma, L3_ffn_beta)
    return h

_drawn_inputs = setup_inputs


def setup_inputs(seed=0):
    import zlib

    import numpy as np

    out = dict(_drawn_inputs(seed))
    spreads = {'L0_tok_D': (1.0, 0.2),
     'L0_tok_b_dt': (0.0, 0.418),
     'L0_ffn_br': (0.0, 0.1),
     'L1_attn_bq': (0.0, 0.1),
     'L1_attn_bk': (0.0, 2.0),
     'L1_attn_bv': (0.0, 0.1),
     'L1_ffn_bias': (0.0, 0.274),
     'L2_attn_ln_gamma': (1.0, 0.6),
     'L2_attn_ln_beta': (0.0, 0.67),
     'L2_attn_bq': (0.0, 0.8),
     'L2_attn_bk': (0.0, 2.0),
     'L2_attn_bv': (0.0, 0.1),
     'L2_attn_bout': (0.0, 0.1),
     'L2_ffn_b1s': (0.0, 0.1),
     'L2_ffn_b2s': (0.0, 0.1),
     'L2_ffn_b1p': (0.0, 0.412),
     'L2_ffn_b2p': (0.0, 0.1),
     'L3_ffn_gate_b': (0.0, 0.1),
     'L3_ffn_b1': (0.0, 0.8),
     'L3_ffn_b2': (0.0, 0.1),
     'L3_ffn_gamma': (1.0, 0.2),
     'L3_ffn_beta': (0.0, 0.1)}
    factors = {'L0_tok_A_log': 3.846,
     'L0_tok_W_dt': 8.0,
     'L0_ffn_gamma': 8.0,
     'L0_ffn_beta': 6.786,
     'L0_ffn_Wr': 2.67,
     'L0_ffn_b1': 5.069,
     'L1_ffn_bg': 4.489,
     'L1_ffn_b1': 7.684,
     'L2_attn_Wq': 8.0,
     'L2_attn_Wk': 8.0,
     'L2_attn_Wpos': 8.0,
     'L2_attn_u_bias': 22.523,
     'L2_attn_v_bias': 64.0,
     'L3_ffn_w1': 6.071,
     'L3_ffn_w2': 4.432}
    for name, (base, spread) in spreads.items():
        noise = np.random.default_rng([zlib.crc32(name.encode()), seed]).standard_normal(out[name].shape)
        drawn = base * np.exp(spread * noise) if base else spread * noise
        out[name] = jnp.asarray(drawn.astype(out[name].dtype))
    for name, factor in factors.items():
        out[name] = (out[name] * factor).astype(out[name].dtype)
    return out
```

```python
from contextlib import ExitStack

import concourse.bass as bass
from concourse import mybir

F32 = mybir.dt.float32
BF16 = mybir.dt.bfloat16
ACT = mybir.ActivationFunctionType
ALU = mybir.AluOpType
AX = mybir.AxisListType
ds = bass.ds

BATCH, SEQ, D, NSTATE, SSM_LAYERS = 16, 750, 64, 64, 3
HALF = BATCH // 2
LENS = [SEQ, SEQ // 2, SEQ // 4]
TOK = LENS[-1]
COLS = HALF * TOK
SLACK = 8
PIECE = 512

SSM_WD, SSM_WB, SSM_WC = 0, 128, 384
SSM_VEC, SSM_A = 640, 643
SSM_COLS = 675
PAIRS = D // 2
YSEL = SSM_LAYERS * SSM_COLS
SSM_W = YSEL + 128


def pieces(width):
    return [(a, min(a + PIECE, width)) for a in range(0, width, PIECE)]


INPUT_DMAS = 32


def selector_of(pool, out, width, selected):
    pool.memset(out[:, :], 0.0).then_inc(selected, 1)
    pool.wait_ge(selected, 1)
    for s in range(3):
        view = out[32 * s:32 * s + 32, :].rearrange("p (c n) -> p c n", n=width)
        pool.affine_select(out=view, in_=view, compare_op=ALU.not_equal, fill=1.0, base=0,
                           pattern=[[-1, 32], [0, width]], channel_multiplier=1).then_inc(selected, 1)


def settle(eng, value):
    return value if isinstance(value, int) else eng.snap(eng.to_reg(value))


class Phases:

    def __init__(self, nc):
        self.nc, self.held, self.before, self.now = nc, [], [], []

    def open(self, phase):
        if len(self.held) == 2:
            self.held.pop(0).close()
        self.held.append(ExitStack())
        self.before, self.now, self.phase = self.now, [], phase
        return self

    def __call__(self, name):
        s = self.held[-1].enter_context(self.nc.semaphore(f"{self.phase}_{name}"))
        self.now.append(s)
        return s

    def clear_before(self, block):
        before = self.before

        @block.sync
        def _(sp):
            for s in before:
                sp.sem_clear(s)


def ssm_prep(nc, phases, inputs_loaded, layer, L, x, weights, b_rep, c_rep, split_dram):
    seqs = max(1, SEQ // L)
    width = seqs * L
    groups = HALF // seqs
    base = layer * SSM_COLS
    w = lambda a, n: weights[:, base + a:base + a + n]
    with ExitStack() as ctx:
        sb = lambda name, shape, dt: ctx.enter_context(nc.sbuf_tensor(f"prep{layer}_{name}", shape, dt))
        sem = phases.open(f"prep{layer}")
        raw = [ctx.enter_context(nc.psum_tensor(f"raw{layer}_{p}", [128, 1024], F32)) for p in range(2)]
        bc = [ctx.enter_context(nc.psum_tensor(f"bc{layer}_{p}", [128, 1024], F32)) for p in range(2)]
        z = [sb(f"z{p}", [128, width], F32) for p in range(2)]
        soft = [sb(f"soft{p}", [128, width], F32) for p in range(2)]
        val = [[sb(f"val{t}{p}", [128, width], F32) for p in range(2)] for t in range(2)]
        rest = [[sb(f"rest{t}{p}", [128, width], F32) for p in range(2)] for t in range(2)]
        part = [[[sb(f"part{t}{s}{p}", [128, width], BF16) for p in range(2)] for s in range(3)] for t in range(2)]
        raw_ready, z_ready, soft_ready, soft_step = sem("raw_ready"), sem("z_ready"), sem("soft_ready"), sem("soft_step")
        bc_ready, bc_even, bc_odd = sem("bc_ready"), sem("bc_even"), sem("bc_odd")
        val_ready, cast_done, sub_done, stored = sem("val_ready"), sem("cast_done"), sem("sub_done"), sem("stored")

        with nc.Block() as block:
            phases.clear_before(block)

            @block.tensor
            def _(pe):
                with pe.Fori(0, groups // 2) as i:
                    for p in range(2):
                        g = 2 * i + p
                        pe.wait_ge(z_ready, SLACK + 2 * i)
                        for a, b in pieces(width):
                            mm = pe.matmul(raw[p][:, a:b], w(SSM_WD, 128), x[:, ds(g * width + a, b - a)],
                                           start=True, stop=True)
                        mm.then_inc(raw_ready, 1)
                        for q in range(4):
                            pe.wait_ge(bc_even if q % 2 == 0 else bc_odd, SLACK + 2 * g + q // 2)
                            for a, b in pieces(width):
                                mm = pe.matmul(bc[q % 2][:, a:b], w(SSM_WB + 128 * q, 128),
                                               x[:, ds(g * width + a, b - a)], start=True, stop=True)
                            mm.then_inc(bc_ready, 1)

            def target(q):
                return (b_rep, c_rep)[q // 2], (q % 2) * HALF * L

            @block.vector
            def _(dve):
                with dve.Fori(0, groups // 2) as i:
                    for p in range(2):
                        g = 2 * i + p
                        dve.wait_ge(raw_ready, g + 1)
                        dve.wait_ge(val_ready, SLACK + 2 * g)
                        dve.tensor_scalar(z[p][:, :], raw[p][:, 0:width], w(SSM_VEC, 1), w(SSM_VEC + 1, 1),
                                          ALU.mult, ALU.add).then_inc(z_ready, 1)
                        for q in (1, 3):
                            dst, off = target(q)
                            dve.wait_ge(bc_ready, 4 * g + q + 1)
                            dve.tensor_copy(dst[:, ds(off + g * width, width)], bc[1][:, 0:width]).then_inc(bc_odd, 1)
                        dve.wait_ge(soft_ready, g + 1)
                        dve.wait_ge(cast_done, SLACK + 4 * (g - p))
                        dve.wait_ge(sub_done, SLACK + 4 * (g - p))
                        dve.scalar_tensor_tensor(val[0][p][:, :], z[p][:, :], 0.0, soft[p][:, :],
                                                 ALU.max, ALU.add).then_inc(val_ready, 1)
                        dve.wait_ge(val_ready, SLACK + 2 * g + 1)
                        dve.tensor_tensor(val[1][p][:, :], val[0][p][:, :], x[:, ds(g * width, width)],
                                          ALU.mult).then_inc(val_ready, 1)

            @block.scalar
            def _(act):
                with act.Fori(0, groups // 2) as i:
                    for p in range(2):
                        g = 2 * i + p
                        act.wait_ge(z_ready, SLACK + g + 1)
                        act.activation(soft[p][:, :], z[p][:, :], ACT.Abs).then_inc(soft_step, 1)
                        act.wait_ge(soft_step, 2 * g + 1)
                        act.activation(soft[p][:, :], soft[p][:, :], ACT.Exp, scale=-1.0).then_inc(soft_step, 1)
                        act.wait_ge(soft_step, 2 * g + 2)
                        act.activation(soft[p][:, :], soft[p][:, :], ACT.Ln, bias=1.0).then_inc(soft_ready, 1)
                        for q in (0, 2):
                            dst, off = target(q)
                            projected = settle(act, 4 * g + q + 1)
                            act.wait_ge(inputs_loaded, INPUT_DMAS)
                            act.wait_ge(bc_ready, projected)
                            act.activation(dst[:, ds(off + g * width, width)], bc[0][:, 0:width],
                                           ACT.Copy).then_inc(bc_even, 1)
                        act.wait_ge(stored, SLACK + 192 * (g - p))
                        for t in range(2):
                            act.wait_ge(val_ready, SLACK + 2 * g + t + 1)
                            act.activation(part[t][0][p][:, :], val[t][p][:, :], ACT.Copy).then_inc(cast_done, 1)
                        for t in range(2):
                            act.wait_ge(sub_done, SLACK + 4 * g + t + 1)
                            act.activation(part[t][1][p][:, :], rest[t][p][:, :], ACT.Copy).then_inc(cast_done, 1)

            @block.gpsimd
            def _(pool):
                for free in (z_ready, bc_even, bc_odd, val_ready, cast_done, sub_done, stored):
                    pool.sem_inc(free, SLACK)
                with pool.Fori(0, groups // 2) as i:
                    for p in range(2):
                        g = 2 * i + p
                        for t in range(2):
                            pool.wait_ge(cast_done, SLACK + 4 * g + t + 1)
                            pool.tensor_tensor(rest[t][p][:, :], val[t][p][:, :], part[t][0][p][:, :],
                                               ALU.subtract).then_inc(sub_done, 1)
                        for t in range(2):
                            pool.wait_ge(cast_done, SLACK + 4 * g + 2 + t + 1)
                            pool.tensor_tensor(part[t][2][p][:, :], rest[t][p][:, :], part[t][1][p][:, :],
                                               ALU.subtract).then_inc(sub_done, 1)

            @block.sync
            def _(sp):
                with sp.Fori(0, groups // 2) as i:
                    for p in range(2):
                        g = 2 * i + p
                        sp.wait_ge(sub_done, SLACK + 4 * g + 4)
                        for t in range(2):
                            for s in range(3):
                                for h in range(2):
                                    dst = split_dram[t, s, ds(g + h * groups, 1)].rearrange("a e w -> (a e) w")
                                    sp.dma_start(dst, part[t][s][p][64 * h:64 * h + 64, :]).then_inc(stored, 16)
                sp.wait_ge(stored, SLACK + 192 * groups)


def ssm_scan(nc, phases, inputs_loaded, layer, L, weights, selector, a_neg, b_rep, c_rep, split_dram, y_dram):
    seqs = max(1, SEQ // L)
    width = seqs * L
    turns = 2 * HALF // seqs
    with ExitStack() as ctx:
        sb = lambda name, shape, dt: ctx.enter_context(nc.sbuf_tensor(f"scan{layer}_{name}", shape, dt))
        sem = phases.open(f"scan{layer}")
        decay = [ctx.enter_context(nc.psum_tensor(f"decay{layer}_{p}", [128, 1024], F32)) for p in range(2)]
        spread = ctx.enter_context(nc.psum_tensor(f"spread{layer}", [128, 1024], F32))
        y_sum = ctx.enter_context(nc.psum_tensor(f"ysum{layer}", [64, 1024], F32))
        stack = [[sb(f"stack{t}{e}", [96, width], BF16) for e in range(2)] for t in range(2)]
        dbx = [sb(f"dbx{p}", [128, width], F32) for p in range(4)]
        state = [sb(f"state{p}", [128, width], F32) for p in range(2)]
        weighed = [sb(f"weighed{p}", [128, width], F32) for p in range(2)]
        y_out = sb("y_out", [64, width], F32)
        loaded = [sem(f"loaded{e}") for e in range(2)]
        delta_ready, spread_ready, decay_ready = sem("delta_ready"), sem("spread_ready"), sem("decay_ready")
        dbx_ready, scanned, weighed_ready = sem("dbx_ready"), sem("scanned"), sem("weighed_ready")
        y_added, y_copied, y_stored = sem("y_added"), sem("y_copied"), sem("y_stored")

        with nc.Block() as block:
            phases.clear_before(block)

            @block.sync
            def _(sp):
                def load(j, e, first):
                    if not first:
                        sp.wait_ge(delta_ready, PAIRS * (j - 1) + 16 * (e + 1))
                        sp.wait_ge(spread_ready, PAIRS * (j - 1) + 16 * (e + 1))
                    for t in range(2):
                        for s in range(3):
                            sp.dma_start(stack[t][e][32 * s:32 * s + 32, :],
                                         split_dram[t, s, ds(j, 1), 32 * e:32 * e + 32, :]
                                         .rearrange("a e w -> (a e) w")).then_inc(loaded[e], 16)

                def store(j):
                    sp.wait_ge(y_copied, SLACK + j + 1)
                    sp.dma_start(y_dram[ds(j, 1)].rearrange("a e w -> (a e) w"), y_out[:, :]).then_inc(y_stored, 16)

                load(0, 0, True)
                load(0, 1, True)
                with sp.Fori(0, turns - 1) as i:
                    load(i + 1, 0, False)
                    load(i + 1, 1, False)
                    store(i)
                store(turns - 1)
                sp.wait_ge(y_stored, SLACK + 16 * turns)

            @block.tensor
            def _(pe):
                def spread_delta(j, k):
                    e, u = k // 16, PAIRS * j + k
                    if not (isinstance(j, int) and j == 0 and k < 2):
                        pe.wait_ge(scanned, u - 1)
                    for a, b in pieces(width):
                        mm = pe.matmul(decay[k % 2][:, a:b], selector[:, 128 * (k % 16):128 * (k % 16) + 128],
                                       stack[0][e][:, a:b], start=True, stop=True)
                    mm.then_inc(delta_ready, 1)

                def spread_dx(j, k):
                    e, u = k // 16, PAIRS * j + k
                    if k % 16 == 0:
                        pe.wait_ge(loaded[e], 96 * (j + 1))
                    if not (isinstance(j, int) and u == 0):
                        pe.wait_ge(dbx_ready, u)
                    for a, b in pieces(width):
                        mm = pe.matmul(spread[:, a:b], selector[:, 128 * (k % 16):128 * (k % 16) + 128],
                                       stack[1][e][:, a:b], start=True, stop=True)
                    mm.then_inc(spread_ready, 1)

                def sum_states(j, k, part):
                    u = PAIRS * j + k
                    if part == 0:
                        pe.wait_ge(weighed_ready, u + 1)
                        if k == 0:
                            pe.wait_ge(y_copied, SLACK + j)
                    lhs = weights[:, YSEL + 62 - 2 * k:YSEL + 126 - 2 * k]
                    a, b = pieces(width)[part]
                    mm = pe.matmul(y_sum[:, a:b], lhs, weighed[k % 2][:, a:b], start=(k == 0), stop=(k == PAIRS - 1))
                    if part == 1:
                        mm.then_inc(y_added, 1)

                def step(j, k, first=False, last=False):
                    nj, nk = (j, k + 1) if k + 1 < PAIRS else (j + 1, 0)
                    sj, sk = (j, k - 2) if k >= 2 else (j - 1, k - 2 + PAIRS)
                    sums, spreads = not (first and k < 2), not (last and k == PAIRS - 1)
                    if spreads:
                        spread_dx(nj, nk)
                    if k == 2:
                        spread_delta(nj, nk)
                    if sums:
                        sum_states(sj, sk, 0)
                    if k != 2 and spreads:
                        spread_delta(nj, nk)
                    if sums:
                        sum_states(sj, sk, 1)

                spread_dx(0, 0)
                spread_delta(0, 0)
                for k in range(2):
                    step(0, k, first=True)
                with pe.Fori(0, turns - 1) as i:
                    for k in range(2, PAIRS):
                        step(i, k)
                    for k in range(2):
                        step(i + 1, k)
                for k in range(2, PAIRS):
                    step(turns - 1, k, last=True)
                for k in (PAIRS - 2, PAIRS - 1):
                    for part in range(2):
                        sum_states(turns - 1, k, part)

            @block.scalar
            def _(act):
                def decays(j, ks):
                    for k in ks:
                        act.wait_ge(delta_ready, PAIRS * j + k + 1)
                        act.activation(decay[k % 2][:, 0:width], decay[k % 2][:, 0:width], ACT.Exp,
                                       scale=a_neg[:, PAIRS * layer + k:PAIRS * layer + k + 1]).then_inc(decay_ready, 1)

                def copy_sums(j, first):
                    act.wait_ge(y_added, PAIRS * (j + 1))
                    if not first:
                        act.wait_ge(y_stored, SLACK + 16 * j)
                    act.activation(y_out[:, :], y_sum[:, 0:width], ACT.Copy).then_inc(y_copied, 1)

                decays(0, range(3))
                with act.Fori(0, turns - 1) as i:
                    decays(i, range(3, PAIRS))
                    decays(i + 1, range(3))
                    copy_sums(i, False)
                decays(turns - 1, range(3, PAIRS))
                copy_sums(turns - 1, False)

            @block.vector
            def _(dve):
                def product(j, k):
                    dve.wait_ge(spread_ready, PAIRS * j + k + 1)
                    dve.tensor_tensor(dbx[k % 4][:, :], spread[:, 0:width], b_rep[:, ds(j * width, width)],
                                      ALU.mult).then_inc(dbx_ready, 1)

                def scan(j, k):
                    u = PAIRS * j + k
                    dve.wait_ge(decay_ready, u + 1)
                    dve.wait_ge(dbx_ready, u + 1)
                    if not (isinstance(j, int) and j == 0 and k < 2):
                        dve.wait_ge(weighed_ready, u - 1)
                    for s in range(seqs):
                        sl = slice(s * L, (s + 1) * L)
                        op = dve.tensor_tensor_scan(state[k % 2][:, sl], decay[k % 2][:, sl], dbx[k % 4][:, sl],
                                                    0.0, ALU.mult, ALU.add)
                    op.then_inc(scanned, 1)

                def turn(j, first, last):
                    for k in range(PAIRS):
                        if k + 1 < PAIRS:
                            product(j, k + 1)
                        elif not last:
                            product(j + 1, 0)
                        scan(j, k)

                product(0, 0)
                turn(0, True, False)
                with dve.Fori(1, turns - 1) as i:
                    turn(i, False, False)
                turn(turns - 1, False, True)

            @block.gpsimd
            def _(pool):
                def weigh(j, k):
                    u = PAIRS * j + k
                    here, before = settle(pool, u + 1), settle(pool, u - 1)
                    pool.wait_ge(inputs_loaded, INPUT_DMAS)
                    pool.wait_ge(scanned, here)
                    if not (isinstance(j, int) and j == 0 and k < 2):
                        pool.wait_ge(y_added, before)
                    pool.tensor_tensor(weighed[k % 2][:, :], state[k % 2][:, :], c_rep[:, ds(j * width, width)],
                                       ALU.mult).then_inc(weighed_ready, 1)

                pool.sem_inc(y_copied, SLACK)
                pool.sem_inc(y_stored, SLACK)
                for k in range(PAIRS):
                    weigh(0, k)
                with pool.Fori(1, turns) as i:
                    for k in range(PAIRS):
                        weigh(i, k)


def ssm_finish(nc, phases, layer, L, x, out, weights, y_dram):
    seqs = max(1, SEQ // L)
    width = seqs * L
    groups = HALF // seqs
    vec = weights[:, layer * SSM_COLS + SSM_VEC + 2:layer * SSM_COLS + SSM_VEC + 3]
    with ExitStack() as ctx:
        sem = phases.open(f"fin{layer}")
        y = ctx.enter_context(nc.sbuf_tensor(f"fin{layer}_y", [128, groups, width], F32))
        loaded, summed, pooled = sem("loaded"), sem("summed"), sem("pooled")
        with nc.Block() as block:
            phases.clear_before(block)

            @block.sync
            def _(sp):
                src = y_dram.rearrange("(h g) e w -> h e g w", h=2)
                for h in range(2):
                    sp.dma_start(y[64 * h:64 * h + 64, :, :], src[h]).then_inc(loaded, 16)

            @block.vector
            def _(dve):
                dve.wait_ge(loaded, 32)
                flat = y[:, :, :].rearrange("p g w -> p (g w)")
                if layer == SSM_LAYERS - 1:
                    dve.scalar_tensor_tensor(out[:, 0:COLS], x[:, 0:HALF * L], vec, flat, ALU.mult, ALU.add).then_inc(summed, 1)
                else:
                    half = L // 2
                    dve.scalar_tensor_tensor(flat, x[:, 0:HALF * L], vec, flat, ALU.mult, ALU.add).then_inc(summed, 1)
                    dve.wait_ge(summed, 1)
                    seq = flat.rearrange("p (b l) -> p b l", l=L)
                    pair = seq[:, :, 0:2 * half].rearrange("p b (l two) -> p b l two", two=2)
                    dst = out[:, 0:HALF * half].rearrange("p (b l) -> p b l", l=half)
                    dve.tensor_tensor(dst, pair[:, :, :, 0], pair[:, :, :, 1], ALU.add).then_inc(pooled, 1)
                    dve.wait_ge(pooled, 1)
                    dve.tensor_scalar(dst, dst, 0.5, None, ALU.mult).then_inc(pooled, 1)


CHUNKS = 4
CHUNK = COLS // CHUNKS
GT = 88
GTILES = COLS // GT
QN, QO = [94, 93], [0, 94]


class Columns:

    def __init__(self):
        self.at, self.n = {}, 0

    def add(self, name, n):
        self.at[name] = (self.n, n)
        self.n += n


ATTN = {"L0": dict(heads=4, proj=True, pos=False), "L1": dict(heads=1, proj=False, pos=False),
        "L2": dict(heads=4, proj=True, pos=True), "L3": dict(heads=1, proj=False, pos=False)}
FFN = {"L0": dict(E=8, blocks=1, shared=0, act="Gelu", softmax_first=False),
       "L1": dict(E=8, blocks=1, shared=0, act="Relu", softmax_first=False),
       "L2": dict(E=8, blocks=2, shared=2, act="Gelu", softmax_first=True),
       "L3": dict(E=16, blocks=1, shared=0, act="Relu", softmax_first=False)}


def post_columns():
    c = Columns()
    c.add("mean", 128)
    c.add("ident", 128)
    for e in (8, 16):
        c.add(f"rank{e}", e)
    for n in ("f0_gamma", "f0_beta", "a2_gamma", "a2_beta", "f3_gamma", "f3_beta"):
        c.add(n, 1)
    for L, a in ATTN.items():
        for n in ("wq", "wk", "wv", "bv"):
            c.add(L + n, 128)
        for n in ("bq", "bk"):
            c.add(L + n, 1)
        c.add(L + "mask", 2 * a["heads"])
        if a["proj"]:
            c.add(L + "wo", 128)
            c.add(L + "bo", 1)
        if a["pos"]:
            c.add(L + "wpos", 128)
            c.add(L + "pe", TOK)
            c.add(L + "u", 1)
            c.add(L + "v", 1)
    c.add("L1scale", 1)
    for L, f in FFN.items():
        nb = f["E"] * f["blocks"] + f["shared"]
        c.add(L + "w1", 2 * nb * 128)
        c.add(L + "b1", nb)
        c.add(L + "w2", nb * 192)
        c.add(L + "b2", 128)
        c.add(L + "wr", 2 * f["E"])
        c.add(L + "br", 2 * f["E"])
    c.add("L2b2s", 1)
    return c


PC = post_columns()


class Post:

    def __init__(self, nc, phases, W, sel, hidden, ready):
        self.phases = phases
        self.nc, self.W, self.sel, self.hidden, self.ready = nc, W, sel, hidden, ready
        self.phase = 0

    def w(self, name, a=0, n=None):
        o, size = PC.at[name]
        return self.W[:, o + a:o + a + (size - a if n is None else n)]

    def sems(self, ctx, kind):
        self.phase += 1
        return self.phases.open(f"p{self.phase}{kind}")

    def norm(self, src, dst, affine=None):
        with ExitStack() as ctx:
            sem = self.sems(ctx, "norm")
            nc, tag = self.nc, f"n{self.phase}"
            mean = ctx.enter_context(nc.psum_tensor(tag + "mean", [128, CHUNKS, PIECE], F32))
            var = ctx.enter_context(nc.psum_tensor(tag + "var", [128, CHUNKS, PIECE], F32))
            centred = ctx.enter_context(nc.sbuf_tensor(tag + "c", [128, COLS], F32))
            squares = ctx.enter_context(nc.sbuf_tensor(tag + "s", [128, COLS], F32))
            rstd = ctx.enter_context(nc.sbuf_tensor(tag + "r", [128, COLS], F32))
            eps = ctx.enter_context(nc.sbuf_tensor(tag + "e", [128, 1], F32))
            meaned, centred_r, squared, var_r, log_r, rstd_r, out_r, eps_r = (
                sem(n) for n in ("meaned", "centred", "squared", "var", "log", "rstd", "out", "eps"))
            with nc.Block() as block:
                self.phases.clear_before(block)

                @block.tensor
                def _(pe):
                    with pe.Fori(0, CHUNKS) as c:
                        pe.matmul(mean[:, ds(c, 1), 0:CHUNK].rearrange("p a n -> p (a n)"), self.w("mean"),
                                  src[:, ds(c * CHUNK, CHUNK)], start=True, stop=True).then_inc(meaned, 1)
                    with pe.Fori(0, CHUNKS) as c:
                        pe.wait_ge(squared, c + 1)
                        pe.matmul(var[:, ds(c, 1), 0:CHUNK].rearrange("p a n -> p (a n)"), self.w("mean"),
                                  squares[:, ds(c * CHUNK, CHUNK)], start=True, stop=True).then_inc(var_r, 1)

                @block.vector
                def _(dve):
                    dve.memset(eps[:, :], 1e-5).then_inc(eps_r, 1)
                    with dve.Fori(0, CHUNKS) as c:
                        dve.wait_ge(meaned, c + 1)
                        dve.tensor_tensor(centred[:, ds(c * CHUNK, CHUNK)], src[:, ds(c * CHUNK, CHUNK)],
                                          mean[:, ds(c, 1), 0:CHUNK].rearrange("p a n -> p (a n)"),
                                          ALU.subtract).then_inc(centred_r, 1)
                    with dve.Fori(0, CHUNKS) as c:
                        cols = ds(c * CHUNK, CHUNK)
                        dve.wait_ge(rstd_r, c + 1)
                        dve.tensor_tensor(dst[:, cols], centred[:, cols], rstd[:, cols], ALU.mult).then_inc(out_r, 1)
                        if affine:
                            dve.wait_ge(out_r, 2 * c + 1)
                            dve.tensor_scalar(dst[:, cols], dst[:, cols], self.w(affine[0]), self.w(affine[1]),
                                              ALU.mult, ALU.add).then_inc(out_r, 1)

                @block.scalar
                def _(act):
                    act.wait_ge(eps_r, 1)
                    with act.Fori(0, CHUNKS) as c:
                        cols = ds(c * CHUNK, CHUNK)
                        here = settle(act, c + 1)
                        act.wait_ge(self.ready[0], self.ready[1])
                        act.wait_ge(centred_r, here)
                        act.activation(squares[:, cols], centred[:, cols], ACT.Square).then_inc(squared, 1)
                    with act.Fori(0, CHUNKS) as c:
                        cols = ds(c * CHUNK, CHUNK)
                        here = settle(act, c + 1)
                        act.wait_ge(self.ready[0], self.ready[1])
                        act.wait_ge(var_r, here)
                        act.activation(rstd[:, cols], var[:, ds(c, 1), 0:CHUNK].rearrange("p a n -> p (a n)"),
                                       ACT.Ln, bias=eps[:, 0:1]).then_inc(log_r, 1)
                        act.wait_ge(self.ready[0], self.ready[1])
                        act.wait_ge(log_r, here)
                        act.activation(rstd[:, cols], rstd[:, cols], ACT.Exp, scale=-0.5).then_inc(rstd_r, 1)

    def attention(self, L, xn):
        a = ATTN[L]
        H, pos = a["heads"], a["pos"]
        NV, G = (4, 2) if H == 4 else (2, 1)
        dh = D // H
        NI = 2 * G
        NH = NV * G
        nc, hidden = self.nc, self.hidden
        with ExitStack() as ctx:
            sem = self.sems(ctx, "attn")
            tag = f"at{L}"
            sb = lambda name, shape, dt=F32: ctx.enter_context(nc.sbuf_tensor(tag + name, shape, dt))
            ps = lambda name, shape: ctx.enter_context(nc.psum_tensor(tag + name, shape, F32))
            xb = [sb(f"x{p}", [128, TOK]) for p in range(2)]
            qz = [sb(f"q{p}", [128, NH, TOK]) for p in range(2)]
            ks = [sb(f"k{p}", [128, TOK]) for p in range(2)]
            vz = [[sb(f"v{p}{t}", [128, NH * (128 + dh)]) for t in range(2)] for p in range(2)]
            prob = [sb(f"p{p}", [128, NV, TOK]) for p in range(2)]
            probT = [[sb(f"pt{p}{t}", [128, NV, 94]) for t in range(2)] for p in range(2)]
            top = [sb(f"m{p}", [128, NV]) for p in range(2)]
            total = [sb(f"t{p}", [128, NV]) for p in range(2)]
            inv = [sb(f"i{p}", [128, NV]) for p in range(2)]
            o_s = [sb(f"o{p}", [128, TOK]) for p in range(2)]
            mask = sb("mask", [128, NH])
            rscale = sb("rscale", [128, 1])
            bias = sb("bias", [128, 2])
            nb = NV // 2
            S = [ps(f"S{p}", [128, nb, PIECE]) for p in range(2)]
            T = ps("T", [128, 2, PIECE])
            O = ps("O", [128, PIECE])
            M = ps("M", [128, PIECE])
            names = ("setup", "xb", "qk", "qd", "kd", "v", "vd", "s", "max", "exp", "rinv", "nrm", "t", "tca", "tcv",
                     "pv", "oc", "proj", "res", "added", "posq", "poss", "posc", "pt", "credit")
            q = {n: sem(n) for n in names}
            pos_stored = [sem(f"pos_stored{k}") for k in range(2)]
            shifted_in = [sem(f"shifted_in{k}") for k in range(2)]
            if pos:
                skew = nc.dram_tensor(f"skew{L}", (8, NH, TOK * (TOK + 1)), F32, kind="Internal").ap()
                shifted = [sb(f"sh{p}", [128, NV, TOK]) for p in range(2)]
                score = [sb(f"sc{p}", [128, NV, TOK]) for p in range(2)]
                posT = sb("posT", [128, TOK])
                padded = [sb(f"pad{p}", [128, NV, TOK + 1]) for p in range(2)]

            def s_view(m, n):
                return S[m % 2][0:n, :, 0:2 * TOK]

            with nc.Block() as block:
                self.phases.clear_before(block)

                @block.gpsimd
                def _(pool):
                    for p in range(2):
                        for t in range(2):
                            pool.memset(vz[p][t][:, :], 0.0).then_inc(q["setup"], 1)
                        if pos:
                            pool.memset(padded[p][:, :, 0:1], 0.0).then_inc(q["setup"], 1)
                    for n in ("exp", "t", "pv", "oc", "res", "vd", "tca", "tcv", "added", "posq", "posc", "poss", "qd"):
                        pool.sem_inc(q[n], SLACK)
                    for k in range(2):
                        pool.sem_inc(pos_stored[k], SLACK)

                @block.vector
                def _(dve):
                    if L == "L1":
                        dve.reciprocal(rscale[:, :], self.w("L1scale")).then_inc(q["credit"], 1)
                        dve.wait_ge(q["credit"], 1)
                        dve.tensor_scalar(mask[:, :], self.w(L + "mask"), rscale[:, 0:1], None, ALU.mult).then_inc(q["credit"], 1)
                    else:
                        dve.tensor_copy(mask[:, :], self.w(L + "mask")).then_inc(q["credit"], 1)
                    if pos:
                        dve.tensor_tensor(bias[:, 0:1], self.w(L + "bq"), self.w(L + "u"), ALU.add).then_inc(q["credit"], 1)
                        dve.tensor_tensor(bias[:, 1:2], self.w(L + "bq"), self.w(L + "v"), ALU.add).then_inc(q["credit"], 1)
                    else:
                        dve.tensor_copy(bias[:, 0:1], self.w(L + "bq")).then_inc(q["credit"], 1)

                if pos:
                    @block.tensor
                    def _(pe):
                        pe.matmul(M[:, 0:TOK], self.w(L + "wpos"), self.w(L + "pe"), start=True, stop=True).then_inc(q["pt"], 1)

                    @block.scalar
                    def _(act):
                        act.wait_ge(q["pt"], 1)
                        act.activation(posT[:, :], M[:, 0:TOK], ACT.Copy).then_inc(q["pt"], 1)

            if pos:
                with nc.Block() as block:
                    @block.gpsimd
                    def _(pool):
                        with pool.Fori(0, 4) as i:
                            for p in range(2):
                                b = 2 * i + p
                                free = settle(pool, SLACK + b - 1)
                                pool.wait_ge(self.ready[0], self.ready[1])
                                pool.wait_ge(q["posq"], free)
                                pool.tensor_copy(xb[p][:, :], xn[:, ds(b * TOK, TOK)]).then_inc(q["xb"], 1)

                    @block.tensor
                    def _(pe):
                        with pe.Fori(0, 4) as i:
                            for p in range(2):
                                b = 2 * i + p
                                pe.wait_ge(q["xb"], b + 1)
                                pe.wait_ge(q["qd"], SLACK + b)
                                pe.matmul(M[:, 0:TOK], self.w(L + "wq"), xb[p][:, :], start=True, stop=True).then_inc(q["posq"], 1)
                                pe.wait_ge(q["qd"], SLACK + b + 1)
                                for m in range(NI):
                                    t, g = m // G, m % G
                                    n = QN[t]
                                    pe.wait_ge(q["posc"], SLACK + b * NI + m - 1)
                                    for v in range(NV):
                                        mm = pe.matmul(S[m % 2][0:n, v // 2, (v % 2) * TOK:(v % 2) * TOK + TOK],
                                                       qz[p][:, g * NV + v, QO[t]:QO[t] + n], posT[:, :],
                                                       start=True, stop=True)
                                    mm.then_inc(q["poss"], 1)

                    @block.vector
                    def _(dve):
                        with dve.Fori(0, 4) as i:
                            for p in range(2):
                                b = 2 * i + p
                                dve.wait_ge(q["posq"], SLACK + b + 1)
                                dve.wait_ge(q["poss"], SLACK + NI * (b - 1))
                                for v in range(NH):
                                    op = dve.tensor_scalar(qz[p][:, v, :], M[:, 0:TOK], bias[:, 1:2], mask[:, v:v + 1],
                                                           ALU.add, ALU.mult)
                                op.then_inc(q["qd"], 1)

                    @block.scalar
                    def _(act):
                        with act.Fori(0, 4) as i:
                            for p in range(2):
                                b = 2 * i + p
                                for m in range(NI):
                                    n = QN[m // G]
                                    act.wait_ge(q["poss"], SLACK + b * NI + m + 1)
                                    act.wait_ge(pos_stored[m % 2], SLACK + 16 * (i * NI + (p * NI + m) // 2))
                                    act.activation(padded[m % 2][0:n, :, 1:TOK + 1].rearrange("p (a v) n -> p a v n", a=nb),
                                                   s_view(m, n).rearrange("p a (v n) -> p a v n", v=2),
                                                   ACT.Copy).then_inc(q["posc"], 1)

                    @block.sync
                    def _(sp):
                        with sp.Fori(0, 4) as i:
                            for p in range(2):
                                b = 2 * i + p
                                for m in range(NI):
                                    t, g = m // G, m % G
                                    sp.wait_ge(q["posc"], SLACK + b * NI + m + 1)
                                    dst = skew[ds(b, 1), g * NV:(g + 1) * NV, QO[t] * (TOK + 1):(QO[t] + QN[t]) * (TOK + 1)]
                                    sp.dma_start(dst.rearrange("o v (q n) -> (o q) v n", n=TOK + 1),
                                                 padded[m % 2][0:QN[t], :, :]).then_inc(pos_stored[m % 2], 16)
                        for k in range(2):
                            sp.wait_ge(pos_stored[k], SLACK + 16 * 4 * NI)

            with nc.Block() as block:
                XB0 = 8 if pos else 0
                QD0 = SLACK + (8 if pos else 0)

                @block.gpsimd
                def _(pool):
                    with pool.Fori(0, 4) as i:
                        for p in range(2):
                            b = 2 * i + p
                            free = settle(pool, SLACK + b - 1)
                            pool.wait_ge(self.ready[0], self.ready[1])
                            pool.wait_ge(q["vd"], free)
                            pool.tensor_copy(xb[p][:, :], xn[:, ds(b * TOK, TOK)]).then_inc(q["xb"], 1)

                if pos:
                    @block.sync
                    def _(sp):
                        with sp.Fori(0, 4) as i:
                            for p in range(2):
                                b = 2 * i + p
                                for m in range(NI):
                                    t, g = m // G, m % G
                                    sp.wait_ge(q["added"], SLACK + b * NI + m - 1)
                                    src = skew[ds(b, 1), g * NV:(g + 1) * NV, TOK * (1 + QO[t]):TOK * (1 + QO[t] + QN[t])]
                                    sp.dma_start(shifted[m % 2][0:QN[t], :, :],
                                                 src.rearrange("o v (q n) -> (o q) v n", n=TOK)).then_inc(shifted_in[m % 2], 16)

                @block.tensor
                def _(pe):
                    def front(b, p):
                        pe.wait_ge(q["xb"], XB0 + b + 1)
                        pe.wait_ge(q["vd"], SLACK + b)
                        if a["proj"] and p == 0:
                            pe.wait_ge(q["res"], SLACK + b)
                        pe.matmul(M[:, 0:TOK], self.w(L + "wq"), xb[p][:, :], start=True, stop=True)
                        pe.matmul(M[:, TOK:2 * TOK], self.w(L + "wk"), xb[p][:, :], start=True, stop=True).then_inc(q["qk"], 1)
                        pe.wait_ge(q["qd"], QD0 + b + 1)
                        pe.wait_ge(q["kd"], b + 1)
                        for t in range(2):
                            mm = pe.matmul(M[0:QN[t], 128 * t:128 * t + 128], xb[p][:, QO[t]:QO[t] + QN[t]],
                                           self.w(L + "wv"), start=True, stop=True)
                        mm.then_inc(q["v"], 1)

                    def scores(b0, x):
                        p, m = x // NI, x % NI
                        t, g = m // G, m % G
                        pe.wait_ge(q["exp"], SLACK + b0 * NI + x - 1)
                        if pos:
                            pe.wait_ge(q["added"], SLACK + b0 * NI + x - 1)
                        for v in range(NV):
                            mm = pe.matmul(S[x % 2][0:QN[t], v // 2, (v % 2) * TOK:(v % 2) * TOK + TOK],
                                           qz[p][:, g * NV + v, QO[t]:QO[t] + QN[t]], ks[p][:, :], start=True, stop=True)
                        mm.then_inc(q["s"], 1)

                    def turn(b0, x):
                        m = x % NI
                        n = QN[m // G]
                        pe.wait_ge(q["nrm"], b0 * NI + x + 1)
                        pe.wait_ge(q["tca"], SLACK + b0 * NI + x)
                        pe.wait_ge(q["tcv"], SLACK + b0 * NI + x)
                        for t in range(2):
                            for v in range(NV):
                                mm = pe.transpose(T[0:QN[t], t, v * 94:v * 94 + n], prob[x % 2][0:n, v, QO[t]:QO[t] + QN[t]],
                                                  self.w("ident")[0:n, 0:n])
                        mm.then_inc(q["t"], 1)

                    def values(b0, x):
                        p, m = x // NI, x % NI
                        t, g = m // G, m % G
                        n = QN[t]
                        pe.wait_ge(q["tca"], SLACK + b0 * NI + x + 1)
                        pe.wait_ge(q["tcv"], SLACK + b0 * NI + x + 1)
                        if m == 0:
                            pe.wait_ge(q["vd"], SLACK + b0 + p + 1)
                            pe.wait_ge(q["oc"], SLACK + b0 + p)
                        for v in range(NV):
                            gv = g * NV + v
                            for k in range(2):
                                mm = pe.matmul(O[:, QO[t]:QO[t] + n], vz[p][k][0:QN[k], gv * 128:gv * 128 + 128],
                                               probT[x % 2][k][0:QN[k], v, 0:n], start=(gv == 0 and k == 0),
                                               stop=(gv == NH - 1 and k == 1))
                        mm.then_inc(q["pv"], 1)

                    def project(b, p):
                        pe.wait_ge(q["oc"], SLACK + b + 1)
                        if p == 1:
                            pe.wait_ge(q["res"], SLACK + b)
                        pe.matmul(M[:, 0:TOK], self.w(L + "wo"), o_s[p][:, :], start=True, stop=True).then_inc(q["proj"], 1)

                    n = 2 * NI
                    with pe.Fori(0, 4) as i:
                        b0 = 2 * i
                        front(b0, 0)
                        front(b0 + 1, 1)
                        scores(b0, 0)
                        scores(b0, 1)
                        turn(b0, 0)
                        for x in range(n):
                            if x + 2 < n:
                                scores(b0, x + 2)
                            if x + 1 < n:
                                turn(b0, x + 1)
                            values(b0, x)
                            if a["proj"] and x == NI:
                                project(b0, 0)
                        if a["proj"]:
                            project(b0 + 1, 1)

                @block.vector
                def _(dve):
                    def front(b, p):
                        dve.wait_ge(q["qk"], b + 1)
                        for v in range(NH):
                            op = dve.tensor_scalar(qz[p][:, v, :], M[:, 0:TOK], bias[:, 0:1], mask[:, v:v + 1],
                                                   ALU.add, ALU.mult)
                        op.then_inc(q["qd"], 1)
                        dve.wait_ge(q["v"], b + 1)
                        for t in range(2):
                            out = vz[p][t][0:QN[t], :].rearrange("p (v c) -> p v c", c=128 + dh)[:, :, 0:dh]
                            op = dve.tensor_tensor(out, M[0:QN[t], 128 * t:128 * t + 128].rearrange("p (v c) -> p v c", c=dh),
                                                   self.w(L + "bv")[0:QN[t], :].rearrange("p (v c) -> p v c", c=dh), ALU.add)
                        op.then_inc(q["vd"], 1)

                    def maxima(b0, x):
                        n = QN[x % NI // G]
                        if pos:
                            dve.wait_ge(q["s"], b0 * NI + x + 1)
                            dve.wait_ge(shifted_in[x % 2], 8 * NI * b0 + 16 * (x // 2 + 1))
                            dve.wait_ge(q["exp"], SLACK + b0 * NI + x - 1)
                            dve.tensor_tensor(score[x % 2][0:n, :, :].rearrange("p (a v) n -> p a (v n)", a=nb), s_view(x, n),
                                              shifted[x % 2][0:n, :, :].rearrange("p (a v) n -> p a (v n)", a=nb),
                                              ALU.add).then_inc(q["added"], 1)
                            dve.wait_ge(q["added"], SLACK + b0 * NI + x + 1)
                            dve.tensor_reduce(top[x % 2][0:n, :], score[x % 2][0:n, :, :], AX.X, ALU.max,
                                              negate=True).then_inc(q["max"], 1)
                        else:
                            dve.wait_ge(q["s"], b0 * NI + x + 1)
                            dve.tensor_reduce(top[x % 2][0:n, :].rearrange("p (a v) -> p a v", a=nb),
                                              s_view(x, n).rearrange("p a (v n) -> p a v n", v=2), AX.X, ALU.max,
                                              negate=True).then_inc(q["max"], 1)

                    def normalise(b0, x):
                        n = QN[x % NI // G]
                        dve.wait_ge(q["exp"], SLACK + b0 * NI + x + 1)
                        dve.reciprocal(inv[x % 2][0:n, :], total[x % 2][0:n, :]).then_inc(q["rinv"], 1)
                        dve.wait_ge(q["rinv"], b0 * NI + x + 1)
                        dve.tensor_tensor(prob[x % 2][0:n, :, :], prob[x % 2][0:n, :, :],
                                          inv[x % 2][0:n, :].unsqueeze(2).to_broadcast([n, NV, TOK]),
                                          ALU.mult).then_inc(q["nrm"], 1)

                    def copy_turned(b0, x):
                        n = QN[x % NI // G]
                        dve.wait_ge(q["t"], SLACK + b0 * NI + x + 1)
                        dve.wait_ge(q["pv"], SLACK + b0 * NI + x - 1)
                        dve.tensor_copy(probT[x % 2][1][0:QN[1], :, 0:n],
                                        T[0:QN[1], 1, 0:NV * 94].rearrange("p (v n) -> p v n", n=94)[:, :, 0:n]).then_inc(q["tcv"], 1)

                    def residual(b, p):
                        cols = ds(b * TOK, TOK)
                        if a["proj"]:
                            dve.wait_ge(q["proj"], b + 1)
                            dve.scalar_tensor_tensor(hidden[:, cols], M[:, 0:TOK], self.w(L + "bo"), hidden[:, cols],
                                                     ALU.add, ALU.add).then_inc(q["res"], 1)
                        else:
                            dve.wait_ge(q["pv"], SLACK + NI * (b + 1))
                            dve.tensor_tensor(hidden[:, cols], O[:, 0:TOK], hidden[:, cols], ALU.add).then_inc(q["oc"], 1)

                    n = 2 * NI
                    with dve.Fori(0, 4) as i:
                        b0 = 2 * i
                        front(b0, 0)
                        front(b0 + 1, 1)
                        maxima(b0, 0)
                        normalise(b0, 0)
                        maxima(b0, 1)
                        for x in range(n):
                            copy_turned(b0, x)
                            if x + 1 < n:
                                normalise(b0, x + 1)
                            if x + 2 < n:
                                maxima(b0, x + 2)
                            if not a["proj"] and x == NI - 1:
                                residual(b0, 0)
                            if a["proj"] and x == NI + 1:
                                residual(b0, 0)
                        residual(b0 + 1, 1)

                @block.scalar
                def _(act):
                    def keys(b, p):
                        act.wait_ge(q["qk"], b + 1)
                        act.wait_ge(q["qd"], QD0 + b + 1)
                        act.activation(ks[p][:, :], M[:, TOK:2 * TOK], ACT.Identity, bias=self.w(L + "bk")).then_inc(q["kd"], 1)

                    def exps(b0, x):
                        n = QN[x % NI // G]
                        act.wait_ge(q["max"], b0 * NI + x + 1)
                        act.wait_ge(q["t"], SLACK + b0 * NI + x - 1)
                        for v in range(NV):
                            src = score[x % 2][0:n, v, :] if pos else S[x % 2][0:n, v // 2, (v % 2) * TOK:(v % 2) * TOK + TOK]
                            op = act.activation(prob[x % 2][0:n, v, :], src, ACT.Exp, bias=top[x % 2][0:n, v:v + 1],
                                                accum_out=total[x % 2][0:n, v:v + 1])
                        op.then_inc(q["exp"], 1)

                    def copy_turned(b0, x):
                        n = QN[x % NI // G]
                        act.wait_ge(q["t"], SLACK + b0 * NI + x + 1)
                        act.wait_ge(q["pv"], SLACK + b0 * NI + x - 1)
                        act.activation(probT[x % 2][0][0:QN[0], :, 0:n],
                                       T[0:QN[0], 0, 0:NV * 94].rearrange("p (v n) -> p v n", n=94)[:, :, 0:n],
                                       ACT.Copy).then_inc(q["tca"], 1)

                    def out(b, p):
                        act.wait_ge(q["pv"], SLACK + NI * (b + 1))
                        act.activation(o_s[p][:, :], O[:, 0:TOK], ACT.Copy).then_inc(q["oc"], 1)

                    n = 2 * NI
                    with act.Fori(0, 4) as i:
                        b0 = 2 * i
                        keys(b0, 0)
                        keys(b0 + 1, 1)
                        exps(b0, 0)
                        exps(b0, 1)
                        for x in range(n):
                            copy_turned(b0, x)
                            if x + 2 < n:
                                exps(b0, x + 2)
                            if a["proj"] and x == NI - 1:
                                out(b0, 0)
                        if a["proj"]:
                            out(b0 + 1, 1)

    def gate(self, L, xn, parts_T, weights_T):
        f = FFN[L]
        E = f["E"]
        nc = self.nc
        with ExitStack() as ctx:
            sem = self.sems(ctx, "gate")
            tag = f"g{L}"
            sb = lambda name, shape, dt=F32: ctx.enter_context(nc.sbuf_tensor(tag + name, shape, dt))
            LG = ctx.enter_context(nc.psum_tensor(tag + "LG", [128, 2 * PIECE], F32))
            TB = ctx.enter_context(nc.psum_tensor(tag + "TB", [96, 2, 2 * PIECE], BF16))
            TF = ctx.enter_context(nc.psum_tensor(tag + "TF", [32, 4, PIECE], F32))
            R = 2 * GTILES
            val, work, hot1, hot2, w = (sb(n, [GT, R, E]) for n in ("val", "work", "hot1", "hot2", "w"))
            m1, m2, r, ex, rd = (sb(n, [GT, R]) for n in ("m1", "m2", "r", "ex", "rd"))
            parts = sb("parts", [GT, GTILES, 3, 32], BF16)
            wpad = sb("wpad", [GT, GTILES, 32])
            identb = sb("identb", [128, 128], BF16)
            logits, step, exped, turned, copied, cleared = (sem(n) for n in ("logits", "step", "exped", "turned", "copied", "cleared"))
            wide = lambda t: t[:, :].unsqueeze(2).to_broadcast([GT, R, E])
            rank = self.w(f"rank{E}")[0:GT, :].unsqueeze(1).to_broadcast([GT, R, E])
            bias = self.w(L + "br")[0:GT, 0:E].unsqueeze(1).to_broadcast([GT, R, E])
            count = [0]
            fu = f["softmax_first"]

            with nc.Block() as block:
                self.phases.clear_before(block)

                @block.gpsimd
                def _(pool):
                    if E == 8:
                        pool.memset(parts[:, :, :, :], 0.0).then_inc(cleared, 1)
                        pool.memset(wpad[:, :, :], 0.0).then_inc(cleared, 1)
                    pool.tensor_copy(identb[:, :], self.w("ident")).then_inc(cleared, 1)

                @block.tensor
                def _(pe):
                    for t in range(GTILES):
                        mm = pe.matmul(LG[0:GT, 2 * E * t:2 * E * t + 2 * E], xn[:, GT * t:GT * t + GT], self.w(L + "wr"),
                                       start=True, stop=True)
                    mm.then_inc(logits, 1)
                    pe.wait_ge(copied, 1)
                    pe.wait_ge(cleared, 3 if E == 8 else 1)
                    for t in range(GTILES):
                        mm = pe.transpose(TB[0:96, t // 9, (t % 9) * GT:(t % 9) * GT + GT],
                                          parts[:, t, :, :].rearrange("p s r -> p (s r)"), identb[0:GT, 0:GT])
                    mm.then_inc(turned, 1)
                    for t in range(GTILES):
                        mm = pe.transpose(TF[0:32, t // 5, (t % 5) * GT:(t % 5) * GT + GT], wpad[:, t, :],
                                          self.w("ident")[0:GT, 0:GT])
                    mm.then_inc(turned, 1)

                @block.scalar
                def _(act):
                    act.wait_ge(exped, 1)
                    if fu:
                        act.activation(work[:, :, :], val[:, :, :], ACT.Exp).then_inc(exped, 1)
                    else:
                        act.activation(ex[:, :], ex[:, :], ACT.Exp).then_inc(exped, 1)
                    act.wait_ge(turned, 2)
                    for k in range(4):
                        n = min(5, GTILES - 5 * k) * GT
                        act.activation(weights_T[:, 5 * GT * k:5 * GT * k + n], TF[0:32, k, 0:n], ACT.Copy).then_inc(copied, 1)

                @block.vector
                def _(dve):
                    def done(ins):
                        count[0] += 1
                        ins.then_inc(step, 1)
                        dve.wait_ge(step, count[0])

                    dve.wait_ge(logits, 1)
                    done(dve.tensor_tensor(val[:, :, :], LG[0:GT, 0:R * E].rearrange("p (r e) -> p r e", e=E), bias, ALU.add))
                    if L == "L1":
                        done(dve.tensor_tensor(val[:, :, :], val[:, :, :],
                                               self.w(L + "br")[0:GT, E:2 * E].unsqueeze(1).to_broadcast([GT, R, E]), ALU.add))
                    if fu:
                        done(dve.tensor_reduce(m1[:, :], val[:, :, :], AX.X, ALU.max))
                        dve.tensor_tensor(val[:, :, :], val[:, :, :], wide(m1), ALU.subtract).then_inc(exped, 1)
                        dve.wait_ge(exped, 2)
                        done(dve.tensor_reduce(r[:, :], work[:, :, :], AX.X, ALU.add))
                        done(dve.reciprocal(rd[:, :], r[:, :]))
                        done(dve.tensor_tensor(val[:, :, :], work[:, :, :], wide(rd), ALU.mult))

                    def choose(top, hot):
                        done(dve.tensor_reduce(top[:, :], val[:, :, :], AX.X, ALU.max))
                        done(dve.tensor_tensor(work[:, :, :], val[:, :, :], wide(top), ALU.is_equal))
                        done(dve.tensor_tensor(work[:, :, :], work[:, :, :], rank, ALU.mult))
                        done(dve.tensor_reduce(r[:, :], work[:, :, :], AX.X, ALU.max))
                        done(dve.tensor_tensor(hot[:, :, :], work[:, :, :], wide(r), ALU.is_equal))

                    choose(m1, hot1)
                    done(dve.scalar_tensor_tensor(val[:, :, :], hot1[:, :, :], -1e30, val[:, :, :], ALU.mult, ALU.add))
                    choose(m2, hot2)
                    if fu:
                        done(dve.tensor_tensor(ex[:, :], m1[:, :], m2[:, :], ALU.add))
                        done(dve.reciprocal(rd[:, :], ex[:, :]))
                        done(dve.tensor_tensor(m1[:, :], m1[:, :], rd[:, :], ALU.mult))
                        done(dve.tensor_tensor(m2[:, :], m2[:, :], rd[:, :], ALU.mult))
                    else:
                        dve.tensor_tensor(ex[:, :], m2[:, :], m1[:, :], ALU.subtract).then_inc(exped, 1)
                        dve.wait_ge(exped, 2)
                        done(dve.tensor_scalar(r[:, :], ex[:, :], 1.0, None, ALU.add))
                        done(dve.reciprocal(m1[:, :], r[:, :]))
                        done(dve.tensor_tensor(m2[:, :], ex[:, :], m1[:, :], ALU.mult))
                    done(dve.tensor_tensor(hot1[:, :, :], hot1[:, :, :], wide(m1), ALU.mult))
                    done(dve.tensor_tensor(hot2[:, :, :], hot2[:, :, :], wide(m2), ALU.mult))
                    done(dve.tensor_tensor(w[:, :, :], hot1[:, :, :], hot2[:, :, :], ALU.add))
                    dve.wait_ge(cleared, 3 if E == 8 else 1)
                    flat = w[:, :, :].rearrange("p (t h) e -> p t (h e)", h=2)
                    rest = hot1[:, :, :].rearrange("p (t h) e -> p t (h e)", h=2)
                    part = lambda s: parts[:, :, s, 0:2 * E]
                    done(dve.tensor_copy(part(0), flat))
                    done(dve.tensor_tensor(rest, flat, part(0), ALU.subtract))
                    done(dve.tensor_copy(part(1), rest))
                    done(dve.tensor_tensor(part(2), rest, part(1), ALU.subtract))
                    dve.tensor_copy(wpad[:, :, 0:2 * E], flat).then_inc(copied, 1)
                    dve.wait_ge(turned, 1)
                    for k in range(2):
                        n = (9, GTILES - 9)[k] * GT
                        dve.tensor_copy(parts_T[:, 9 * GT * k:9 * GT * k + n], TB[0:96, k, 0:n]).then_inc(copied, 1)

    def experts(self, L, xn, parts_T, weights_T, dst, base):
        f = FFN[L]
        E = f["E"]
        blocks = [(e, k) for e in range(E) for k in range(f["blocks"])] + [(None, k) for k in range(f["shared"])]
        nblk = len(blocks)
        units = [(h, n) for n in range(nblk) for h in range(2)]
        NU = len(units)
        nc = self.nc
        func = function(f["act"])
        with ExitStack() as ctx:
            sem = self.sems(ctx, "moe")
            tag = f"m{L}"
            Hp = [ctx.enter_context(nc.psum_tensor(tag + f"H{k}", [128, PIECE], F32)) for k in range(2)]
            Bp = [ctx.enter_context(nc.psum_tensor(tag + f"B{k}", [128, PIECE], F32)) for k in range(2)]
            Y = ctx.enter_context(nc.psum_tensor(tag + "Y", [128, PIECE], F32))
            g = [ctx.enter_context(nc.sbuf_tensor(tag + f"g{k}", [128, CHUNK], F32)) for k in range(2)]
            gw = [ctx.enter_context(nc.sbuf_tensor(tag + f"gw{k}", [128, CHUNK], F32)) for k in range(2)]
            h_r, b_r, g_r, gw_r, y_r, used, y_done = (sem(n) for n in ("h", "b", "g", "gw", "y", "used", "ydone"))
            w1 = lambda h, n: self.w(L + "w1", (h * nblk + n) * 128, 128)
            w2 = lambda h, n: self.w(L + "w2", n * 192 + (64 if h == 0 else 0), 128)

            with nc.Block() as block:
                self.phases.clear_before(block)

                @block.tensor
                def _(pe):
                    pe.sem_inc(y_done, SLACK)

                    def up(c, u):
                        h, n = units[u]
                        pe.wait_ge(g_r, SLACK + c * NU + u - 1)
                        pe.matmul(Hp[u % 2][:, 0:CHUNK], w1(h, n), xn[:, ds(c * CHUNK, CHUNK)], start=True, stop=True).then_inc(h_r, 1)
                        pe.wait_ge(gw_r, SLACK + c * NU + u - 1)
                        e = blocks[n][0]
                        r = (h * E + e) if e is not None else 0
                        pe.matmul(Bp[u % 2][:, 0:CHUNK], self.sel[:, 128 * r:128 * r + 128], parts_T[:, ds(c * CHUNK, CHUNK)],
                                  start=True, stop=True).then_inc(b_r, 1)

                    def down(c, u):
                        h, n = units[u]
                        pe.wait_ge(gw_r, SLACK + c * NU + u + 1)
                        pe.matmul(Y[:, 0:CHUNK], w2(h, n), gw[u % 2][:, :], start=False, stop=(u == NU - 1)).then_inc(used, 1)

                    with pe.Fori(0, CHUNKS) as c:
                        up(c, 0)
                        pe.wait_ge(y_done, SLACK + c)
                        up(c, 1)
                        pe.matmul(Y[:, 0:CHUNK], self.w(L + "b2")[0:32, :], weights_T[:, ds(c * CHUNK, CHUNK)],
                                  start=True, stop=False)
                        for u in range(NU):
                            if u + 2 < NU:
                                down(c, u)
                                up(c, u + 2)
                            else:
                                down(c, u)

                @block.scalar
                def _(act):
                    act.sem_inc(g_r, SLACK)
                    with act.Fori(0, CHUNKS) as c:
                        for u in range(NU):
                            n = units[u][1]
                            act.wait_ge(h_r, c * NU + u + 1)
                            act.wait_ge(gw_r, SLACK + c * NU + u - 1)
                            act.activation(g[u % 2][:, :], Hp[u % 2][:, 0:CHUNK], func, bias=self.w(L + "b1", n, 1)).then_inc(g_r, 1)

                @block.vector
                def _(dve):
                    dve.sem_inc(gw_r, SLACK)
                    with dve.Fori(0, CHUNKS) as c:
                        for u in range(NU):
                            n = units[u][1]
                            dve.wait_ge(g_r, SLACK + c * NU + u + 1)
                            dve.wait_ge(b_r, c * NU + u + 1)
                            dve.wait_ge(used, SLACK + c * NU + u - 1)
                            if blocks[n][0] is None:
                                dve.tensor_copy(gw[u % 2][:, :], g[u % 2][:, :]).then_inc(gw_r, 1)
                            else:
                                dve.tensor_tensor(gw[u % 2][:, :], g[u % 2][:, :], Bp[u % 2][:, 0:CHUNK], ALU.mult).then_inc(gw_r, 1)
                        dve.wait_ge(used, SLACK + (c + 1) * NU)
                        cols = ds(c * CHUNK, CHUNK)
                        if f["shared"]:
                            dve.scalar_tensor_tensor(dst[:, cols], Y[:, 0:CHUNK], self.w("L2b2s"), base[:, cols],
                                                     ALU.add, ALU.add).then_inc(y_done, 1)
                        else:
                            dve.tensor_tensor(dst[:, cols], Y[:, 0:CHUNK], base[:, cols], ALU.add).then_inc(y_done, 1)

                @block.gpsimd
                def _(pool):
                    pool.sem_inc(used, SLACK)

    def add(self, dst, a, b):
        with ExitStack() as ctx, self.nc.Block() as block:
            sem = self.sems(ctx, "add")
            s = sem("s")
            self.phases.clear_before(block)

            @block.vector
            def _(dve):
                dve.tensor_tensor(dst[:, :], a[:, :], b[:, :], ALU.add).then_inc(s, 1)


def function(name):
    return {"Gelu": ACT.Gelu, "Relu": ACT.Relu}[name]


def post(nc, phases, hidden, weights_in):
    with ExitStack() as ctx:
        sb = lambda name, shape, dt=F32: ctx.enter_context(nc.sbuf_tensor(name, shape, dt))
        W = sb("post_weights", [128, PC.n])
        sel = sb("expert_sel", [96, 32 * 128], BF16)
        xn, x2 = sb("xn", [128, COLS]), sb("x2", [128, COLS])
        parts_T = sb("parts_T", [96, COLS], BF16)
        weights_T = sb("weights_T", [32, COLS])
        loaded = ctx.enter_context(nc.semaphore("post_loaded"))
        selected = ctx.enter_context(nc.semaphore("post_selected"))
        with nc.Block() as block:
            @block.gpsimd
            def _(pool):
                selector_of(pool, sel, 128, selected)

            @block.sync
            def _(sp):
                sp.dma_start(W[:, :], weights_in).then_inc(loaded, 16)
                sp.wait_ge(loaded, 16)
        P = Post(nc, phases, W, sel, hidden, (loaded, 16))
        for L in ("L0", "L1", "L2", "L3"):
            P.norm(hidden, xn)
            if L == "L2":
                P.norm(xn, xn, ("a2_gamma", "a2_beta"))
            P.attention(L, xn)
            P.norm(hidden, xn)
            if L == "L0":
                P.norm(xn, xn, ("f0_gamma", "f0_beta"))
            P.gate(L, xn, parts_T, weights_T)
            if L == "L3":
                P.experts(L, xn, parts_T, weights_T, x2, xn)
                P.norm(x2, x2, ("f3_gamma", "f3_beta"))
                P.add(hidden, hidden, x2)
            else:
                P.experts(L, xn, parts_T, weights_T, hidden, hidden)


def build(nc, x_in, ssm_w, post_w, out):
    phases = Phases(nc)
    with ExitStack() as ctx:
        sb = lambda name, shape, dt: ctx.enter_context(nc.sbuf_tensor(name, shape, dt))
        hidden = sb("hidden", [128, COLS], F32)
        inputs_loaded = ctx.enter_context(nc.semaphore("inputs_loaded"))
        with ExitStack() as ssm:
            ssb = lambda name, shape, dt: ssm.enter_context(nc.sbuf_tensor(name, shape, dt))
            weights = ssb("ssm_weights", [128, SSM_W], F32)
            selector = ssb("selector", [96, 16 * 128], BF16)
            a_neg = ssb("a_neg", [128, SSM_LAYERS * PAIRS], F32)
            xa = ssb("xa", [128, HALF * SEQ], F32)
            xb = ssb("xb", [128, HALF * LENS[1]], F32)
            a_done = ctx.enter_context(nc.semaphore("a_done"))
            selected = ctx.enter_context(nc.semaphore("selected"))
            with nc.Block() as block:

                @block.sync
                def _(sp):
                    sp.dma_start(weights[:, :], ssm_w).then_inc(inputs_loaded, 16)
                    sp.dma_start(xa[:, :], x_in).then_inc(inputs_loaded, 16)
                    sp.wait_ge(inputs_loaded, INPUT_DMAS)

                @block.gpsimd
                def _(pool):
                    selector_of(pool, selector, 64, selected)

                @block.scalar
                def _(act):
                    act.wait_ge(inputs_loaded, INPUT_DMAS)
                    for i in range(SSM_LAYERS):
                        act.activation(a_neg[:, PAIRS * i:PAIRS * (i + 1)],
                                       weights[:, i * SSM_COLS + SSM_A:i * SSM_COLS + SSM_A + PAIRS], ACT.Exp).then_inc(a_done, 1)

                @block.vector
                def _(dve):
                    dve.wait_ge(a_done, SSM_LAYERS)
                    dve.tensor_scalar(a_neg[:, :], a_neg[:, :], -1.0, None, ALU.mult).then_inc(a_done, 1)

            x = [xa, xb, xa]
            nxt = [xb, xa, hidden]
            for layer in range(SSM_LAYERS):
                L = LENS[layer]
                seqs = max(1, SEQ // L)
                width, turns = seqs * L, 2 * HALF // seqs
                split_dram = nc.dram_tensor(f"split{layer}", (2, 3, turns, 64, width), BF16, kind="Internal").ap()
                y_dram = nc.dram_tensor(f"y{layer}", (turns, 64, width), F32, kind="Internal").ap()
                with (nc.sbuf_tensor(f"b_rep{layer}", [128, 2 * HALF * L], F32) as b_rep,
                      nc.sbuf_tensor(f"c_rep{layer}", [128, 2 * HALF * L], F32) as c_rep):
                    ssm_prep(nc, phases, inputs_loaded, layer, L, x[layer], weights, b_rep, c_rep, split_dram)
                    ssm_scan(nc, phases, inputs_loaded, layer, L, weights, selector, a_neg, b_rep, c_rep, split_dram, y_dram)
                ssm_finish(nc, phases, layer, L, x[layer], nxt[layer], weights, y_dram)
        post(nc, phases, hidden, post_w)
        with ExitStack() as c2, nc.Block() as block:
            done = c2.enter_context(nc.semaphore("out_done"))

            @block.sync
            def _(sp):
                sp.dma_start(out, hidden[:, :]).then_inc(done, 16)
                sp.wait_ge(done, 16)


def ssm_layout(inp):
    import numpy as np
    f = np.float32
    x = np.asarray(inp["x"]).reshape(2, HALF, SEQ, D).transpose(0, 3, 1, 2).reshape(128, HALF * SEQ)
    w = np.zeros((128, SSM_W), f)
    A_log, Dp, Wdbc, Wdt, bdt = (np.asarray(inp["L0_tok_" + n]) for n in ("A_log", "D", "W_dbc", "W_dt", "b_dt"))
    for i in range(SSM_LAYERS):
        o = i * SSM_COLS
        for h in range(2):
            r = slice(64 * h, 64 * h + 64)
            w[r, o + 64 * h:o + 64 * h + 64] = Wdbc[i, 0][:, None]
            for c in range(2):
                w[r, o + SSM_WB + 128 * h + 64 * c:o + SSM_WB + 128 * h + 64 * c + 64] = Wdbc[i, 1:65].T
                w[r, o + SSM_WC + 128 * h + 64 * c:o + SSM_WC + 128 * h + 64 * c + 64] = Wdbc[i, 65:129].T
            w[r, o + SSM_VEC] = Wdt[i, :, 0]
            w[r, o + SSM_VEC + 1] = bdt[i]
            w[r, o + SSM_VEC + 2] = Dp[i]
            w[r, o + SSM_A:o + SSM_A + PAIRS] = A_log[i, h::2, :].T
        w[0:64, YSEL + 62] = 1
        w[64:128, YSEL + 63] = 1
    return {"x_in": np.ascontiguousarray(x), "ssm_w": w}


def post_layout(inp):
    import numpy as np
    f = np.float32
    W = np.zeros((128, PC.n), f)
    g = {k: np.asarray(v) for k, v in inp.items()}

    def at(name):
        o, n = PC.at[name]
        return W[:, o:o + n]

    def diag(name, m):
        at(name)[0:64, 0:64] = m
        at(name)[64:128, 64:128] = m

    def col(name, v):
        at(name)[0:64, 0] = v
        at(name)[64:128, 0] = v

    diag("mean", np.full((64, 64), 1 / 64, f))
    at("ident")[:] = np.eye(128, dtype=f)
    for e in (8, 16):
        at(f"rank{e}")[:] = e - np.arange(e, dtype=f)
    col("f0_gamma", g["L0_ffn_gamma"]); col("f0_beta", g["L0_ffn_beta"])
    col("a2_gamma", g["L2_attn_ln_gamma"]); col("a2_beta", g["L2_attn_ln_beta"])
    col("f3_gamma", g["L3_ffn_gamma"]); col("f3_beta", g["L3_ffn_beta"])
    wqkv, bqkv = g["L0_attn_W_qkv"], g["L0_attn_b_qkv"]
    att = {"L0": [wqkv[0:64].T, wqkv[64:128].T, wqkv[128:192].T, bqkv[0:64], bqkv[64:128], bqkv[128:192]],
           "L1": [g["L1_attn_Wq"].T, g["L1_attn_Wk"].T, g["L1_attn_Wv"].T, g["L1_attn_bq"], g["L1_attn_bk"], g["L1_attn_bv"]],
           "L2": [g["L2_attn_Wq"], g["L2_attn_Wk"], g["L2_attn_Wv"], g["L2_attn_bq"], g["L2_attn_bk"], g["L2_attn_bv"]],
           "L3": [g["L3_attn_Wq"].T, g["L3_attn_Wk"].T, g["L3_attn_Wv"].T, None, None, None]}
    scale = {"L0": 0.25, "L1": 1.0, "L2": 0.125, "L3": 0.125}
    for L, (wq, wk, wv, bq, bk, bv) in att.items():
        diag(L + "wq", wq); diag(L + "wk", wk); diag(L + "wv", wv)
        if bq is not None:
            col(L + "bq", bq); col(L + "bk", bk)
            at(L + "bv")[:, 0:64] = bv; at(L + "bv")[:, 64:128] = bv
        H = ATTN[L]["heads"]
        for v in range(2 * H):
            dh = 64 // H
            at(L + "mask")[v * dh:(v + 1) * dh, v] = scale[L]
    diag("L0wo", g["L0_attn_W_proj"].T); col("L0bo", g["L0_attn_b_proj"])
    diag("L2wo", g["L2_attn_Wout"]); col("L2bo", g["L2_attn_bout"])
    diag("L2wpos", g["L2_attn_Wpos"])
    pos = np.arange(TOK, dtype=f)[:, None]
    div = np.exp(np.arange(0, D, 2, dtype=f) * f(-np.log(10000.0) / D)).astype(f)
    pe = np.zeros((TOK, D), f)
    pe[:, 0::2] = np.sin(pos * div)
    pe[:, 1::2] = np.cos(pos * div)
    at("L2pe")[0:64] = pe.T; at("L2pe")[64:128] = pe.T
    col("L2u", g["L2_attn_u_bias"].reshape(64)); col("L2v", g["L2_attn_v_bias"].reshape(64))
    at("L1scale")[:, 0] = g["L1_attn_scale"][0]
    col("L2b2s", g["L2_ffn_b2s"])
    ffn = {"L0": ("L0_ffn_W1", "L0_ffn_b1", "L0_ffn_W2", "L0_ffn_b2", "L0_ffn_Wr"),
           "L1": ("L1_ffn_W1", "L1_ffn_b1", "L1_ffn_W2", "L1_ffn_b2", "L1_ffn_Wg"),
           "L2": ("L2_ffn_W1p", "L2_ffn_b1p", "L2_ffn_W2p", "L2_ffn_b2p", "L2_ffn_Wr"),
           "L3": ("L3_ffn_w1", "L3_ffn_b1", "L3_ffn_w2", "L3_ffn_b2", "L3_ffn_gate_w")}
    for L, names in ffn.items():
        W1, b1, W2, b2, wr = (g[n] for n in names)
        E, nbk = FFN[L]["E"], FFN[L]["blocks"]
        nblk = E * nbk + FFN[L]["shared"]
        w1 = at(L + "w1").reshape(128, 2, nblk, 128)
        w2 = at(L + "w2").reshape(128, nblk, 192)
        o1, o2 = PC.at[L + "w1"][0], PC.at[L + "w2"][0]
        srcs = [(W1[e][:, k * 128:(k + 1) * 128], b1[e][k * 128:(k + 1) * 128], W2[e][k * 128:(k + 1) * 128]) for e in range(E) for k in range(nbk)]
        if L == "L2":
            srcs += [(g["L2_ffn_W1s"][:, k * 128:(k + 1) * 128], g["L2_ffn_b1s"][k * 128:(k + 1) * 128], g["L2_ffn_W2s"][k * 128:(k + 1) * 128]) for k in range(2)]
        for n, (a, b, c) in enumerate(srcs):
            W[0:64, o1 + n * 128:o1 + n * 128 + 128] = a
            W[64:128, o1 + (nblk + n) * 128:o1 + (nblk + n) * 128 + 128] = a
            at(L + "b1")[:, n] = b
            W[:, o2 + n * 192 + 64:o2 + n * 192 + 128] = c
        at(L + "b2")[0:E, 0:64] = b2
        at(L + "b2")[E:2 * E, 64:128] = b2
        at(L + "wr")[0:64, 0:E] = wr
        at(L + "wr")[64:128, E:2 * E] = wr
    at("L0br")[:, 0:8] = g["L0_ffn_br"]; at("L0br")[:, 8:16] = g["L0_ffn_br"]
    at("L1br")[:, 0:8] = g["L1_ffn_bg"]; at("L1br")[:, 8:16] = g["L1_ffn_bias"]
    at("L3br")[:, 0:16] = g["L3_ffn_gate_b"]
    return {"post_w": W}


def kernel(**inputs):
    import numpy as np
    import concourse.bacc as bacc
    from concourse.bass_utils import run_bass_kernel_spmd
    nc = bacc.Bacc("TRN2", target_bir_lowering=False, num_devices=1)
    arrays = {**ssm_layout(inputs), **post_layout(inputs)}
    aps = {n: nc.dram_tensor(n, a.shape, mybir.dt.from_np(a.dtype), kind="ExternalInput").ap() for n, a in arrays.items()}
    out = nc.dram_tensor("out", (128, COLS), F32, kind="ExternalOutput").ap()
    build(nc, aps["x_in"], aps["ssm_w"], aps["post_w"], out)
    r = run_bass_kernel_spmd(nc, [arrays], core_ids=[0])
    y = r.results[0]["out"]
    return np.ascontiguousarray(y.reshape(2, D, HALF, TOK).transpose(0, 2, 3, 1)).reshape(BATCH, TOK, D)
```

```python
from contextlib import ExitStack

import concourse.bass as bass
from concourse import mybir

F32 = mybir.dt.float32
BF16 = mybir.dt.bfloat16
ACT = mybir.ActivationFunctionType
ALU = mybir.AluOpType
AX = mybir.AxisListType
ds = bass.ds

BATCH, SEQ, D, NSTATE, SSM_LAYERS = 16, 750, 64, 64, 3
HALF = BATCH // 2
LENS = [SEQ, SEQ // 2, SEQ // 4]
TOK = LENS[-1]
COLS = HALF * TOK
SLACK = 8
LOG_AND_EXP = "natural_log_exp_and_others"
PIECE = 512

SSM_WD, SSM_WB, SSM_WC = 0, 128, 384
SSM_VEC, SSM_A = 640, 643
SSM_COLS = 675
PAIRS = D // 2
YSEL = SSM_LAYERS * SSM_COLS
SSM_W = YSEL + 128


def pieces(width):
    return [(a, min(a + PIECE, width)) for a in range(0, width, PIECE)]


INPUT_DMAS = 32


def selector_of(pool, out, width, selected):
    pool.memset(out[:, :], 0.0).then_inc(selected, 1)
    pool.wait_ge(selected, 1)
    for s in range(3):
        view = out[32 * s:32 * s + 32, :].rearrange("p (c n) -> p c n", n=width)
        pool.affine_select(out=view, in_=view, compare_op=ALU.not_equal, fill=1.0, base=0,
                           pattern=[[-1, 32], [0, width]], channel_multiplier=1).then_inc(selected, 1)


def settle(eng, value):
    return value if isinstance(value, int) else eng.snap(eng.to_reg(value))


class Phases:

    def __init__(self, nc):
        self.nc, self.held, self.before, self.now = nc, [], [], []

    def open(self, phase):
        if len(self.held) == 2:
            self.held.pop(0).close()
        self.held.append(ExitStack())
        self.before, self.now, self.phase = self.now, [], phase
        return self

    def __call__(self, name):
        s = self.held[-1].enter_context(self.nc.semaphore(f"{self.phase}_{name}"))
        self.now.append(s)
        return s

    def clear_before(self, block):
        before = self.before

        @block.sync
        def _(sp):
            for s in before:
                sp.sem_clear(s)


def ssm_prep(nc, phases, inputs_loaded, layer, L, x, weights, b_rep, c_rep, split_dram):
    seqs = max(1, SEQ // L)
    width = seqs * L
    groups = HALF // seqs
    base = layer * SSM_COLS
    w = lambda a, n: weights[:, base + a:base + a + n]
    with ExitStack() as ctx:
        sb = lambda name, shape, dt: ctx.enter_context(nc.sbuf_tensor(f"prep{layer}_{name}", shape, dt))
        sem = phases.open(f"prep{layer}")
        raw = [ctx.enter_context(nc.psum_tensor(f"raw{layer}_{p}", [128, 1024], F32)) for p in range(2)]
        bc = [ctx.enter_context(nc.psum_tensor(f"bc{layer}_{p}", [128, 1024], F32)) for p in range(2)]
        z = [sb(f"z{p}", [128, width], F32) for p in range(2)]
        soft = [sb(f"soft{p}", [128, width], F32) for p in range(2)]
        val = [[sb(f"val{t}{p}", [128, width], F32) for p in range(2)] for t in range(2)]
        rest = [[sb(f"rest{t}{p}", [128, width], F32) for p in range(2)] for t in range(2)]
        part = [sb(f"part{p}", [128, 3, 2, width], BF16) for p in range(2)]
        raw_ready, z_ready, soft_ready, soft_step = sem("raw_ready"), sem("z_ready"), sem("soft_ready"), sem("soft_step")
        bc_ready, bc_even, bc_odd = sem("bc_ready"), sem("bc_even"), sem("bc_odd")
        val_ready, first_cut, rest_ready, second_cut, third_cut = (
            sem(n) for n in ("val_ready", "first_cut", "rest_ready", "second_cut", "third_cut"))
        stored = [sem(f"stored{p}") for p in range(2)]

        def run(eng, step):
            step(0, 0)
            step(1, 1)
            if groups > 2:
                with eng.Fori(0, groups // 2 - 1) as i:
                    step(2 * i + 2, 2)
                    step(2 * i + 3, 3)
            step(groups, groups)
            step(groups + 1, groups + 1)

        def has(s, back):
            return 0 <= s - back < groups

        with nc.Block() as block:
            phases.clear_before(block)

            @block.tensor
            def _(pe):
                def step(g, s):
                    if not has(s, 0):
                        return
                    p = s % 2
                    pe.wait_ge(z_ready, SLACK + g - 1)
                    for a, b in pieces(width):
                        mm = pe.matmul(raw[p][:, a:b], w(SSM_WD, 128), x[:, ds(g * width + a, b - a)],
                                       start=True, stop=True)
                    mm.then_inc(raw_ready, 1)
                    for q in range(4):
                        pe.wait_ge(bc_even if q % 2 == 0 else bc_odd, SLACK + 2 * g + q // 2)
                        for a, b in pieces(width):
                            mm = pe.matmul(bc[q % 2][:, a:b], w(SSM_WB + 128 * q, 128),
                                           x[:, ds(g * width + a, b - a)], start=True, stop=True)
                        mm.then_inc(bc_ready, 1)

                run(pe, step)

            def target(q):
                return (b_rep, c_rep)[q // 2], (q % 2) * HALF * L

            @block.vector
            def _(dve):
                def copy_projection(g, q):
                    dst, off = target(q)
                    dve.wait_ge(bc_ready, 4 * g + q + 1)
                    dve.tensor_copy(dst[:, ds(off + g * width, width)], bc[1][:, 0:width]).then_inc(bc_odd, 1)

                def step(g, s):
                    p = s % 2
                    if has(s, 0):
                        dve.wait_ge(raw_ready, g + 1)
                        dve.wait_ge(val_ready, SLACK + 2 * g)
                        dve.tensor_scalar(z[p][:, :], raw[p][:, 0:width], w(SSM_VEC, 1), w(SSM_VEC + 1, 1),
                                          ALU.mult, ALU.add).then_inc(z_ready, 1)
                    if has(s, 2):
                        for t in range(2):
                            dve.wait_ge(second_cut, SLACK + 2 * (g - 2) + t + 1)
                            dve.tensor_tensor(part[p][:, 2, t, :], rest[t][p][:, :], part[p][:, 1, t, :],
                                              ALU.subtract).then_inc(third_cut, 1)
                    if has(s, 0):
                        copy_projection(g, 1)
                        dve.wait_ge(soft_ready, g + 1)
                        dve.wait_ge(first_cut, SLACK + 2 * (g - 1))
                        dve.wait_ge(rest_ready, SLACK + 2 * (g - 1))
                        dve.scalar_tensor_tensor(val[0][p][:, :], z[p][:, :], 0.0, soft[p][:, :],
                                                 ALU.max, ALU.add).then_inc(val_ready, 1)
                        dve.wait_ge(val_ready, SLACK + 2 * g + 1)
                        dve.tensor_tensor(val[1][p][:, :], val[0][p][:, :], x[:, ds(g * width, width)],
                                          ALU.mult).then_inc(val_ready, 1)
                        copy_projection(g, 3)

                run(dve, step)

            @block.scalar
            def _(act):
                def step(g, s):
                    if has(s, 1):
                        p = (s - 1) % 2
                        turn = (s - 1) // 2 if isinstance(g, int) else (g - s) // 2 + (s - 1) // 2
                        act.wait_ge(stored[p], SLACK + 64 * turn)
                        for t in range(2):
                            act.wait_ge(val_ready, SLACK + 2 * (g - 1) + t + 1)
                            act.activation(part[p][:, 0, t, :], val[t][p][:, :], ACT.Copy).then_inc(first_cut, 1)
                    if has(s, 0):
                        p = s % 2
                        act.wait_ge(z_ready, SLACK + g + 1)
                        act.activation(soft[p][:, :], z[p][:, :], ACT.Abs).then_inc(soft_step, 1)
                        act.wait_ge(soft_step, 2 * g + 1)
                        act.activation(soft[p][:, :], soft[p][:, :], ACT.Exp, scale=-1.0).then_inc(soft_step, 1)
                        act.wait_ge(soft_step, 2 * g + 2)
                        act.activation(soft[p][:, :], soft[p][:, :], ACT.Ln, bias=1.0).then_inc(soft_ready, 1)
                        for q in (0, 2):
                            dst, off = target(q)
                            projected = settle(act, 4 * g + q + 1)
                            act.wait_ge(inputs_loaded, INPUT_DMAS)
                            act.wait_ge(bc_ready, projected)
                            act.activation(dst[:, ds(off + g * width, width)], bc[0][:, 0:width],
                                           ACT.Copy).then_inc(bc_even, 1)
                    if has(s, 1):
                        p = (s - 1) % 2
                        for t in range(2):
                            act.wait_ge(rest_ready, SLACK + 2 * (g - 1) + t + 1)
                            act.activation(part[p][:, 1, t, :], rest[t][p][:, :], ACT.Copy).then_inc(second_cut, 1)

                act.preload_act_table_set(LOG_AND_EXP)
                run(act, step)

            @block.gpsimd
            def _(pool):
                def step(g, s):
                    if not has(s, 1):
                        return
                    p = (s - 1) % 2
                    for t in range(2):
                        pool.wait_ge(first_cut, SLACK + 2 * (g - 1) + t + 1)
                        pool.tensor_tensor(rest[t][p][:, :], val[t][p][:, :], part[p][:, 0, t, :],
                                           ALU.subtract).then_inc(rest_ready, 1)

                for free in (z_ready, bc_even, bc_odd, val_ready, first_cut, rest_ready, second_cut, third_cut,
                             stored[0], stored[1]):
                    pool.sem_inc(free, SLACK)
                run(pool, step)

            @block.sync
            def _(sp):
                def step(g, s):
                    if not has(s, 2):
                        return
                    p = s % 2
                    sp.wait_ge(third_cut, SLACK + 2 * (g - 2) + 2)
                    for h in range(2):
                        for e in range(2):
                            dst = split_dram[ds(g - 2 + h * groups, 1), e].rearrange("a (s r) t w -> (a r) s (t w)", s=3)
                            src = part[p][64 * h + 32 * e:64 * h + 32 * e + 32, :, :, :]
                            sp.dma_start(dst, src.rearrange("r s t w -> r s (t w)")).then_inc(stored[p], 16)

                run(sp, step)
                for p in range(2):
                    sp.wait_ge(stored[p], SLACK + 64 * (groups // 2))


def ssm_scan(nc, phases, inputs_loaded, layer, L, weights, selector, a_neg, b_rep, c_rep, split_dram, y_dram):
    seqs = max(1, SEQ // L)
    width = seqs * L
    turns = 2 * HALF // seqs
    with ExitStack() as ctx:
        sb = lambda name, shape, dt: ctx.enter_context(nc.sbuf_tensor(f"scan{layer}_{name}", shape, dt))
        sem = phases.open(f"scan{layer}")
        decay = [ctx.enter_context(nc.psum_tensor(f"decay{layer}_{p}", [128, 1024], F32)) for p in range(2)]
        spread = ctx.enter_context(nc.psum_tensor(f"spread{layer}", [128, 1024], F32))
        y_sum = ctx.enter_context(nc.psum_tensor(f"ysum{layer}", [64, 1024], F32))
        stack = [sb(f"stack{e}", [96, 2, width], BF16) for e in range(2)]
        dbx = [sb(f"dbx{p}", [128, width], F32) for p in range(4)]
        state = [sb(f"state{p}", [128, width], F32) for p in range(2)]
        weighed = [sb(f"weighed{p}", [128, width], F32) for p in range(2)]
        y_out = sb("y_out", [64, width], F32)
        loaded = [sem(f"loaded{e}") for e in range(2)]
        delta_ready, spread_ready, decay_ready = sem("delta_ready"), sem("spread_ready"), sem("decay_ready")
        dbx_ready, scanned, weighed_ready = sem("dbx_ready"), sem("scanned"), sem("weighed_ready")
        y_added, y_copied, y_stored = sem("y_added"), sem("y_copied"), sem("y_stored")

        with nc.Block() as block:
            phases.clear_before(block)

            @block.sync
            def _(sp):
                def load(j, e, first):
                    if not first:
                        sp.wait_ge(delta_ready, PAIRS * (j - 1) + 16 * (e + 1))
                        sp.wait_ge(spread_ready, PAIRS * (j - 1) + 16 * (e + 1))
                    sp.dma_start(stack[e][:, :, :],
                                 split_dram[ds(j, 1), e].rearrange("a q t w -> (a q) t w")).then_inc(loaded[e], 16)

                def store(j):
                    sp.wait_ge(y_copied, SLACK + j + 1)
                    sp.dma_start(y_dram[ds(j, 1)].rearrange("a e w -> (a e) w"), y_out[:, :]).then_inc(y_stored, 16)

                load(0, 0, True)
                load(0, 1, True)
                with sp.Fori(0, turns - 1) as i:
                    load(i + 1, 0, False)
                    load(i + 1, 1, False)
                    store(i)
                store(turns - 1)
                sp.wait_ge(y_stored, SLACK + 16 * turns)

            @block.tensor
            def _(pe):
                def spread_delta(j, k):
                    e, u = k // 16, PAIRS * j + k
                    if not (isinstance(j, int) and j == 0 and k < 2):
                        pe.wait_ge(scanned, u - 1)
                    for a, b in pieces(width):
                        mm = pe.matmul(decay[k % 2][:, a:b], selector[:, 128 * (k % 16):128 * (k % 16) + 128],
                                       stack[e][:, 0, a:b], start=True, stop=True)
                    mm.then_inc(delta_ready, 1)

                def spread_dx(j, k):
                    e, u = k // 16, PAIRS * j + k
                    if k % 16 == 0:
                        pe.wait_ge(loaded[e], 16 * (j + 1))
                    if not (isinstance(j, int) and u == 0):
                        pe.wait_ge(dbx_ready, u)
                    for a, b in pieces(width):
                        mm = pe.matmul(spread[:, a:b], selector[:, 128 * (k % 16):128 * (k % 16) + 128],
                                       stack[e][:, 1, a:b], start=True, stop=True)
                    mm.then_inc(spread_ready, 1)

                def sum_states(j, k, part):
                    u = PAIRS * j + k
                    if part == 0:
                        pe.wait_ge(weighed_ready, u + 1)
                        if k == 0:
                            pe.wait_ge(y_copied, SLACK + j)
                    lhs = weights[:, YSEL + 62 - 2 * k:YSEL + 126 - 2 * k]
                    a, b = pieces(width)[part]
                    mm = pe.matmul(y_sum[:, a:b], lhs, weighed[k % 2][:, a:b], start=(k == 0), stop=(k == PAIRS - 1))
                    if part == 1:
                        mm.then_inc(y_added, 1)

                def step(j, k, first=False, last=False):
                    nj, nk = (j, k + 1) if k + 1 < PAIRS else (j + 1, 0)
                    sj, sk = (j, k - 2) if k >= 2 else (j - 1, k - 2 + PAIRS)
                    sums, spreads = not (first and k < 2), not (last and k == PAIRS - 1)
                    if spreads:
                        spread_dx(nj, nk)
                    if k == 2:
                        spread_delta(nj, nk)
                    if sums:
                        sum_states(sj, sk, 0)
                    if k != 2 and spreads:
                        spread_delta(nj, nk)
                    if sums:
                        sum_states(sj, sk, 1)

                spread_dx(0, 0)
                spread_delta(0, 0)
                for k in range(2):
                    step(0, k, first=True)
                with pe.Fori(0, turns - 1) as i:
                    for k in range(2, PAIRS):
                        step(i, k)
                    for k in range(2):
                        step(i + 1, k)
                for k in range(2, PAIRS):
                    step(turns - 1, k, last=True)
                for k in (PAIRS - 2, PAIRS - 1):
                    for part in range(2):
                        sum_states(turns - 1, k, part)

            @block.scalar
            def _(act):
                def decays(j, ks):
                    for k in ks:
                        act.wait_ge(delta_ready, PAIRS * j + k + 1)
                        act.activation(decay[k % 2][:, 0:width], decay[k % 2][:, 0:width], ACT.Exp,
                                       scale=a_neg[:, PAIRS * layer + k:PAIRS * layer + k + 1]).then_inc(decay_ready, 1)

                def copy_sums(j, first):
                    act.wait_ge(y_added, PAIRS * (j + 1))
                    if not first:
                        act.wait_ge(y_stored, SLACK + 16 * j)
                    act.activation(y_out[:, :], y_sum[:, 0:width], ACT.Copy).then_inc(y_copied, 1)

                decays(0, range(3))
                with act.Fori(0, turns - 1) as i:
                    decays(i, range(3, PAIRS))
                    decays(i + 1, range(3))
                    copy_sums(i, False)
                decays(turns - 1, range(3, PAIRS))
                copy_sums(turns - 1, False)

            @block.vector
            def _(dve):
                def product(j, k):
                    dve.wait_ge(spread_ready, PAIRS * j + k + 1)
                    dve.tensor_tensor(dbx[k % 4][:, :], spread[:, 0:width], b_rep[:, ds(j * width, width)],
                                      ALU.mult).then_inc(dbx_ready, 1)

                def scan(j, k):
                    u = PAIRS * j + k
                    dve.wait_ge(decay_ready, u + 1)
                    dve.wait_ge(dbx_ready, u + 1)
                    if not (isinstance(j, int) and j == 0 and k < 2):
                        dve.wait_ge(weighed_ready, u - 1)
                    for s in range(seqs):
                        sl = slice(s * L, (s + 1) * L)
                        op = dve.tensor_tensor_scan(state[k % 2][:, sl], decay[k % 2][:, sl], dbx[k % 4][:, sl],
                                                    0.0, ALU.mult, ALU.add)
                    op.then_inc(scanned, 1)

                def turn(j, first, last):
                    for k in range(PAIRS):
                        if k + 1 < PAIRS:
                            product(j, k + 1)
                        elif not last:
                            product(j + 1, 0)
                        scan(j, k)

                product(0, 0)
                turn(0, True, False)
                with dve.Fori(1, turns - 1) as i:
                    turn(i, False, False)
                turn(turns - 1, False, True)

            @block.gpsimd
            def _(pool):
                def weigh(j, k):
                    u = PAIRS * j + k
                    here, before = settle(pool, u + 1), settle(pool, u - 1)
                    pool.wait_ge(inputs_loaded, INPUT_DMAS)
                    pool.wait_ge(scanned, here)
                    if not (isinstance(j, int) and j == 0 and k < 2):
                        pool.wait_ge(y_added, before)
                    pool.tensor_tensor(weighed[k % 2][:, :], state[k % 2][:, :], c_rep[:, ds(j * width, width)],
                                       ALU.mult).then_inc(weighed_ready, 1)

                pool.sem_inc(y_copied, SLACK)
                pool.sem_inc(y_stored, SLACK)
                for k in range(PAIRS):
                    weigh(0, k)
                with pool.Fori(1, turns) as i:
                    for k in range(PAIRS):
                        weigh(i, k)


def ssm_finish(nc, phases, layer, L, x, out, weights, y_dram):
    seqs = max(1, SEQ // L)
    width = seqs * L
    groups = HALF // seqs
    vec = weights[:, layer * SSM_COLS + SSM_VEC + 2:layer * SSM_COLS + SSM_VEC + 3]
    with ExitStack() as ctx:
        sem = phases.open(f"fin{layer}")
        y = ctx.enter_context(nc.sbuf_tensor(f"fin{layer}_y", [128, groups, width], F32))
        loaded, summed, pooled = sem("loaded"), sem("summed"), sem("pooled")
        with nc.Block() as block:
            phases.clear_before(block)

            @block.sync
            def _(sp):
                src = y_dram.rearrange("(h g) e w -> h e g w", h=2)
                for h in range(2):
                    sp.dma_start(y[64 * h:64 * h + 64, :, :], src[h]).then_inc(loaded, 16)

            @block.vector
            def _(dve):
                dve.wait_ge(loaded, 32)
                flat = y[:, :, :].rearrange("p g w -> p (g w)")
                if layer == SSM_LAYERS - 1:
                    dve.scalar_tensor_tensor(out[:, 0:COLS], x[:, 0:HALF * L], vec, flat, ALU.mult, ALU.add).then_inc(summed, 1)
                else:
                    half = L // 2
                    dve.scalar_tensor_tensor(flat, x[:, 0:HALF * L], vec, flat, ALU.mult, ALU.add).then_inc(summed, 1)
                    dve.wait_ge(summed, 1)
                    seq = flat.rearrange("p (b l) -> p b l", l=L)
                    pair = seq[:, :, 0:2 * half].rearrange("p b (l two) -> p b l two", two=2)
                    dst = out[:, 0:HALF * half].rearrange("p (b l) -> p b l", l=half)
                    dve.tensor_tensor(dst, pair[:, :, :, 0], pair[:, :, :, 1], ALU.add).then_inc(pooled, 1)
                    dve.wait_ge(pooled, 1)
                    dve.tensor_scalar(dst, dst, 0.5, None, ALU.mult).then_inc(pooled, 1)


CHUNKS = 4
CHUNK = COLS // CHUNKS
GT = 88
GTILES = COLS // GT
QN, QO = [94, 93], [0, 94]


class Columns:

    def __init__(self):
        self.at, self.n = {}, 0

    def add(self, name, n):
        self.at[name] = (self.n, n)
        self.n += n


ATTN = {"L0": dict(heads=4, proj=True, pos=False), "L1": dict(heads=1, proj=False, pos=False),
        "L2": dict(heads=4, proj=True, pos=True), "L3": dict(heads=1, proj=False, pos=False)}
FFN = {"L0": dict(E=8, blocks=1, shared=0, act="Gelu", softmax_first=False),
       "L1": dict(E=8, blocks=1, shared=0, act="Relu", softmax_first=False),
       "L2": dict(E=8, blocks=2, shared=2, act="Gelu", softmax_first=True),
       "L3": dict(E=16, blocks=1, shared=0, act="Relu", softmax_first=False)}


def post_columns():
    c = Columns()
    c.add("mean", 128)
    c.add("ident", 128)
    for e in (8, 16):
        c.add(f"rank{e}", e)
    for n in ("f0_gamma", "f0_beta", "a2_gamma", "a2_beta", "f3_gamma", "f3_beta"):
        c.add(n, 1)
    for L, a in ATTN.items():
        for n in ("wq", "wk", "wv", "bv"):
            c.add(L + n, 128)
        for n in ("bq", "bk"):
            c.add(L + n, 1)
        c.add(L + "mask", 2 * a["heads"])
        if a["proj"]:
            c.add(L + "wo", 128)
            c.add(L + "bo", 1)
        if a["pos"]:
            c.add(L + "wpos", 128)
            c.add(L + "pe", TOK)
            c.add(L + "u", 1)
            c.add(L + "v", 1)
    c.add("L1scale", 1)
    for L, f in FFN.items():
        nb = f["E"] * f["blocks"] + f["shared"]
        c.add(L + "w1", 2 * nb * 128)
        c.add(L + "b1", nb)
        c.add(L + "w2", nb * 192)
        c.add(L + "b2", 128)
        c.add(L + "wr", 2 * f["E"])
        c.add(L + "br", 2 * f["E"])
    c.add("L2b2s", 1)
    return c


PC = post_columns()


class Post:

    def __init__(self, nc, phases, W, sel, hidden, ready):
        self.phases = phases
        self.nc, self.W, self.sel, self.hidden, self.ready = nc, W, sel, hidden, ready
        self.phase = 0

    def w(self, name, a=0, n=None):
        o, size = PC.at[name]
        return self.W[:, o + a:o + a + (size - a if n is None else n)]

    def sems(self, ctx, kind):
        self.phase += 1
        return self.phases.open(f"p{self.phase}{kind}")

    def norm(self, src, dst, affine=None):
        with ExitStack() as ctx:
            sem = self.sems(ctx, "norm")
            nc, tag = self.nc, f"n{self.phase}"
            mean = ctx.enter_context(nc.psum_tensor(tag + "mean", [128, CHUNKS, PIECE], F32))
            var = ctx.enter_context(nc.psum_tensor(tag + "var", [128, CHUNKS, PIECE], F32))
            centred = ctx.enter_context(nc.sbuf_tensor(tag + "c", [128, COLS], F32))
            squares = ctx.enter_context(nc.sbuf_tensor(tag + "s", [128, COLS], F32))
            rstd = ctx.enter_context(nc.sbuf_tensor(tag + "r", [128, COLS], F32))
            eps = ctx.enter_context(nc.sbuf_tensor(tag + "e", [128, 1], F32))
            meaned, centred_r, squared, var_r, log_r, rstd_r, out_r, eps_r = (
                sem(n) for n in ("meaned", "centred", "squared", "var", "log", "rstd", "out", "eps"))
            with nc.Block() as block:
                self.phases.clear_before(block)

                @block.tensor
                def _(pe):
                    with pe.Fori(0, CHUNKS) as c:
                        pe.matmul(mean[:, ds(c, 1), 0:CHUNK].rearrange("p a n -> p (a n)"), self.w("mean"),
                                  src[:, ds(c * CHUNK, CHUNK)], start=True, stop=True).then_inc(meaned, 1)
                    with pe.Fori(0, CHUNKS) as c:
                        pe.wait_ge(squared, c + 1)
                        pe.matmul(var[:, ds(c, 1), 0:CHUNK].rearrange("p a n -> p (a n)"), self.w("mean"),
                                  squares[:, ds(c * CHUNK, CHUNK)], start=True, stop=True).then_inc(var_r, 1)

                @block.vector
                def _(dve):
                    dve.memset(eps[:, :], 1e-5).then_inc(eps_r, 1)
                    with dve.Fori(0, CHUNKS) as c:
                        dve.wait_ge(meaned, c + 1)
                        dve.tensor_tensor(centred[:, ds(c * CHUNK, CHUNK)], src[:, ds(c * CHUNK, CHUNK)],
                                          mean[:, ds(c, 1), 0:CHUNK].rearrange("p a n -> p (a n)"),
                                          ALU.subtract).then_inc(centred_r, 1)
                    with dve.Fori(0, CHUNKS) as c:
                        cols = ds(c * CHUNK, CHUNK)
                        dve.wait_ge(rstd_r, c + 1)
                        dve.tensor_tensor(dst[:, cols], centred[:, cols], rstd[:, cols], ALU.mult).then_inc(out_r, 1)
                        if affine:
                            dve.wait_ge(out_r, 2 * c + 1)
                            dve.tensor_scalar(dst[:, cols], dst[:, cols], self.w(affine[0]), self.w(affine[1]),
                                              ALU.mult, ALU.add).then_inc(out_r, 1)

                @block.scalar
                def _(act):
                    act.preload_act_table_set(LOG_AND_EXP)
                    act.wait_ge(eps_r, 1)
                    with act.Fori(0, CHUNKS) as c:
                        cols = ds(c * CHUNK, CHUNK)
                        here = settle(act, c + 1)
                        act.wait_ge(self.ready[0], self.ready[1])
                        act.wait_ge(centred_r, here)
                        act.activation(squares[:, cols], centred[:, cols], ACT.Square).then_inc(squared, 1)
                    with act.Fori(0, CHUNKS) as c:
                        cols = ds(c * CHUNK, CHUNK)
                        here = settle(act, c + 1)
                        act.wait_ge(self.ready[0], self.ready[1])
                        act.wait_ge(var_r, here)
                        act.activation(rstd[:, cols], var[:, ds(c, 1), 0:CHUNK].rearrange("p a n -> p (a n)"),
                                       ACT.Ln, bias=eps[:, 0:1]).then_inc(log_r, 1)
                        act.wait_ge(self.ready[0], self.ready[1])
                        act.wait_ge(log_r, here)
                        act.activation(rstd[:, cols], rstd[:, cols], ACT.Exp, scale=-0.5).then_inc(rstd_r, 1)

    def attention(self, L, xn):
        a = ATTN[L]
        H, pos = a["heads"], a["pos"]
        NV, G = (4, 2) if H == 4 else (2, 1)
        dh = D // H
        NI = 2 * G
        NH = NV * G
        nc, hidden = self.nc, self.hidden
        with ExitStack() as ctx:
            sem = self.sems(ctx, "attn")
            tag = f"at{L}"
            sb = lambda name, shape, dt=F32: ctx.enter_context(nc.sbuf_tensor(tag + name, shape, dt))
            ps = lambda name, shape: ctx.enter_context(nc.psum_tensor(tag + name, shape, F32))
            xb = [sb(f"x{p}", [128, TOK]) for p in range(2)]
            qz = [sb(f"q{p}", [128, NH, TOK]) for p in range(2)]
            qs = [sb(f"qs{p}", [128, TOK]) for p in range(2)]
            ks = [sb(f"k{p}", [128, TOK]) for p in range(2)]
            vz = [[sb(f"v{p}{t}", [128, NH * (128 + dh)]) for t in range(2)] for p in range(2)]
            prob = [sb(f"p{p}", [128, NV, TOK]) for p in range(2)]
            probT = [[sb(f"pt{p}{t}", [128, NV, 94]) for t in range(2)] for p in range(2)]
            top = [sb(f"m{p}", [128, NV]) for p in range(2)]
            total = [sb(f"t{p}", [128, NV]) for p in range(2)]
            inv = [sb(f"i{p}", [128, NV]) for p in range(2)]
            o_s = [sb(f"o{p}", [128, TOK]) for p in range(2)]
            mask = sb("mask", [128, NH])
            rscale = sb("rscale", [128, 1])
            bias = sb("bias", [128, 2])
            nb = NV // 2
            S = [ps(f"S{p}", [128, nb, PIECE]) for p in range(2)]
            T = ps("T", [128, 2, PIECE])
            O = ps("O", [128, PIECE])
            M = ps("M", [128, PIECE])
            V = M if a["proj"] else ps("V", [128, PIECE])
            set_up, credit, pos_proj = sem("set_up"), sem("credit"), sem("pos_proj")
            pos_x, pos_q, pos_masked, pos_scored, pos_copied = (
                sem(n) for n in ("pos_x", "pos_q", "pos_masked", "pos_scored", "pos_copied"))
            pos_stored = [sem(f"pos_stored{k}") for k in range(2)]
            shifted_in = [sem(f"shifted_in{k}") for k in range(2)]
            x_copied, qk_ready, qk_copied, masked_dve, masked_pool, v_ready, v_placed, o_copied, projected, added_in = (
                sem(n) for n in ("x_copied", "qk_ready", "qk_copied", "masked_dve", "masked_pool", "v_ready", "v_placed",
                                 "o_copied", "projected", "added_in"))
            scored, pos_added, maxed, exped, inverted, normalised, turned, turned_a, turned_v, valued = (
                sem(n) for n in ("scored", "pos_added", "maxed", "exped", "inverted", "normalised", "turned", "turned_a",
                                 "turned_v", "valued"))
            if pos:
                skew = nc.dram_tensor(f"skew{L}", (8, NH, TOK * (TOK + 1)), F32, kind="Internal").ap()
                shifted = [sb(f"sh{p}", [128, NV, TOK]) for p in range(2)]
                score = [sb(f"sc{p}", [128, NV, TOK]) for p in range(2)]
                posT = sb("posT", [128, TOK])
                padded = [sb(f"pad{p}", [128, NV, TOK + 1]) for p in range(2)]

            def s_view(m, n):
                return S[m % 2][0:n, :, 0:2 * TOK]

            with nc.Block() as block:
                self.phases.clear_before(block)

                @block.gpsimd
                def _(pool):
                    for p in range(2):
                        for t in range(2):
                            pool.memset(vz[p][t][:, :], 0.0).then_inc(set_up, 1)
                        if pos:
                            pool.memset(padded[p][:, :, 0:1], 0.0).then_inc(set_up, 1)
                    for free in (pos_q, pos_masked, pos_scored, pos_copied, v_placed, o_copied, added_in,
                                 pos_added, exped, turned, turned_a, turned_v, valued):
                        pool.sem_inc(free, SLACK)
                    for k in range(2):
                        pool.sem_inc(pos_stored[k], SLACK)

                @block.vector
                def _(dve):
                    if L == "L1":
                        dve.reciprocal(rscale[:, :], self.w("L1scale")).then_inc(credit, 1)
                        dve.wait_ge(credit, 1)
                        dve.tensor_scalar(mask[:, :], self.w(L + "mask"), rscale[:, 0:1], None, ALU.mult).then_inc(credit, 1)
                    else:
                        dve.tensor_copy(mask[:, :], self.w(L + "mask")).then_inc(credit, 1)
                    if pos:
                        dve.tensor_tensor(bias[:, 0:1], self.w(L + "bq"), self.w(L + "u"), ALU.add).then_inc(credit, 1)
                        dve.tensor_tensor(bias[:, 1:2], self.w(L + "bq"), self.w(L + "v"), ALU.add).then_inc(credit, 1)
                    else:
                        dve.tensor_copy(bias[:, 0:1], self.w(L + "bq")).then_inc(credit, 1)

                if pos:
                    @block.tensor
                    def _(pe):
                        pe.matmul(M[:, 0:TOK], self.w(L + "wpos"), self.w(L + "pe"), start=True, stop=True).then_inc(pos_proj, 1)

                    @block.scalar
                    def _(act):
                        act.wait_ge(pos_proj, 1)
                        act.activation(posT[:, :], M[:, 0:TOK], ACT.Copy).then_inc(pos_proj, 1)

            if pos:
                with nc.Block() as block:
                    @block.gpsimd
                    def _(pool):
                        with pool.Fori(0, 4) as i:
                            for p in range(2):
                                b = 2 * i + p
                                free = settle(pool, SLACK + b - 1)
                                pool.wait_ge(self.ready[0], self.ready[1])
                                pool.wait_ge(pos_q, free)
                                pool.tensor_copy(xb[p][:, :], xn[:, ds(b * TOK, TOK)]).then_inc(pos_x, 1)

                    @block.tensor
                    def _(pe):
                        with pe.Fori(0, 4) as i:
                            for p in range(2):
                                b = 2 * i + p
                                pe.wait_ge(pos_x, b + 1)
                                pe.wait_ge(pos_masked, SLACK + b)
                                pe.matmul(M[:, 0:TOK], self.w(L + "wq"), xb[p][:, :], start=True, stop=True).then_inc(pos_q, 1)
                                pe.wait_ge(pos_masked, SLACK + b + 1)
                                for m in range(NI):
                                    t, g = m // G, m % G
                                    n = QN[t]
                                    pe.wait_ge(pos_copied, SLACK + b * NI + m - 1)
                                    for v in range(NV):
                                        mm = pe.matmul(S[m % 2][0:n, v // 2, (v % 2) * TOK:(v % 2) * TOK + TOK],
                                                       qz[p][:, g * NV + v, QO[t]:QO[t] + n], posT[:, :],
                                                       start=True, stop=True)
                                    mm.then_inc(pos_scored, 1)

                    @block.vector
                    def _(dve):
                        with dve.Fori(0, 4) as i:
                            for p in range(2):
                                b = 2 * i + p
                                dve.wait_ge(pos_q, SLACK + b + 1)
                                dve.wait_ge(pos_scored, SLACK + NI * (b - 1))
                                for v in range(NH):
                                    op = dve.tensor_scalar(qz[p][:, v, :], M[:, 0:TOK], bias[:, 1:2], mask[:, v:v + 1],
                                                           ALU.add, ALU.mult)
                                op.then_inc(pos_masked, 1)

                    @block.scalar
                    def _(act):
                        with act.Fori(0, 4) as i:
                            for p in range(2):
                                b = 2 * i + p
                                for m in range(NI):
                                    n = QN[m // G]
                                    act.wait_ge(pos_scored, SLACK + b * NI + m + 1)
                                    act.wait_ge(pos_stored[m % 2], SLACK + 16 * (i * NI + (p * NI + m) // 2))
                                    act.activation(padded[m % 2][0:n, :, 1:TOK + 1].rearrange("p (a v) n -> p a v n", a=nb),
                                                   s_view(m, n).rearrange("p a (v n) -> p a v n", v=2),
                                                   ACT.Copy).then_inc(pos_copied, 1)

                    @block.sync
                    def _(sp):
                        with sp.Fori(0, 4) as i:
                            for p in range(2):
                                b = 2 * i + p
                                for m in range(NI):
                                    t, g = m // G, m % G
                                    sp.wait_ge(pos_copied, SLACK + b * NI + m + 1)
                                    dst = skew[ds(b, 1), g * NV:(g + 1) * NV, QO[t] * (TOK + 1):(QO[t] + QN[t]) * (TOK + 1)]
                                    sp.dma_start(dst.rearrange("o v (q n) -> (o q) v n", n=TOK + 1),
                                                 padded[m % 2][0:QN[t], :, :]).then_inc(pos_stored[m % 2], 16)
                        for k in range(2):
                            sp.wait_ge(pos_stored[k], SLACK + 16 * 4 * NI)

            n_items, per_turn = 8 * NI, 2 * NI
            V_AHEAD = 3 if a["proj"] else 2
            FIRST, START = -4, 3
            TURNS = (n_items - START - 5) // per_turn
            END = n_items + (NI - 2 if a["proj"] else 0)

            class At:

                def __init__(self, i, s):
                    self.i, self.s = i, s

                def item(self, ahead):
                    x = self.s + ahead
                    if self.i is None:
                        return (x, x % per_turn) if 0 <= x < n_items else None
                    return self.i * per_turn + x, x % per_turn

                def batch(self, ahead, back=0):
                    x = self.s + ahead
                    if x % NI:
                        return None
                    b = x // NI - back
                    if self.i is None:
                        return (b, b % 2) if 0 <= b < 8 else None
                    return self.i * 2 + b, b % 2

            def run(eng, step):
                for s_ in range(FIRST, START):
                    step(At(None, s_))
                with eng.Fori(0, TURNS) as i:
                    for s_ in range(START, START + per_turn):
                        step(At(i, s_))
                for s_ in range(START + TURNS * per_turn, END + 1):
                    step(At(None, s_))

            def place(m):
                t, g = m % NI // G, m % NI % G
                return t, g, QN[t]

            with nc.Block() as block:
                masked_here = NH // 2

                @block.gpsimd
                def _(pool):
                    def step(at):
                        if at.batch(5):
                            b, p = at.batch(5)
                            free = settle(pool, SLACK + b - 1)
                            pool.wait_ge(self.ready[0], self.ready[1])
                            pool.wait_ge(v_placed, free)
                            pool.tensor_copy(xb[p][:, :], xn[:, ds(b * TOK, TOK)]).then_inc(x_copied, 1)
                        if at.batch(4):
                            b, p = at.batch(4)
                            here = settle(pool, b + 1)
                            pool.wait_ge(self.ready[0], self.ready[1])
                            pool.wait_ge(qk_copied, here)
                            for v in range(masked_here, NH):
                                op = pool.tensor_scalar(qz[p][:, v, :], qs[p][:, :], mask[:, v:v + 1], None, ALU.mult)
                            op.then_inc(masked_pool, 1)

                    step(At(None, FIRST - 1))
                    run(pool, step)

                if pos:
                    @block.sync
                    def _(sp):
                        with sp.Fori(0, 4) as i:
                            for x in range(per_turn):
                                t, g, n = place(x)
                                u, b = i * per_turn + x, 2 * i + x // NI
                                sp.wait_ge(pos_added, SLACK + u - 1)
                                src = skew[ds(b, 1), g * NV:(g + 1) * NV, TOK * (1 + QO[t]):TOK * (1 + QO[t] + n)]
                                sp.dma_start(shifted[x % 2][0:n, :, :],
                                             src.rearrange("o v (q n) -> (o q) v n", n=TOK)).then_inc(shifted_in[x % 2], 16)

                @block.tensor
                def _(pe):
                    def step(at):
                        if at.batch(4):
                            b, p = at.batch(4)
                            pe.wait_ge(x_copied, b + 1)
                            if a["proj"]:
                                pe.wait_ge(v_placed, SLACK + b)
                                pe.wait_ge(added_in, SLACK + b - 2)
                            elif not (isinstance(b, int) and b == 0):
                                pe.wait_ge(qk_copied, b)
                            pe.matmul(M[:, 0:TOK], self.w(L + "wq"), xb[p][:, :], start=True, stop=True)
                            pe.matmul(M[:, TOK:2 * TOK], self.w(L + "wk"), xb[p][:, :], start=True,
                                      stop=True).then_inc(qk_ready, 1)
                        if at.item(3):
                            u, x = at.item(3)
                            t, g, n = place(x)
                            p = x // NI
                            b = u // NI if at.i is None else at.i * 2 + (at.s + 3) // NI
                            if x % NI == 0:
                                pe.wait_ge(masked_dve, b + 1)
                            if x % NI == G - 1:
                                pe.wait_ge(masked_pool, b + 1)
                            pe.wait_ge(exped, SLACK + u - 1)
                            if pos:
                                pe.wait_ge(pos_added, SLACK + u - 1)
                            for v in range(NV):
                                mm = pe.matmul(S[x % 2][0:n, v // 2, (v % 2) * TOK:(v % 2) * TOK + TOK],
                                               qz[p][:, g * NV + v, QO[t]:QO[t] + n], ks[p][:, :], start=True, stop=True)
                            mm.then_inc(scored, 1)
                        if at.item(1):
                            u, x = at.item(1)
                            n = place(x)[2]
                            pe.wait_ge(normalised, u + 1)
                            pe.wait_ge(turned_a, SLACK + u)
                            pe.wait_ge(turned_v, SLACK + u)
                            for t in range(2):
                                for v in range(NV):
                                    mm = pe.transpose(T[0:QN[t], t, v * 94:v * 94 + n],
                                                      prob[x % 2][0:n, v, QO[t]:QO[t] + QN[t]], self.w("ident")[0:n, 0:n])
                            mm.then_inc(turned, 1)
                        if at.batch(V_AHEAD):
                            b, p = at.batch(V_AHEAD)
                            pe.wait_ge(qk_copied, b + 1)
                            pe.wait_ge(v_placed, SLACK + b)
                            for t in range(2):
                                mm = pe.matmul(V[0:QN[t], 128 * t:128 * t + 128], xb[p][:, QO[t]:QO[t] + QN[t]],
                                               self.w(L + "wv"), start=True, stop=True)
                            mm.then_inc(v_ready, 1)
                        if a["proj"] and at.batch(2, back=2):
                            b, p = at.batch(2, back=2)
                            pe.wait_ge(o_copied, SLACK + b + 1)
                            pe.wait_ge(added_in, SLACK + b)
                            pe.wait_ge(v_placed, SLACK + (min(b + 3, 8) if at.i is None else b + 3))
                            pe.matmul(M[:, 0:TOK], self.w(L + "wo"), o_s[p][:, :], start=True, stop=True).then_inc(projected, 1)
                        if at.item(0):
                            u, x = at.item(0)
                            t, g, n = place(x)
                            p = x // NI
                            pe.wait_ge(turned_a, SLACK + u + 1)
                            pe.wait_ge(turned_v, SLACK + u + 1)
                            if x % NI == 0:
                                b = at.batch(0)[0]
                                pe.wait_ge(v_placed, SLACK + b + 1)
                                pe.wait_ge(o_copied, SLACK + b)
                            for v in range(NV):
                                gv = g * NV + v
                                for k in range(2):
                                    mm = pe.matmul(O[:, QO[t]:QO[t] + n], vz[p][k][0:QN[k], gv * 128:gv * 128 + 128],
                                                   probT[x % 2][k][0:QN[k], v, 0:n], start=(gv == 0 and k == 0),
                                                   stop=(gv == NH - 1 and k == 1))
                            mm.then_inc(valued, 1)

                    run(pe, step)

                @block.vector
                def _(dve):
                    def step(at):
                        if at.batch(4):
                            b, p = at.batch(4)
                            dve.wait_ge(qk_copied, b + 1)
                            for v in range(masked_here):
                                op = dve.tensor_scalar(qz[p][:, v, :], qs[p][:, :], mask[:, v:v + 1], None, ALU.mult)
                            op.then_inc(masked_dve, 1)
                        if at.item(2):
                            u, x = at.item(2)
                            n = place(x)[2]
                            dve.wait_ge(exped, SLACK + u + 1)
                            dve.reciprocal(inv[x % 2][0:n, :], total[x % 2][0:n, :]).then_inc(inverted, 1)
                            dve.wait_ge(inverted, u + 1)
                            dve.tensor_tensor(prob[x % 2][0:n, :, :], prob[x % 2][0:n, :, :],
                                              inv[x % 2][0:n, :].unsqueeze(2).to_broadcast([n, NV, TOK]),
                                              ALU.mult).then_inc(normalised, 1)
                        if not a["proj"] and at.batch(0, back=1):
                            b, p = at.batch(0, back=1)
                            cols = ds(b * TOK, TOK)
                            dve.wait_ge(valued, SLACK + NI * (b + 1))
                            dve.tensor_tensor(hidden[:, cols], O[:, 0:TOK], hidden[:, cols], ALU.add).then_inc(o_copied, 1)
                        if at.item(3):
                            u, x = at.item(3)
                            n = place(x)[2]
                            dve.wait_ge(scored, u + 1)
                            if pos:
                                before = 16 * (u // 2 + 1) if at.i is None else at.i * 16 * NI + 16 * ((at.s + 3) // 2 + 1)
                                dve.wait_ge(shifted_in[x % 2], before)
                                dve.tensor_tensor(score[x % 2][0:n, :, :].rearrange("p (a v) n -> p a (v n)", a=nb), s_view(x, n),
                                                  shifted[x % 2][0:n, :, :].rearrange("p (a v) n -> p a (v n)", a=nb),
                                                  ALU.add).then_inc(pos_added, 1)
                                dve.wait_ge(pos_added, SLACK + u + 1)
                                dve.tensor_reduce(top[x % 2][0:n, :], score[x % 2][0:n, :, :], AX.X, ALU.max,
                                                  negate=True).then_inc(maxed, 1)
                            else:
                                dve.tensor_reduce(top[x % 2][0:n, :].rearrange("p (a v) -> p a v", a=nb),
                                                  s_view(x, n).rearrange("p a (v n) -> p a v n", v=2), AX.X, ALU.max,
                                                  negate=True).then_inc(maxed, 1)
                        if at.item(1):
                            u, x = at.item(1)
                            n = place(x)[2]
                            dve.wait_ge(turned, SLACK + u + 1)
                            dve.wait_ge(valued, SLACK + u - 1)
                            dve.tensor_copy(probT[x % 2][1][0:QN[1], :, 0:n],
                                            T[0:QN[1], 1, 0:NV * 94].rearrange("p (v n) -> p v n", n=94)[:, :, 0:n]).then_inc(turned_v, 1)
                        if at.batch(V_AHEAD):
                            b, p = at.batch(V_AHEAD)
                            dve.wait_ge(v_ready, b + 1)
                            for t in range(2):
                                out = vz[p][t][0:QN[t], :].rearrange("p (v c) -> p v c", c=128 + dh)[:, :, 0:dh]
                                op = dve.tensor_tensor(out, V[0:QN[t], 128 * t:128 * t + 128].rearrange("p (v c) -> p v c", c=dh),
                                                       self.w(L + "bv")[0:QN[t], :].rearrange("p (v c) -> p v c", c=dh), ALU.add)
                            op.then_inc(v_placed, 1)
                        if a["proj"] and at.batch(2, back=2):
                            b, p = at.batch(2, back=2)
                            cols = ds(b * TOK, TOK)
                            dve.wait_ge(projected, b + 1)
                            dve.scalar_tensor_tensor(hidden[:, cols], M[:, 0:TOK], self.w(L + "bo"), hidden[:, cols],
                                                     ALU.add, ALU.add).then_inc(added_in, 1)

                    run(dve, step)

                @block.scalar
                def _(act):
                    def step(at):
                        if at.batch(4):
                            b, p = at.batch(4)
                            act.wait_ge(qk_ready, b + 1)
                            act.activation(qs[p][:, :], M[:, 0:TOK], ACT.Identity, bias=bias[:, 0:1])
                            act.activation(ks[p][:, :], M[:, TOK:2 * TOK], ACT.Identity,
                                           bias=self.w(L + "bk")).then_inc(qk_copied, 1)
                        if a["proj"] and at.batch(0, back=1):
                            b, p = at.batch(0, back=1)
                            act.wait_ge(valued, SLACK + NI * (b + 1))
                            act.activation(o_s[p][:, :], O[:, 0:TOK], ACT.Copy).then_inc(o_copied, 1)
                        if at.item(1):
                            u, x = at.item(1)
                            n = place(x)[2]
                            act.wait_ge(turned, SLACK + u + 1)
                            act.wait_ge(valued, SLACK + u - 1)
                            act.activation(probT[x % 2][0][0:QN[0], :, 0:n],
                                           T[0:QN[0], 0, 0:NV * 94].rearrange("p (v n) -> p v n", n=94)[:, :, 0:n],
                                           ACT.Copy).then_inc(turned_a, 1)
                        if at.item(3):
                            u, x = at.item(3)
                            n = place(x)[2]
                            act.wait_ge(maxed, u + 1)
                            act.wait_ge(turned, SLACK + u - 1)
                            for v in range(NV):
                                src = score[x % 2][0:n, v, :] if pos else S[x % 2][0:n, v // 2, (v % 2) * TOK:(v % 2) * TOK + TOK]
                                op = act.activation(prob[x % 2][0:n, v, :], src, ACT.Exp, bias=top[x % 2][0:n, v:v + 1],
                                                    accum_out=total[x % 2][0:n, v:v + 1])
                            op.then_inc(exped, 1)

                    run(act, step)

    def gate(self, L, xn, parts_T, weights_T):
        f = FFN[L]
        E = f["E"]
        nc = self.nc
        with ExitStack() as ctx:
            sem = self.sems(ctx, "gate")
            tag = f"g{L}"
            sb = lambda name, shape, dt=F32: ctx.enter_context(nc.sbuf_tensor(tag + name, shape, dt))
            LG = ctx.enter_context(nc.psum_tensor(tag + "LG", [128, 2 * PIECE], F32))
            TB = ctx.enter_context(nc.psum_tensor(tag + "TB", [96, 2, 2 * PIECE], BF16))
            TF = ctx.enter_context(nc.psum_tensor(tag + "TF", [32, 4, PIECE], F32))
            R = 2 * GTILES
            val, work, hot1, hot2, w = (sb(n, [GT, R, E]) for n in ("val", "work", "hot1", "hot2", "w"))
            m1, m2, r, ex, rd = (sb(n, [GT, R]) for n in ("m1", "m2", "r", "ex", "rd"))
            parts = sb("parts", [GT, GTILES, 3, 32], BF16)
            wpad = sb("wpad", [GT, GTILES, 32])
            identb = sb("identb", [128, 128], BF16)
            logits, step, exped, turned, copied, cleared = (sem(n) for n in ("logits", "step", "exped", "turned", "copied", "cleared"))
            wide = lambda t: t[:, :].unsqueeze(2).to_broadcast([GT, R, E])
            rank = self.w(f"rank{E}")[0:GT, :].unsqueeze(1).to_broadcast([GT, R, E])
            bias = self.w(L + "br")[0:GT, 0:E].unsqueeze(1).to_broadcast([GT, R, E])
            count = [0]
            fu = f["softmax_first"]

            with nc.Block() as block:
                self.phases.clear_before(block)

                @block.gpsimd
                def _(pool):
                    if E == 8:
                        pool.memset(parts[:, :, :, :], 0.0).then_inc(cleared, 1)
                        pool.memset(wpad[:, :, :], 0.0).then_inc(cleared, 1)
                    pool.tensor_copy(identb[:, :], self.w("ident")).then_inc(cleared, 1)

                @block.tensor
                def _(pe):
                    for t in range(GTILES):
                        mm = pe.matmul(LG[0:GT, 2 * E * t:2 * E * t + 2 * E], xn[:, GT * t:GT * t + GT], self.w(L + "wr"),
                                       start=True, stop=True)
                    mm.then_inc(logits, 1)
                    pe.wait_ge(copied, 1)
                    pe.wait_ge(cleared, 3 if E == 8 else 1)
                    for t in range(GTILES):
                        mm = pe.transpose(TB[0:96, t // 9, (t % 9) * GT:(t % 9) * GT + GT],
                                          parts[:, t, :, :].rearrange("p s r -> p (s r)"), identb[0:GT, 0:GT])
                    mm.then_inc(turned, 1)
                    for t in range(GTILES):
                        mm = pe.transpose(TF[0:32, t // 5, (t % 5) * GT:(t % 5) * GT + GT], wpad[:, t, :],
                                          self.w("ident")[0:GT, 0:GT])
                    mm.then_inc(turned, 1)

                @block.scalar
                def _(act):
                    act.wait_ge(exped, 1)
                    if fu:
                        act.activation(work[:, :, :], val[:, :, :], ACT.Exp).then_inc(exped, 1)
                    else:
                        act.activation(ex[:, :], ex[:, :], ACT.Exp).then_inc(exped, 1)
                    act.wait_ge(turned, 2)
                    for k in range(4):
                        n = min(5, GTILES - 5 * k) * GT
                        act.activation(weights_T[:, 5 * GT * k:5 * GT * k + n], TF[0:32, k, 0:n], ACT.Copy).then_inc(copied, 1)

                @block.vector
                def _(dve):
                    def done(ins):
                        count[0] += 1
                        ins.then_inc(step, 1)
                        dve.wait_ge(step, count[0])

                    dve.wait_ge(logits, 1)
                    done(dve.tensor_tensor(val[:, :, :], LG[0:GT, 0:R * E].rearrange("p (r e) -> p r e", e=E), bias, ALU.add))
                    if L == "L1":
                        done(dve.tensor_tensor(val[:, :, :], val[:, :, :],
                                               self.w(L + "br")[0:GT, E:2 * E].unsqueeze(1).to_broadcast([GT, R, E]), ALU.add))
                    if fu:
                        done(dve.tensor_reduce(m1[:, :], val[:, :, :], AX.X, ALU.max))
                        dve.tensor_tensor(val[:, :, :], val[:, :, :], wide(m1), ALU.subtract).then_inc(exped, 1)
                        dve.wait_ge(exped, 2)
                        done(dve.tensor_reduce(r[:, :], work[:, :, :], AX.X, ALU.add))
                        done(dve.reciprocal(rd[:, :], r[:, :]))
                        done(dve.tensor_tensor(val[:, :, :], work[:, :, :], wide(rd), ALU.mult))

                    def choose(top, hot):
                        done(dve.tensor_reduce(top[:, :], val[:, :, :], AX.X, ALU.max))
                        done(dve.tensor_tensor(work[:, :, :], val[:, :, :], wide(top), ALU.is_equal))
                        done(dve.tensor_tensor(work[:, :, :], work[:, :, :], rank, ALU.mult))
                        done(dve.tensor_reduce(r[:, :], work[:, :, :], AX.X, ALU.max))
                        done(dve.tensor_tensor(hot[:, :, :], work[:, :, :], wide(r), ALU.is_equal))

                    choose(m1, hot1)
                    done(dve.scalar_tensor_tensor(val[:, :, :], hot1[:, :, :], -1e30, val[:, :, :], ALU.mult, ALU.add))
                    choose(m2, hot2)
                    if fu:
                        done(dve.tensor_tensor(ex[:, :], m1[:, :], m2[:, :], ALU.add))
                        done(dve.reciprocal(rd[:, :], ex[:, :]))
                        done(dve.tensor_tensor(m1[:, :], m1[:, :], rd[:, :], ALU.mult))
                        done(dve.tensor_tensor(m2[:, :], m2[:, :], rd[:, :], ALU.mult))
                    else:
                        dve.tensor_tensor(ex[:, :], m2[:, :], m1[:, :], ALU.subtract).then_inc(exped, 1)
                        dve.wait_ge(exped, 2)
                        done(dve.tensor_scalar(r[:, :], ex[:, :], 1.0, None, ALU.add))
                        done(dve.reciprocal(m1[:, :], r[:, :]))
                        done(dve.tensor_tensor(m2[:, :], ex[:, :], m1[:, :], ALU.mult))
                    done(dve.tensor_tensor(hot1[:, :, :], hot1[:, :, :], wide(m1), ALU.mult))
                    done(dve.tensor_tensor(hot2[:, :, :], hot2[:, :, :], wide(m2), ALU.mult))
                    done(dve.tensor_tensor(w[:, :, :], hot1[:, :, :], hot2[:, :, :], ALU.add))
                    dve.wait_ge(cleared, 3 if E == 8 else 1)
                    flat = w[:, :, :].rearrange("p (t h) e -> p t (h e)", h=2)
                    rest = hot1[:, :, :].rearrange("p (t h) e -> p t (h e)", h=2)
                    part = lambda s: parts[:, :, s, 0:2 * E]
                    done(dve.tensor_copy(part(0), flat))
                    done(dve.tensor_tensor(rest, flat, part(0), ALU.subtract))
                    done(dve.tensor_copy(part(1), rest))
                    done(dve.tensor_tensor(part(2), rest, part(1), ALU.subtract))
                    dve.tensor_copy(wpad[:, :, 0:2 * E], flat).then_inc(copied, 1)
                    dve.wait_ge(turned, 1)
                    for k in range(2):
                        n = (9, GTILES - 9)[k] * GT
                        dve.tensor_copy(parts_T[:, 9 * GT * k:9 * GT * k + n], TB[0:96, k, 0:n]).then_inc(copied, 1)

    def experts(self, L, xn, parts_T, weights_T, dst, base):
        f = FFN[L]
        E = f["E"]
        blocks = [(e, k) for e in range(E) for k in range(f["blocks"])] + [(None, k) for k in range(f["shared"])]
        nblk = len(blocks)
        units = [(h, n) for n in range(nblk) for h in range(2)]
        NU = len(units)
        nc = self.nc
        func = function(f["act"])
        with ExitStack() as ctx:
            sem = self.sems(ctx, "moe")
            tag = f"m{L}"
            Hp = [ctx.enter_context(nc.psum_tensor(tag + f"H{k}", [128, PIECE], F32)) for k in range(2)]
            Bp = [ctx.enter_context(nc.psum_tensor(tag + f"B{k}", [128, PIECE], F32)) for k in range(2)]
            Y = ctx.enter_context(nc.psum_tensor(tag + "Y", [128, PIECE], F32))
            g = [ctx.enter_context(nc.sbuf_tensor(tag + f"g{k}", [128, CHUNK], F32)) for k in range(2)]
            gw = [ctx.enter_context(nc.sbuf_tensor(tag + f"gw{k}", [128, CHUNK], F32)) for k in range(2)]
            h_r, b_r, g_r, gw_r, y_r, used, y_done = (sem(n) for n in ("h", "b", "g", "gw", "y", "used", "ydone"))
            w1 = lambda h, n: self.w(L + "w1", (h * nblk + n) * 128, 128)
            w2 = lambda h, n: self.w(L + "w2", n * 192 + (64 if h == 0 else 0), 128)

            with nc.Block() as block:
                self.phases.clear_before(block)

                @block.tensor
                def _(pe):
                    pe.sem_inc(y_done, SLACK)

                    def up(c, u):
                        h, n = units[u]
                        pe.wait_ge(g_r, SLACK + c * NU + u - 1)
                        pe.matmul(Hp[u % 2][:, 0:CHUNK], w1(h, n), xn[:, ds(c * CHUNK, CHUNK)], start=True, stop=True).then_inc(h_r, 1)
                        pe.wait_ge(gw_r, SLACK + c * NU + u - 1)
                        e = blocks[n][0]
                        r = (h * E + e) if e is not None else 0
                        pe.matmul(Bp[u % 2][:, 0:CHUNK], self.sel[:, 128 * r:128 * r + 128], parts_T[:, ds(c * CHUNK, CHUNK)],
                                  start=True, stop=True).then_inc(b_r, 1)

                    def down(c, u):
                        h, n = units[u]
                        pe.wait_ge(gw_r, SLACK + c * NU + u + 1)
                        pe.matmul(Y[:, 0:CHUNK], w2(h, n), gw[u % 2][:, :], start=False, stop=(u == NU - 1)).then_inc(used, 1)

                    with pe.Fori(0, CHUNKS) as c:
                        up(c, 0)
                        pe.wait_ge(y_done, SLACK + c)
                        up(c, 1)
                        pe.matmul(Y[:, 0:CHUNK], self.w(L + "b2")[0:32, :], weights_T[:, ds(c * CHUNK, CHUNK)],
                                  start=True, stop=False)
                        for u in range(NU):
                            if u + 2 < NU:
                                down(c, u)
                                up(c, u + 2)
                            else:
                                down(c, u)

                @block.scalar
                def _(act):
                    act.sem_inc(g_r, SLACK)
                    with act.Fori(0, CHUNKS) as c:
                        for u in range(NU):
                            n = units[u][1]
                            act.wait_ge(h_r, c * NU + u + 1)
                            act.wait_ge(gw_r, SLACK + c * NU + u - 1)
                            act.activation(g[u % 2][:, :], Hp[u % 2][:, 0:CHUNK], func, bias=self.w(L + "b1", n, 1)).then_inc(g_r, 1)

                @block.vector
                def _(dve):
                    dve.sem_inc(gw_r, SLACK)
                    with dve.Fori(0, CHUNKS) as c:
                        for u in range(NU):
                            n = units[u][1]
                            dve.wait_ge(g_r, SLACK + c * NU + u + 1)
                            dve.wait_ge(b_r, c * NU + u + 1)
                            dve.wait_ge(used, SLACK + c * NU + u - 1)
                            if blocks[n][0] is None:
                                dve.tensor_copy(gw[u % 2][:, :], g[u % 2][:, :]).then_inc(gw_r, 1)
                            else:
                                dve.tensor_tensor(gw[u % 2][:, :], g[u % 2][:, :], Bp[u % 2][:, 0:CHUNK], ALU.mult).then_inc(gw_r, 1)
                        dve.wait_ge(used, SLACK + (c + 1) * NU)
                        cols = ds(c * CHUNK, CHUNK)
                        if f["shared"]:
                            dve.scalar_tensor_tensor(dst[:, cols], Y[:, 0:CHUNK], self.w("L2b2s"), base[:, cols],
                                                     ALU.add, ALU.add).then_inc(y_done, 1)
                        else:
                            dve.tensor_tensor(dst[:, cols], Y[:, 0:CHUNK], base[:, cols], ALU.add).then_inc(y_done, 1)

                @block.gpsimd
                def _(pool):
                    pool.sem_inc(used, SLACK)

    def add(self, dst, a, b):
        with ExitStack() as ctx, self.nc.Block() as block:
            sem = self.sems(ctx, "add")
            s = sem("s")
            self.phases.clear_before(block)

            @block.vector
            def _(dve):
                dve.tensor_tensor(dst[:, :], a[:, :], b[:, :], ALU.add).then_inc(s, 1)


def function(name):
    return {"Gelu": ACT.Gelu, "Relu": ACT.Relu}[name]


def post(nc, phases, hidden, weights_in):
    with ExitStack() as ctx:
        sb = lambda name, shape, dt=F32: ctx.enter_context(nc.sbuf_tensor(name, shape, dt))
        W = sb("post_weights", [128, PC.n])
        sel = sb("expert_sel", [96, 32 * 128], BF16)
        xn, x2 = sb("xn", [128, COLS]), sb("x2", [128, COLS])
        parts_T = sb("parts_T", [96, COLS], BF16)
        weights_T = sb("weights_T", [32, COLS])
        loaded = ctx.enter_context(nc.semaphore("post_loaded"))
        selected = ctx.enter_context(nc.semaphore("post_selected"))
        with nc.Block() as block:
            @block.gpsimd
            def _(pool):
                selector_of(pool, sel, 128, selected)

            @block.sync
            def _(sp):
                sp.dma_start(W[:, :], weights_in).then_inc(loaded, 16)
                sp.wait_ge(loaded, 16)
        P = Post(nc, phases, W, sel, hidden, (loaded, 16))
        for L in ("L0", "L1", "L2", "L3"):
            P.norm(hidden, xn)
            if L == "L2":
                P.norm(xn, xn, ("a2_gamma", "a2_beta"))
            P.attention(L, xn)
            P.norm(hidden, xn)
            if L == "L0":
                P.norm(xn, xn, ("f0_gamma", "f0_beta"))
            P.gate(L, xn, parts_T, weights_T)
            if L == "L3":
                P.experts(L, xn, parts_T, weights_T, x2, xn)
                P.norm(x2, x2, ("f3_gamma", "f3_beta"))
                P.add(hidden, hidden, x2)
            else:
                P.experts(L, xn, parts_T, weights_T, hidden, hidden)


def build(nc, x_in, ssm_w, post_w, out):
    phases = Phases(nc)
    with ExitStack() as ctx:
        sb = lambda name, shape, dt: ctx.enter_context(nc.sbuf_tensor(name, shape, dt))
        hidden = sb("hidden", [128, COLS], F32)
        inputs_loaded = ctx.enter_context(nc.semaphore("inputs_loaded"))
        with ExitStack() as ssm:
            ssb = lambda name, shape, dt: ssm.enter_context(nc.sbuf_tensor(name, shape, dt))
            weights = ssb("ssm_weights", [128, SSM_W], F32)
            selector = ssb("selector", [96, 16 * 128], BF16)
            a_neg = ssb("a_neg", [128, SSM_LAYERS * PAIRS], F32)
            xa = ssb("xa", [128, HALF * SEQ], F32)
            xb = ssb("xb", [128, HALF * LENS[1]], F32)
            a_done = ctx.enter_context(nc.semaphore("a_done"))
            selected = ctx.enter_context(nc.semaphore("selected"))
            with nc.Block() as block:

                @block.sync
                def _(sp):
                    sp.dma_start(weights[:, :], ssm_w).then_inc(inputs_loaded, 16)
                    sp.dma_start(xa[:, :], x_in).then_inc(inputs_loaded, 16)
                    sp.wait_ge(inputs_loaded, INPUT_DMAS)

                @block.gpsimd
                def _(pool):
                    selector_of(pool, selector, 64, selected)

                @block.scalar
                def _(act):
                    act.wait_ge(inputs_loaded, INPUT_DMAS)
                    for i in range(SSM_LAYERS):
                        act.activation(a_neg[:, PAIRS * i:PAIRS * (i + 1)],
                                       weights[:, i * SSM_COLS + SSM_A:i * SSM_COLS + SSM_A + PAIRS], ACT.Exp).then_inc(a_done, 1)

                @block.vector
                def _(dve):
                    dve.wait_ge(a_done, SSM_LAYERS)
                    dve.tensor_scalar(a_neg[:, :], a_neg[:, :], -1.0, None, ALU.mult).then_inc(a_done, 1)

            x = [xa, xb, xa]
            nxt = [xb, xa, hidden]
            for layer in range(SSM_LAYERS):
                L = LENS[layer]
                seqs = max(1, SEQ // L)
                width, turns = seqs * L, 2 * HALF // seqs
                split_dram = nc.dram_tensor(f"split{layer}", (turns, 2, 96, 2, width), BF16, kind="Internal").ap()
                y_dram = nc.dram_tensor(f"y{layer}", (turns, 64, width), F32, kind="Internal").ap()
                with (nc.sbuf_tensor(f"b_rep{layer}", [128, 2 * HALF * L], F32) as b_rep,
                      nc.sbuf_tensor(f"c_rep{layer}", [128, 2 * HALF * L], F32) as c_rep):
                    ssm_prep(nc, phases, inputs_loaded, layer, L, x[layer], weights, b_rep, c_rep, split_dram)
                    ssm_scan(nc, phases, inputs_loaded, layer, L, weights, selector, a_neg, b_rep, c_rep, split_dram, y_dram)
                ssm_finish(nc, phases, layer, L, x[layer], nxt[layer], weights, y_dram)
        post(nc, phases, hidden, post_w)
        with ExitStack() as c2, nc.Block() as block:
            done = c2.enter_context(nc.semaphore("out_done"))

            @block.sync
            def _(sp):
                sp.dma_start(out, hidden[:, :]).then_inc(done, 16)
                sp.wait_ge(done, 16)


def ssm_layout(inp):
    import numpy as np
    f = np.float32
    x = np.asarray(inp["x"]).reshape(2, HALF, SEQ, D).transpose(0, 3, 1, 2).reshape(128, HALF * SEQ)
    w = np.zeros((128, SSM_W), f)
    A_log, Dp, Wdbc, Wdt, bdt = (np.asarray(inp["L0_tok_" + n]) for n in ("A_log", "D", "W_dbc", "W_dt", "b_dt"))
    for i in range(SSM_LAYERS):
        o = i * SSM_COLS
        for h in range(2):
            r = slice(64 * h, 64 * h + 64)
            w[r, o + 64 * h:o + 64 * h + 64] = Wdbc[i, 0][:, None]
            for c in range(2):
                w[r, o + SSM_WB + 128 * h + 64 * c:o + SSM_WB + 128 * h + 64 * c + 64] = Wdbc[i, 1:65].T
                w[r, o + SSM_WC + 128 * h + 64 * c:o + SSM_WC + 128 * h + 64 * c + 64] = Wdbc[i, 65:129].T
            w[r, o + SSM_VEC] = Wdt[i, :, 0]
            w[r, o + SSM_VEC + 1] = bdt[i]
            w[r, o + SSM_VEC + 2] = Dp[i]
            w[r, o + SSM_A:o + SSM_A + PAIRS] = A_log[i, h::2, :].T
        w[0:64, YSEL + 62] = 1
        w[64:128, YSEL + 63] = 1
    return {"x_in": np.ascontiguousarray(x), "ssm_w": w}


def post_layout(inp):
    import numpy as np
    f = np.float32
    W = np.zeros((128, PC.n), f)
    g = {k: np.asarray(v) for k, v in inp.items()}

    def at(name):
        o, n = PC.at[name]
        return W[:, o:o + n]

    def diag(name, m):
        at(name)[0:64, 0:64] = m
        at(name)[64:128, 64:128] = m

    def col(name, v):
        at(name)[0:64, 0] = v
        at(name)[64:128, 0] = v

    diag("mean", np.full((64, 64), 1 / 64, f))
    at("ident")[:] = np.eye(128, dtype=f)
    for e in (8, 16):
        at(f"rank{e}")[:] = e - np.arange(e, dtype=f)
    col("f0_gamma", g["L0_ffn_gamma"]); col("f0_beta", g["L0_ffn_beta"])
    col("a2_gamma", g["L2_attn_ln_gamma"]); col("a2_beta", g["L2_attn_ln_beta"])
    col("f3_gamma", g["L3_ffn_gamma"]); col("f3_beta", g["L3_ffn_beta"])
    wqkv, bqkv = g["L0_attn_W_qkv"], g["L0_attn_b_qkv"]
    att = {"L0": [wqkv[0:64].T, wqkv[64:128].T, wqkv[128:192].T, bqkv[0:64], bqkv[64:128], bqkv[128:192]],
           "L1": [g["L1_attn_Wq"].T, g["L1_attn_Wk"].T, g["L1_attn_Wv"].T, g["L1_attn_bq"], g["L1_attn_bk"], g["L1_attn_bv"]],
           "L2": [g["L2_attn_Wq"], g["L2_attn_Wk"], g["L2_attn_Wv"], g["L2_attn_bq"], g["L2_attn_bk"], g["L2_attn_bv"]],
           "L3": [g["L3_attn_Wq"].T, g["L3_attn_Wk"].T, g["L3_attn_Wv"].T, None, None, None]}
    scale = {"L0": 0.25, "L1": 1.0, "L2": 0.125, "L3": 0.125}
    for L, (wq, wk, wv, bq, bk, bv) in att.items():
        diag(L + "wq", wq); diag(L + "wk", wk); diag(L + "wv", wv)
        if bq is not None:
            col(L + "bq", bq); col(L + "bk", bk)
            at(L + "bv")[:, 0:64] = bv; at(L + "bv")[:, 64:128] = bv
        H = ATTN[L]["heads"]
        for v in range(2 * H):
            dh = 64 // H
            at(L + "mask")[v * dh:(v + 1) * dh, v] = scale[L]
    diag("L0wo", g["L0_attn_W_proj"].T); col("L0bo", g["L0_attn_b_proj"])
    diag("L2wo", g["L2_attn_Wout"]); col("L2bo", g["L2_attn_bout"])
    diag("L2wpos", g["L2_attn_Wpos"])
    pos = np.arange(TOK, dtype=f)[:, None]
    div = np.exp(np.arange(0, D, 2, dtype=f) * f(-np.log(10000.0) / D)).astype(f)
    pe = np.zeros((TOK, D), f)
    pe[:, 0::2] = np.sin(pos * div)
    pe[:, 1::2] = np.cos(pos * div)
    at("L2pe")[0:64] = pe.T; at("L2pe")[64:128] = pe.T
    col("L2u", g["L2_attn_u_bias"].reshape(64)); col("L2v", g["L2_attn_v_bias"].reshape(64))
    at("L1scale")[:, 0] = g["L1_attn_scale"][0]
    col("L2b2s", g["L2_ffn_b2s"])
    ffn = {"L0": ("L0_ffn_W1", "L0_ffn_b1", "L0_ffn_W2", "L0_ffn_b2", "L0_ffn_Wr"),
           "L1": ("L1_ffn_W1", "L1_ffn_b1", "L1_ffn_W2", "L1_ffn_b2", "L1_ffn_Wg"),
           "L2": ("L2_ffn_W1p", "L2_ffn_b1p", "L2_ffn_W2p", "L2_ffn_b2p", "L2_ffn_Wr"),
           "L3": ("L3_ffn_w1", "L3_ffn_b1", "L3_ffn_w2", "L3_ffn_b2", "L3_ffn_gate_w")}
    for L, names in ffn.items():
        W1, b1, W2, b2, wr = (g[n] for n in names)
        E, nbk = FFN[L]["E"], FFN[L]["blocks"]
        nblk = E * nbk + FFN[L]["shared"]
        w1 = at(L + "w1").reshape(128, 2, nblk, 128)
        w2 = at(L + "w2").reshape(128, nblk, 192)
        o1, o2 = PC.at[L + "w1"][0], PC.at[L + "w2"][0]
        srcs = [(W1[e][:, k * 128:(k + 1) * 128], b1[e][k * 128:(k + 1) * 128], W2[e][k * 128:(k + 1) * 128]) for e in range(E) for k in range(nbk)]
        if L == "L2":
            srcs += [(g["L2_ffn_W1s"][:, k * 128:(k + 1) * 128], g["L2_ffn_b1s"][k * 128:(k + 1) * 128], g["L2_ffn_W2s"][k * 128:(k + 1) * 128]) for k in range(2)]
        for n, (a, b, c) in enumerate(srcs):
            W[0:64, o1 + n * 128:o1 + n * 128 + 128] = a
            W[64:128, o1 + (nblk + n) * 128:o1 + (nblk + n) * 128 + 128] = a
            at(L + "b1")[:, n] = b
            W[:, o2 + n * 192 + 64:o2 + n * 192 + 128] = c
        at(L + "b2")[0:E, 0:64] = b2
        at(L + "b2")[E:2 * E, 64:128] = b2
        at(L + "wr")[0:64, 0:E] = wr
        at(L + "wr")[64:128, E:2 * E] = wr
    at("L0br")[:, 0:8] = g["L0_ffn_br"]; at("L0br")[:, 8:16] = g["L0_ffn_br"]
    at("L1br")[:, 0:8] = g["L1_ffn_bg"]; at("L1br")[:, 8:16] = g["L1_ffn_bias"]
    at("L3br")[:, 0:16] = g["L3_ffn_gate_b"]
    return {"post_w": W}


def kernel(**inputs):
    import numpy as np
    import concourse.bacc as bacc
    from concourse.bass_utils import run_bass_kernel_spmd
    nc = bacc.Bacc("TRN2", target_bir_lowering=False, num_devices=1)
    arrays = {**ssm_layout(inputs), **post_layout(inputs)}
    aps = {n: nc.dram_tensor(n, a.shape, mybir.dt.from_np(a.dtype), kind="ExternalInput").ap() for n, a in arrays.items()}
    out = nc.dram_tensor("out", (128, COLS), F32, kind="ExternalOutput").ap()
    build(nc, aps["x_in"], aps["ssm_w"], aps["post_w"], out)
    r = run_bass_kernel_spmd(nc, [arrays], core_ids=[0])
    y = r.results[0]["out"]
    return np.ascontiguousarray(y.reshape(2, D, HALF, TOK).transpose(0, 2, 3, 1)).reshape(BATCH, TOK, D)
```

```python
from contextlib import ExitStack

import concourse.bass as bass
from concourse import mybir

F32 = mybir.dt.float32
BF16 = mybir.dt.bfloat16
ACT = mybir.ActivationFunctionType
ALU = mybir.AluOpType
AX = mybir.AxisListType
ds = bass.ds

BATCH, SEQ, D, NSTATE, SSM_LAYERS = 16, 750, 64, 64, 3
HALF = BATCH // 2
LENS = [SEQ, SEQ // 2, SEQ // 4]
TOK = LENS[-1]
COLS = HALF * TOK
SLACK = 8
LOG_AND_EXP = "natural_log_exp_and_others"
PIECE = 512

SSM_WD, SSM_WB, SSM_WC = 0, 128, 384
SSM_VEC, SSM_A = 640, 643
SSM_COLS = 675
PAIRS = D // 2
YSEL = SSM_LAYERS * SSM_COLS
SSM_W = YSEL + 128


def pieces(width):
    return [(a, min(a + PIECE, width)) for a in range(0, width, PIECE)]


INPUT_DMAS = 32
FIRST_COLS = 2 * SEQ


def selector_of(pool, out, width, selected):
    pool.memset(out[:, :], 0.0).then_inc(selected, 1)
    pool.wait_ge(selected, 1)
    for s in range(3):
        view = out[32 * s:32 * s + 32, :].rearrange("p (c n) -> p c n", n=width)
        pool.affine_select(out=view, in_=view, compare_op=ALU.not_equal, fill=1.0, base=0,
                           pattern=[[-1, 32], [0, width]], channel_multiplier=1).then_inc(selected, 1)


def expert_selector(pool, out, E, selected, done):
    if done:
        pool.wait_ge(selected, done)
    pool.memset(out[:, :], 0.0).then_inc(selected, 1)
    pool.wait_ge(selected, done + 1)
    for s in range(3):
        for h in range(2):
            view = out[32 * s:32 * s + 32, :].rearrange("p (e c) -> p e c", c=128)[:, :, 64 * h:64 * h + 64]
            pool.affine_select(out=view, in_=view, compare_op=ALU.not_equal, fill=1.0, base=-E * h,
                               pattern=[[-1, E], [0, 64]], channel_multiplier=1).then_inc(selected, 1)


def settle(eng, value):
    return value if isinstance(value, int) else eng.snap(eng.to_reg(value))


class Phases:

    def __init__(self, nc):
        self.nc, self.held, self.before, self.now = nc, [], [], []

    def open(self, phase):
        if len(self.held) == 2:
            self.held.pop(0).close()
        self.held.append(ExitStack())
        self.before, self.now, self.phase = self.now, [], phase
        return self

    def __call__(self, name):
        s = self.held[-1].enter_context(self.nc.semaphore(f"{self.phase}_{name}"))
        self.now.append(s)
        return s

    def clear_before(self, block):
        before = self.before

        @block.sync
        def _(sp):
            for s in before:
                sp.sem_clear(s)


def ssm_prep(nc, phases, inputs_loaded, rest_loaded, layer, L, x, weights, b_rep, c_rep, split_dram):
    seqs = max(1, SEQ // L)
    width = seqs * L
    groups = HALF // seqs
    base = layer * SSM_COLS
    w = lambda a, n: weights[:, base + a:base + a + n]
    with ExitStack() as ctx:
        sb = lambda name, shape, dt: ctx.enter_context(nc.sbuf_tensor(f"prep{layer}_{name}", shape, dt))
        sem = phases.open(f"prep{layer}")
        raw = [ctx.enter_context(nc.psum_tensor(f"raw{layer}_{p}", [128, 1024], F32)) for p in range(2)]
        bc = [ctx.enter_context(nc.psum_tensor(f"bc{layer}_{p}", [128, 1024], F32)) for p in range(2)]
        z = [sb(f"z{p}", [128, width], F32) for p in range(2)]
        soft = [sb(f"soft{p}", [128, width], F32) for p in range(2)]
        val = [[sb(f"val{t}{p}", [128, width], F32) for p in range(2)] for t in range(2)]
        rest = [[sb(f"rest{t}{p}", [128, width], F32) for p in range(2)] for t in range(2)]
        part = [sb(f"part{p}", [128, 3, 2, width], BF16) for p in range(2)]
        raw_ready, z_ready, soft_ready, soft_step = sem("raw_ready"), sem("z_ready"), sem("soft_ready"), sem("soft_step")
        bc_ready, bc_even, bc_odd = sem("bc_ready"), sem("bc_even"), sem("bc_odd")
        val_ready, first_cut, rest_ready, second_cut, third_cut = (
            sem(n) for n in ("val_ready", "first_cut", "rest_ready", "second_cut", "third_cut"))
        stored = [sem(f"stored{p}") for p in range(2)]

        def run(eng, step):
            step(0, 0)
            step(1, 1)
            if groups > 2:
                with eng.Fori(0, groups // 2 - 1) as i:
                    step(2 * i + 2, 2)
                    step(2 * i + 3, 3)
            step(groups, groups)
            step(groups + 1, groups + 1)

        def has(s, back):
            return 0 <= s - back < groups

        with nc.Block() as block:
            phases.clear_before(block)

            @block.tensor
            def _(pe):
                def step(g, s):
                    if not has(s, 0):
                        return
                    p = s % 2
                    if layer == 0 and s >= 2:
                        pe.wait_ge(rest_loaded, 16)
                    pe.wait_ge(z_ready, SLACK + g - 1)
                    for a, b in pieces(width):
                        mm = pe.matmul(raw[p][:, a:b], w(SSM_WD, 128), x[:, ds(g * width + a, b - a)],
                                       start=True, stop=True)
                    mm.then_inc(raw_ready, 1)
                    for q in range(4):
                        pe.wait_ge(bc_even if q % 2 == 0 else bc_odd, SLACK + 2 * g + q // 2)
                        for a, b in pieces(width):
                            mm = pe.matmul(bc[q % 2][:, a:b], w(SSM_WB + 128 * q, 128),
                                           x[:, ds(g * width + a, b - a)], start=True, stop=True)
                        mm.then_inc(bc_ready, 1)

                run(pe, step)

            def target(q):
                return (b_rep, c_rep)[q // 2], (q % 2) * HALF * L

            @block.vector
            def _(dve):
                def copy_projection(g, q):
                    dst, off = target(q)
                    dve.wait_ge(bc_ready, 4 * g + q + 1)
                    dve.tensor_copy(dst[:, ds(off + g * width, width)], bc[1][:, 0:width]).then_inc(bc_odd, 1)

                def step(g, s):
                    p = s % 2
                    if has(s, 0):
                        dve.wait_ge(raw_ready, g + 1)
                        dve.wait_ge(val_ready, SLACK + 2 * g)
                        dve.tensor_scalar(z[p][:, :], raw[p][:, 0:width], w(SSM_VEC, 1), w(SSM_VEC + 1, 1),
                                          ALU.mult, ALU.add).then_inc(z_ready, 1)
                    if has(s, 2):
                        for t in range(2):
                            dve.wait_ge(second_cut, SLACK + 2 * (g - 2) + t + 1)
                            dve.tensor_tensor(part[p][:, 2, t, :], rest[t][p][:, :], part[p][:, 1, t, :],
                                              ALU.subtract).then_inc(third_cut, 1)
                    if has(s, 0):
                        copy_projection(g, 1)
                        dve.wait_ge(soft_ready, g + 1)
                        dve.wait_ge(first_cut, SLACK + 2 * (g - 1))
                        dve.wait_ge(rest_ready, SLACK + 2 * (g - 1))
                        dve.scalar_tensor_tensor(val[0][p][:, :], z[p][:, :], 0.0, soft[p][:, :],
                                                 ALU.max, ALU.add).then_inc(val_ready, 1)
                        dve.wait_ge(val_ready, SLACK + 2 * g + 1)
                        dve.tensor_tensor(val[1][p][:, :], val[0][p][:, :], x[:, ds(g * width, width)],
                                          ALU.mult).then_inc(val_ready, 1)
                        copy_projection(g, 3)

                run(dve, step)

            @block.scalar
            def _(act):
                def step(g, s):
                    if has(s, 1):
                        p = (s - 1) % 2
                        turn = (s - 1) // 2 if isinstance(g, int) else (g - s) // 2 + (s - 1) // 2
                        act.wait_ge(stored[p], SLACK + 64 * turn)
                        for t in range(2):
                            act.wait_ge(val_ready, SLACK + 2 * (g - 1) + t + 1)
                            act.activation(part[p][:, 0, t, :], val[t][p][:, :], ACT.Copy).then_inc(first_cut, 1)
                    if has(s, 0):
                        p = s % 2
                        act.wait_ge(z_ready, SLACK + g + 1)
                        act.activation(soft[p][:, :], z[p][:, :], ACT.Abs).then_inc(soft_step, 1)
                        act.wait_ge(soft_step, 2 * g + 1)
                        act.activation(soft[p][:, :], soft[p][:, :], ACT.Exp, scale=-1.0).then_inc(soft_step, 1)
                        act.wait_ge(soft_step, 2 * g + 2)
                        act.activation(soft[p][:, :], soft[p][:, :], ACT.Ln, bias=1.0).then_inc(soft_ready, 1)
                        for q in (0, 2):
                            dst, off = target(q)
                            projected = settle(act, 4 * g + q + 1)
                            act.wait_ge(inputs_loaded, INPUT_DMAS)
                            act.wait_ge(bc_ready, projected)
                            act.activation(dst[:, ds(off + g * width, width)], bc[0][:, 0:width],
                                           ACT.Copy).then_inc(bc_even, 1)
                    if has(s, 1):
                        p = (s - 1) % 2
                        for t in range(2):
                            act.wait_ge(rest_ready, SLACK + 2 * (g - 1) + t + 1)
                            act.activation(part[p][:, 1, t, :], rest[t][p][:, :], ACT.Copy).then_inc(second_cut, 1)

                act.preload_act_table_set(LOG_AND_EXP)
                run(act, step)

            @block.gpsimd
            def _(pool):
                def step(g, s):
                    if not has(s, 1):
                        return
                    p = (s - 1) % 2
                    for t in range(2):
                        pool.wait_ge(first_cut, SLACK + 2 * (g - 1) + t + 1)
                        pool.tensor_tensor(rest[t][p][:, :], val[t][p][:, :], part[p][:, 0, t, :],
                                           ALU.subtract).then_inc(rest_ready, 1)

                for free in (z_ready, bc_even, bc_odd, val_ready, first_cut, rest_ready, second_cut, third_cut,
                             stored[0], stored[1]):
                    pool.sem_inc(free, SLACK)
                run(pool, step)

            @block.sync
            def _(sp):
                def step(g, s):
                    if not has(s, 2):
                        return
                    p = s % 2
                    sp.wait_ge(third_cut, SLACK + 2 * (g - 2) + 2)
                    for h in range(2):
                        for e in range(2):
                            dst = split_dram[ds(g - 2, 1), e, :, h].rearrange("a (s r) t w -> (a r) s (t w)", s=3)
                            src = part[p][64 * h + 32 * e:64 * h + 32 * e + 32, :, :, :]
                            sp.dma_start(dst, src.rearrange("r s t w -> r s (t w)")).then_inc(stored[p], 16)

                run(sp, step)
                for p in range(2):
                    sp.wait_ge(stored[p], SLACK + 64 * (groups // 2))


def ssm_scan(nc, phases, inputs_loaded, layer, L, x, out, weights, selector, a_neg, b_rep, c_rep, split_dram):
    seqs = max(1, SEQ // L)
    width = seqs * L
    half = width // 2
    groups = HALF // seqs
    segment, carried = (half, True) if L > half else (L, False)
    UNITS = 2 * PAIRS
    vec = SSM_COLS * layer + SSM_VEC + 2
    LAG = 3
    with ExitStack() as ctx:
        sb = lambda name, shape, dt: ctx.enter_context(nc.sbuf_tensor(f"scan{layer}_{name}", shape, dt))
        ps = lambda name: ctx.enter_context(nc.psum_tensor(f"{name}{layer}", [128, 2, PIECE], F32))
        sem = phases.open(f"scan{layer}")
        decay = [ps(f"decay{p}_") for p in range(2)]
        spread, y_sum = ps("spread"), ps("ysum")
        stack = [sb(f"stack{e}", [96, 4, width], BF16) for e in range(2)]
        dbx = [sb(f"dbx{p}", [128, 2, half], F32) for p in range(4)]
        state = [sb(f"state{p}", [128, 2, half], F32) for p in range(4)]
        weighed = [sb(f"weighed{p}", [128, 2, half], F32) for p in range(4)]
        loaded = [sem(f"loaded{e}") for e in range(2)]
        delta_ready, spread_ready, decay_ready = sem("delta_ready"), sem("spread_ready"), sem("decay_ready")
        dbx_ready, scanned, weighed_ready = sem("dbx_ready"), sem("scanned"), sem("weighed_ready")
        y_added, y_taken = sem("y_added"), sem("y_taken")

        def repeated(tensor, g, c):
            return tensor[:, :].rearrange("p (h n) -> p h n", h=2)[:, :, ds(g * width + c * half, half)]

        with nc.Block() as block:
            phases.clear_before(block)

            @block.sync
            def _(sp):
                def load(g, first):
                    for e in range(2):
                        if not first:
                            sp.wait_ge(delta_ready, UNITS * (g - 1) + PAIRS * (e + 1))
                            sp.wait_ge(spread_ready, UNITS * (g - 1) + PAIRS * (e + 1))
                        sp.dma_start(stack[e][:, :, :],
                                     split_dram[ds(g, 1), e].rearrange("a q h t w -> (a q) (h t) w")).then_inc(loaded[e], 16)

                load(0, True)
                with sp.Fori(0, groups - 1) as i:
                    load(i + 1, False)

            @block.tensor
            def _(pe):
                def spread_rows(out, j, t):
                    k, c = j // 2, j % 2
                    for h in range(2):
                        mm = pe.matmul(out[:, h, 0:half], selector[:, 128 * (k % 16):128 * (k % 16) + 128],
                                       stack[k // 16][:, 2 * h + t, c * half:(c + 1) * half], start=True, stop=True)
                    return mm

                def spread_delta(g, j):
                    u = UNITS * g + j
                    if not (isinstance(u, int) and u < 2):
                        pe.wait_ge(scanned, u - 1)
                    spread_rows(decay[j % 2], j, 0).then_inc(delta_ready, 1)

                def spread_dx(g, j):
                    u = UNITS * g + j
                    if j % PAIRS == 0:
                        pe.wait_ge(loaded[j // PAIRS], 16 * (g + 1))
                    if not (isinstance(u, int) and u == 0):
                        pe.wait_ge(dbx_ready, u)
                    spread_rows(spread, j, 1).then_inc(spread_ready, 1)

                def sum_states(g, j):
                    k, c = j // 2, j % 2
                    pe.wait_ge(weighed_ready, SLACK + UNITS * g + j + 1)
                    if k == 0:
                        pe.wait_ge(y_taken, SLACK + 2 * g + c - 1)
                    for h in range(2):
                        mm = pe.matmul(y_sum[64 * h:64 * h + 64, c, 0:half], weights[:, YSEL + 62 - 2 * k:YSEL + 126 - 2 * k],
                                       weighed[j % 4][:, h, :], start=(k == 0), stop=(k == PAIRS - 1))
                    mm.then_inc(y_added, 1)

                def step(g, j, first=False, last=False):
                    spreads = not (last and j == UNITS - 1)
                    following = (g, j + 1) if j + 1 < UNITS else (g + 1, 0)
                    if spreads:
                        spread_dx(*following)
                    if j >= LAG:
                        sum_states(g, j - LAG)
                    elif not first:
                        sum_states(g - 1, j - LAG + UNITS)
                    if spreads:
                        spread_delta(*following)

                spread_dx(0, 0)
                spread_delta(0, 0)
                for j in range(LAG):
                    step(0, j, first=True)
                with pe.Fori(0, groups - 1) as i:
                    for j in range(LAG, UNITS):
                        step(i, j)
                    for j in range(LAG):
                        step(i + 1, j)
                for j in range(LAG, UNITS):
                    step(groups - 1, j, last=True)
                for j in range(UNITS - LAG, UNITS):
                    sum_states(groups - 1, j)

            @block.scalar
            def _(act):
                with act.Fori(0, groups) as i:
                    for j in range(UNITS):
                        k = j // 2
                        act.wait_ge(delta_ready, UNITS * i + j + 1)
                        act.activation(decay[j % 2][:, :, 0:half], decay[j % 2][:, :, 0:half], ACT.Exp,
                                       scale=a_neg[:, PAIRS * layer + k:PAIRS * layer + k + 1]).then_inc(decay_ready, 1)

            @block.vector
            def _(dve):
                def product(g, j):
                    dve.wait_ge(spread_ready, UNITS * g + j + 1)
                    dve.tensor_tensor(dbx[j % 4][:, :, :], spread[:, :, 0:half], repeated(b_rep, g, j % 2),
                                      ALU.mult).then_inc(dbx_ready, 1)

                def scan(g, j):
                    u = UNITS * g + j
                    goes_on = carried and j % 2 == 1
                    dve.wait_ge(decay_ready, u + 1)
                    dve.wait_ge(dbx_ready, u + 1)
                    dve.wait_ge(weighed_ready, SLACK + u - 3)
                    if goes_on:
                        dve.wait_ge(scanned, u)
                    for h in range(2):
                        start = state[(j - 1) % 4][:, h, half - 1:half] if goes_on else 0.0
                        for a in range(0, half, segment):
                            sl = slice(a, a + segment)
                            op = dve.tensor_tensor_scan(state[j % 4][:, h, sl], decay[j % 2][:, h, sl], dbx[j % 4][:, h, sl],
                                                        start, ALU.mult, ALU.add)
                    op.then_inc(scanned, 1)

                def take_sums(g, c):
                    cols = ds(g * width + c * half, half)
                    dve.wait_ge(y_added, SLACK + UNITS * g + UNITS - 1 + c)
                    dve.scalar_tensor_tensor(out[:, cols], x[:, cols], weights[:, vec:vec + 1], y_sum[:, c, 0:half],
                                             ALU.mult, ALU.add).then_inc(y_taken, 1)

                def unit(g, j, before=True, last=False):
                    if j + 1 < UNITS:
                        product(g, j + 1)
                    elif not last:
                        product(g + 1, 0)
                    scan(g, j)
                    if before and j in (LAG - 1, LAG):
                        take_sums(g - 1, j - LAG + 1)

                product(0, 0)
                for j in range(LAG + 1):
                    unit(0, j, before=False)
                with dve.Fori(0, groups - 1) as i:
                    for j in range(LAG + 1, UNITS):
                        unit(i, j)
                    for j in range(LAG + 1):
                        unit(i + 1, j)
                for j in range(LAG + 1, UNITS):
                    unit(groups - 1, j, last=True)
                for c in range(2):
                    take_sums(groups - 1, c)

            @block.gpsimd
            def _(pool):
                for free in (weighed_ready, y_added, y_taken):
                    pool.sem_inc(free, SLACK)
                with pool.Fori(0, groups) as i:
                    for j in range(UNITS):
                        u = UNITS * i + j
                        here, before = settle(pool, u + 1), settle(pool, SLACK + u - 3)
                        pool.wait_ge(inputs_loaded, INPUT_DMAS)
                        pool.wait_ge(scanned, here)
                        pool.wait_ge(y_added, before)
                        pool.tensor_tensor(weighed[j % 4][:, :, :], state[j % 4][:, :, :], repeated(c_rep, i, j % 2),
                                           ALU.mult).then_inc(weighed_ready, 1)


def mean_of_pairs(nc, phases, layer, L, y, out):
    with nc.Block() as block:
        sem = phases.open(f"pairs{layer}")
        phases.clear_before(block)
        pooled = sem("pooled")
        half = L // 2

        @block.vector
        def _(dve):
            seq = y[:, 0:HALF * L].rearrange("p (b l) -> p b l", l=L)
            pair = seq[:, :, 0:2 * half].rearrange("p b (l two) -> p b l two", two=2)
            dst = out[:, 0:HALF * half].rearrange("p (b l) -> p b l", l=half)
            dve.tensor_tensor(dst, pair[:, :, :, 0], pair[:, :, :, 1], ALU.add).then_inc(pooled, 1)
            dve.wait_ge(pooled, 1)
            dve.tensor_scalar(dst, dst, 0.5, None, ALU.mult).then_inc(pooled, 1)


CHUNKS = 4
CHUNK = COLS // CHUNKS
GT = 88
GTILES = COLS // GT
QN, QO = [94, 93], [0, 94]


class Columns:

    def __init__(self):
        self.at, self.n = {}, 0

    def add(self, name, n):
        self.at[name] = (self.n, n)
        self.n += n


ATTN = {"L0": dict(heads=4, proj=True, pos=False), "L1": dict(heads=1, proj=False, pos=False),
        "L2": dict(heads=4, proj=True, pos=True), "L3": dict(heads=1, proj=False, pos=False)}
FFN = {"L0": dict(E=8, blocks=1, shared=0, act="Gelu", softmax_first=False),
       "L1": dict(E=8, blocks=1, shared=0, act="Relu", softmax_first=False),
       "L2": dict(E=8, blocks=2, shared=2, act="Gelu", softmax_first=True),
       "L3": dict(E=16, blocks=1, shared=0, act="Relu", softmax_first=False)}


def post_columns():
    c = Columns()
    c.add("mean", 128)
    c.add("ident", 128)
    for e in (8, 16):
        c.add(f"rank{e}", e)
    for n in ("f0_gamma", "f0_beta", "a2_gamma", "a2_beta", "f3_gamma", "f3_beta"):
        c.add(n, 1)
    for L, a in ATTN.items():
        for n in ("wq", "wk", "wv", "bv"):
            c.add(L + n, 128)
        for n in ("bq", "bk"):
            c.add(L + n, 1)
        c.add(L + "mask", 2 * a["heads"])
        if a["proj"]:
            c.add(L + "wo", 128)
            c.add(L + "bo", 1)
        if a["pos"]:
            c.add(L + "wpos", 128)
            c.add(L + "pe", TOK)
            c.add(L + "u", 1)
            c.add(L + "v", 1)
    c.add("L1scale", 1)
    for L, f in FFN.items():
        c.add(L + "wr", 2 * f["E"])
        c.add(L + "br", 2 * f["E"])
    c.add("L2b2s", 1)
    c.loads = [(0, c.n)]
    for L, f in FFN.items():
        nb, start = f["E"] * f["blocks"] + f["shared"], c.n
        c.add(L + "w1", 2 * nb * 128)
        c.add(L + "b1", nb)
        c.add(L + "w2", nb * 64)
        c.add(L + "b2", 128)
        c.loads.append((start, c.n))
    return c


PC = post_columns()


class Post:

    def __init__(self, nc, phases, W, hidden, ready):
        self.phases = phases
        self.nc, self.W, self.hidden, self.ready = nc, W, hidden, ready
        self.phase = 0

    def w(self, name, a=0, n=None):
        o, size = PC.at[name]
        return self.W[:, o + a:o + a + (size - a if n is None else n)]

    def sems(self, kind):
        self.phase += 1
        return self.phases.open(f"p{self.phase}{kind}")

    def norm(self, src, dst, affine=None, alongside=None):
        with ExitStack() as ctx:
            sem = self.sems("norm")
            nc, tag = self.nc, f"n{self.phase}"
            mean = ctx.enter_context(nc.psum_tensor(tag + "mean", [128, CHUNKS, PIECE], F32))
            var = ctx.enter_context(nc.psum_tensor(tag + "var", [128, CHUNKS, PIECE], F32))
            centred = ctx.enter_context(nc.sbuf_tensor(tag + "c", [128, COLS], F32))
            squares = ctx.enter_context(nc.sbuf_tensor(tag + "s", [128, COLS], F32))
            rstd = ctx.enter_context(nc.sbuf_tensor(tag + "r", [128, COLS], F32))
            eps = ctx.enter_context(nc.sbuf_tensor(tag + "e", [128, 1], F32))
            meaned, centred_ready, squared, var_ready, log_ready, rstd_ready, written, eps_ready = (
                sem(n) for n in ("meaned", "centred", "squared", "var", "log", "rstd", "written", "eps"))
            with nc.Block() as block:
                self.phases.clear_before(block)

                if alongside:
                    @block.gpsimd
                    def _(pool):
                        alongside(pool)

                @block.tensor
                def _(pe):
                    with pe.Fori(0, CHUNKS) as c:
                        pe.matmul(mean[:, ds(c, 1), 0:CHUNK].rearrange("p a n -> p (a n)"), self.w("mean"),
                                  src[:, ds(c * CHUNK, CHUNK)], start=True, stop=True).then_inc(meaned, 1)
                    with pe.Fori(0, CHUNKS) as c:
                        pe.wait_ge(squared, c + 1)
                        pe.matmul(var[:, ds(c, 1), 0:CHUNK].rearrange("p a n -> p (a n)"), self.w("mean"),
                                  squares[:, ds(c * CHUNK, CHUNK)], start=True, stop=True).then_inc(var_ready, 1)

                @block.vector
                def _(dve):
                    dve.memset(eps[:, :], 1e-5).then_inc(eps_ready, 1)
                    with dve.Fori(0, CHUNKS) as c:
                        dve.wait_ge(meaned, c + 1)
                        dve.tensor_tensor(centred[:, ds(c * CHUNK, CHUNK)], src[:, ds(c * CHUNK, CHUNK)],
                                          mean[:, ds(c, 1), 0:CHUNK].rearrange("p a n -> p (a n)"),
                                          ALU.subtract).then_inc(centred_ready, 1)
                    with dve.Fori(0, CHUNKS) as c:
                        cols = ds(c * CHUNK, CHUNK)
                        dve.wait_ge(rstd_ready, c + 1)
                        dve.tensor_tensor(dst[:, cols], centred[:, cols], rstd[:, cols], ALU.mult).then_inc(written, 1)
                        if affine:
                            dve.wait_ge(written, 2 * c + 1)
                            dve.tensor_scalar(dst[:, cols], dst[:, cols], self.w(affine[0]), self.w(affine[1]),
                                              ALU.mult, ALU.add).then_inc(written, 1)

                @block.scalar
                def _(act):
                    act.preload_act_table_set(LOG_AND_EXP)
                    act.wait_ge(eps_ready, 1)
                    with act.Fori(0, CHUNKS) as c:
                        cols = ds(c * CHUNK, CHUNK)
                        here = settle(act, c + 1)
                        act.wait_ge(self.ready[0], self.ready[1])
                        act.wait_ge(centred_ready, here)
                        act.activation(squares[:, cols], centred[:, cols], ACT.Square).then_inc(squared, 1)
                    with act.Fori(0, CHUNKS) as c:
                        cols = ds(c * CHUNK, CHUNK)
                        here = settle(act, c + 1)
                        act.wait_ge(self.ready[0], self.ready[1])
                        act.wait_ge(var_ready, here)
                        act.activation(rstd[:, cols], var[:, ds(c, 1), 0:CHUNK].rearrange("p a n -> p (a n)"),
                                       ACT.Ln, bias=eps[:, 0:1]).then_inc(log_ready, 1)
                        act.wait_ge(self.ready[0], self.ready[1])
                        act.wait_ge(log_ready, here)
                        act.activation(rstd[:, cols], rstd[:, cols], ACT.Exp, scale=-0.5).then_inc(rstd_ready, 1)

    def attention(self, L, xn):
        a = ATTN[L]
        H, pos = a["heads"], a["pos"]
        NV, G = (4, 2) if H == 4 else (2, 1)
        dh = D // H
        NI = 2 * G
        NH = NV * G
        nc, hidden = self.nc, self.hidden
        with ExitStack() as ctx:
            sem = self.sems("attn")
            tag = f"at{L}"
            sb = lambda name, shape, dt=F32: ctx.enter_context(nc.sbuf_tensor(tag + name, shape, dt))
            ps = lambda name, shape: ctx.enter_context(nc.psum_tensor(tag + name, shape, F32))
            xb = [sb(f"x{p}", [128, TOK]) for p in range(2)]
            qz = [sb(f"q{p}", [128, NH, TOK]) for p in range(2)]
            qs = [sb(f"qs{p}", [128, TOK]) for p in range(2)]
            ks = [sb(f"k{p}", [128, TOK]) for p in range(2)]
            vz = [[sb(f"v{p}{t}", [128, NH * (128 + dh)]) for t in range(2)] for p in range(2)]
            prob = [sb(f"p{p}", [128, NV, TOK]) for p in range(2)]
            probT = [[sb(f"pt{p}{t}", [128, NV, 94]) for t in range(2)] for p in range(2)]
            top = [sb(f"m{p}", [128, NV]) for p in range(2)]
            total = [sb(f"t{p}", [128, NV]) for p in range(2)]
            inv = [sb(f"i{p}", [128, NV]) for p in range(2)]
            o_s = [sb(f"o{p}", [128, TOK]) for p in range(2)]
            mask = sb("mask", [128, NH])
            rscale = sb("rscale", [128, 1])
            bias = sb("bias", [128, 2])
            nb = NV // 2
            S = [ps(f"S{p}", [128, nb, PIECE]) for p in range(2)]
            T = ps("T", [128, 2, PIECE])
            O = ps("O", [128, PIECE])
            M = ps("M", [128, PIECE])
            V = M if a["proj"] else ps("V", [128, PIECE])
            set_up, prepared, pos_proj = sem("set_up"), sem("prepared"), sem("pos_proj")
            pos_q, pos_taken, pos_scored = sem("pos_q"), sem("pos_taken"), sem("pos_scored")
            pos_copied = [sem(f"pos_copied{k}") for k in range(2)]
            pos_stored = [sem(f"pos_stored{m}") for m in range(4)]
            shifted_in = [sem(f"shifted_in{k}") for k in range(4)]
            x_copied, qk_ready, qk_copied, masked_dve, masked_pool, v_ready, v_placed, o_copied, projected, added_in = (
                sem(n) for n in ("x_copied", "qk_ready", "qk_copied", "masked_dve", "masked_pool", "v_ready", "v_placed",
                                 "o_copied", "projected", "added_in"))
            scored, pos_added, maxed, exped, inverted, normalised, turned, turned_a, turned_v, valued = (
                sem(n) for n in ("scored", "pos_added", "maxed", "exped", "inverted", "normalised", "turned", "turned_a",
                                 "turned_v", "valued"))
            if pos:
                skew = nc.dram_tensor(f"skew{L}", (8, NH, TOK * (TOK + 1)), F32, kind="Internal").ap()
                shifted = [sb(f"sh{p}", [128, NV, TOK]) for p in range(4)]
                score = [sb(f"sc{p}", [128, NV, TOK]) for p in range(2)]
                posT = sb("posT", [128, TOK])
                pos_heads = sb("pos_heads", [128, NH, TOK])
                q_pos = [sb(f"qp{p}", [128, TOK]) for p in range(2)]
                padded = [sb(f"pad{m}", [128, NV, TOK + 1]) for m in range(NI)]

            def s_view(m, n):
                return S[m % 2][0:n, :, 0:2 * TOK]

            with nc.Block() as block:
                self.phases.clear_before(block)

                @block.gpsimd
                def _(pool):
                    for p in range(2):
                        for t in range(2):
                            pool.memset(vz[p][t][:, :], 0.0).then_inc(set_up, 1)
                    if pos:
                        for m in range(NI):
                            pool.memset(padded[m][:, :, 0:1], 0.0).then_inc(set_up, 1)
                    for free in (pos_taken, *pos_copied, *pos_stored, v_placed, o_copied, added_in,
                                 pos_added, exped, turned, turned_a, turned_v, valued):
                        pool.sem_inc(free, SLACK)

                @block.vector
                def _(dve):
                    if L == "L1":
                        dve.reciprocal(rscale[:, :], self.w("L1scale")).then_inc(prepared, 1)
                        dve.wait_ge(prepared, 1)
                        dve.tensor_scalar(mask[:, :], self.w(L + "mask"), rscale[:, 0:1], None, ALU.mult).then_inc(prepared, 1)
                    else:
                        dve.tensor_copy(mask[:, :], self.w(L + "mask")).then_inc(prepared, 1)
                    if pos:
                        dve.tensor_tensor(bias[:, 0:1], self.w(L + "bq"), self.w(L + "u"), ALU.add).then_inc(prepared, 1)
                        dve.tensor_tensor(bias[:, 1:2], self.w(L + "bq"), self.w(L + "v"), ALU.add).then_inc(prepared, 1)
                        dve.wait_ge(pos_proj, 2)
                        for v in range(NH):
                            dve.tensor_scalar(pos_heads[:, v, :], posT[:, :], self.w(L + "mask", v, 1), None,
                                              ALU.mult).then_inc(prepared, 1)
                    else:
                        dve.tensor_copy(bias[:, 0:1], self.w(L + "bq")).then_inc(prepared, 1)

                if pos:
                    @block.tensor
                    def _(pe):
                        pe.matmul(M[:, 0:TOK], self.w(L + "wpos"), self.w(L + "pe"), start=True, stop=True).then_inc(pos_proj, 1)

                    @block.scalar
                    def _(act):
                        act.wait_ge(pos_proj, 1)
                        act.activation(posT[:, :], M[:, 0:TOK], ACT.Copy).then_inc(pos_proj, 1)

            if pos:
                proj_bank = [M, O]
                with nc.Block() as block:
                    @block.tensor
                    def _(pe):
                        def project_q(b, p):
                            pe.wait_ge(pos_taken, SLACK + b - 1)
                            pe.matmul(proj_bank[p][:, 0:TOK], self.w(L + "wq"), xn[:, ds(b * TOK, TOK)], start=True,
                                      stop=True).then_inc(pos_q, 1)

                        def batches(i, last):
                            for p in range(2):
                                b = 2 * i + p
                                if not (last and p == 1):
                                    project_q(b + 1, 1 - p)
                                pe.wait_ge(pos_taken, SLACK + b + 1)
                                for m in range(NI):
                                    t, g = m // G, m % G
                                    n = QN[t]
                                    pe.wait_ge(pos_copied[m % 2], SLACK + 2 * b + m // 2)
                                    for v in range(NV):
                                        mm = pe.matmul(S[m % 2][0:n, v // 2, (v % 2) * TOK:(v % 2) * TOK + TOK],
                                                       q_pos[p][:, QO[t]:QO[t] + n], pos_heads[:, g * NV + v, :],
                                                       start=True, stop=True)
                                    mm.then_inc(pos_scored, 1)

                        project_q(0, 0)
                        with pe.Fori(0, 3) as i:
                            batches(i, False)
                        batches(3, True)

                    def copy_scores(b, m, eng, copy):
                        n = QN[m // G]
                        eng.wait_ge(pos_scored, b * NI + m + 1)
                        eng.wait_ge(pos_stored[m], SLACK + 16 * b)
                        copy(padded[m][0:n, :, 1:TOK + 1].rearrange("p (a v) n -> p a v n", a=nb),
                             s_view(m, n).rearrange("p a (v n) -> p a v n", v=2)).then_inc(pos_copied[m % 2], 1)

                    @block.vector
                    def _(dve):
                        def take_q(b, p):
                            dve.wait_ge(pos_q, b + 1)
                            if not (isinstance(b, int) and b < 2):
                                dve.wait_ge(pos_scored, NI * (b - 1))
                            dve.tensor_scalar(q_pos[p][:, :], proj_bank[p][:, 0:TOK], bias[:, 1:2], None,
                                              ALU.add).then_inc(pos_taken, 1)

                        def batches(i, last):
                            for p in range(2):
                                b = 2 * i + p
                                for m in (1, 3):
                                    copy_scores(b, m, dve, dve.tensor_copy)
                                    if m == 1 and not (last and p == 1) and not (isinstance(b, int) and b == 0):
                                        take_q(b + 1, 1 - p)

                        take_q(0, 0)
                        take_q(1, 1)
                        batches(0, False)
                        with dve.Fori(1, 3) as i:
                            batches(i, False)
                        batches(3, True)

                    @block.scalar
                    def _(act):
                        with act.Fori(0, 4) as i:
                            for p in range(2):
                                for m in (0, 2):
                                    copy_scores(2 * i + p, m, act, lambda out, src: act.activation(out, src, ACT.Copy))

                    @block.sync
                    def _(sp):
                        with sp.Fori(0, 8) as b:
                            for m in range(NI):
                                t, g = m // G, m % G
                                sp.wait_ge(pos_copied[m % 2], SLACK + 2 * b + m // 2 + 1)
                                dst = skew[ds(b, 1), g * NV:(g + 1) * NV, QO[t] * (TOK + 1):(QO[t] + QN[t]) * (TOK + 1)]
                                sp.dma_start(dst.rearrange("o v (q n) -> (o q) v n", n=TOK + 1),
                                             padded[m][0:QN[t], :, :]).then_inc(pos_stored[m], 16)
                        for m in range(NI):
                            sp.wait_ge(pos_stored[m], SLACK + 16 * 8)

            n_items, per_turn = 8 * NI, 2 * NI
            V_AHEAD = 3 if a["proj"] else 2
            FIRST, START = -4, 3
            TURNS = (n_items - START - 5) // per_turn
            END = n_items + (NI - 2 if a["proj"] else 0)

            class At:

                def __init__(self, i, s):
                    self.i, self.s = i, s

                def item(self, ahead):
                    x = self.s + ahead
                    if self.i is None:
                        return (x, x % per_turn) if 0 <= x < n_items else None
                    return self.i * per_turn + x, x % per_turn

                def batch(self, ahead, back=0):
                    x = self.s + ahead
                    if x % NI:
                        return None
                    b = x // NI - back
                    if self.i is None:
                        return (b, b % 2) if 0 <= b < 8 else None
                    return self.i * 2 + b, b % 2

            def run(eng, step):
                for s_ in range(FIRST, START):
                    step(At(None, s_))
                with eng.Fori(0, TURNS) as i:
                    for s_ in range(START, START + per_turn):
                        step(At(i, s_))
                for s_ in range(START + TURNS * per_turn, END + 1):
                    step(At(None, s_))

            def place(m):
                t, g = m % NI // G, m % NI % G
                return t, g, QN[t]

            with nc.Block() as block:
                masked_here = NH // 2

                @block.gpsimd
                def _(pool):
                    def step(at):
                        if at.batch(5):
                            b, p = at.batch(5)
                            free = settle(pool, SLACK + b - 1)
                            pool.wait_ge(self.ready[0], self.ready[1])
                            pool.wait_ge(v_placed, free)
                            pool.tensor_copy(xb[p][:, :], xn[:, ds(b * TOK, TOK)]).then_inc(x_copied, 1)
                        if at.batch(4):
                            b, p = at.batch(4)
                            here = settle(pool, b + 1)
                            pool.wait_ge(self.ready[0], self.ready[1])
                            pool.wait_ge(qk_copied, here)
                            for v in range(masked_here, NH):
                                op = pool.tensor_scalar(qz[p][:, v, :], qs[p][:, :], mask[:, v:v + 1], None, ALU.mult)
                            op.then_inc(masked_pool, 1)

                    step(At(None, FIRST - 1))
                    run(pool, step)

                if pos:
                    @block.sync
                    def _(sp):
                        with sp.Fori(0, 4) as i:
                            for x in range(per_turn):
                                t, g, n = place(x)
                                u, b = i * per_turn + x, 2 * i + x // NI
                                sp.wait_ge(pos_added, SLACK + u - 3)
                                src = skew[ds(b, 1), g * NV:(g + 1) * NV, TOK * (1 + QO[t]):TOK * (1 + QO[t] + n)]
                                sp.dma_start(shifted[x % 4][0:n, :, :],
                                             src.rearrange("o v (q n) -> (o q) v n", n=TOK)).then_inc(shifted_in[x % 4], 16)

                @block.tensor
                def _(pe):
                    def step(at):
                        if at.batch(4):
                            b, p = at.batch(4)
                            pe.wait_ge(x_copied, b + 1)
                            if a["proj"]:
                                pe.wait_ge(v_placed, SLACK + b)
                                pe.wait_ge(added_in, SLACK + b - 2)
                            elif not (isinstance(b, int) and b == 0):
                                pe.wait_ge(qk_copied, b)
                            pe.matmul(M[:, 0:TOK], self.w(L + "wq"), xb[p][:, :], start=True, stop=True)
                            pe.matmul(M[:, TOK:2 * TOK], self.w(L + "wk"), xb[p][:, :], start=True,
                                      stop=True).then_inc(qk_ready, 1)
                        if at.item(3):
                            u, x = at.item(3)
                            t, g, n = place(x)
                            p = x // NI
                            b = u // NI if at.i is None else at.i * 2 + (at.s + 3) // NI
                            if x % NI == 0:
                                pe.wait_ge(masked_dve, b + 1)
                            if x % NI == G - 1:
                                pe.wait_ge(masked_pool, b + 1)
                            pe.wait_ge(exped, SLACK + u - 1)
                            if pos:
                                pe.wait_ge(pos_added, SLACK + u - 1)
                            for v in range(NV):
                                mm = pe.matmul(S[x % 2][0:n, v // 2, (v % 2) * TOK:(v % 2) * TOK + TOK],
                                               qz[p][:, g * NV + v, QO[t]:QO[t] + n], ks[p][:, :], start=True, stop=True)
                            mm.then_inc(scored, 1)
                        if at.item(1):
                            u, x = at.item(1)
                            n = place(x)[2]
                            pe.wait_ge(normalised, u + 1)
                            pe.wait_ge(turned_a, SLACK + u)
                            pe.wait_ge(turned_v, SLACK + u)
                            for t in range(2):
                                for v in range(NV):
                                    mm = pe.transpose(T[0:QN[t], t, v * 94:v * 94 + n],
                                                      prob[x % 2][0:n, v, QO[t]:QO[t] + QN[t]], self.w("ident")[0:n, 0:n])
                            mm.then_inc(turned, 1)
                        if at.batch(V_AHEAD):
                            b, p = at.batch(V_AHEAD)
                            pe.wait_ge(qk_copied, b + 1)
                            pe.wait_ge(v_placed, SLACK + b)
                            for t in range(2):
                                mm = pe.matmul(V[0:QN[t], 128 * t:128 * t + 128], xb[p][:, QO[t]:QO[t] + QN[t]],
                                               self.w(L + "wv"), start=True, stop=True)
                            mm.then_inc(v_ready, 1)
                        if a["proj"] and at.batch(2, back=2):
                            b, p = at.batch(2, back=2)
                            pe.wait_ge(o_copied, SLACK + b + 1)
                            pe.wait_ge(added_in, SLACK + b)
                            pe.wait_ge(v_placed, SLACK + (min(b + 3, 8) if at.i is None else b + 3))
                            pe.matmul(M[:, 0:TOK], self.w(L + "wo"), o_s[p][:, :], start=True, stop=True).then_inc(projected, 1)
                        if at.item(0):
                            u, x = at.item(0)
                            t, g, n = place(x)
                            p = x // NI
                            pe.wait_ge(turned_a, SLACK + u + 1)
                            pe.wait_ge(turned_v, SLACK + u + 1)
                            if x % NI == 0:
                                b = at.batch(0)[0]
                                pe.wait_ge(v_placed, SLACK + b + 1)
                                pe.wait_ge(o_copied, SLACK + b)
                            for v in range(NV):
                                gv = g * NV + v
                                for k in range(2):
                                    mm = pe.matmul(O[:, QO[t]:QO[t] + n], vz[p][k][0:QN[k], gv * 128:gv * 128 + 128],
                                                   probT[x % 2][k][0:QN[k], v, 0:n], start=(gv == 0 and k == 0),
                                                   stop=(gv == NH - 1 and k == 1))
                            mm.then_inc(valued, 1)

                    run(pe, step)

                @block.vector
                def _(dve):
                    def step(at):
                        if at.batch(4):
                            b, p = at.batch(4)
                            dve.wait_ge(qk_copied, b + 1)
                            for v in range(masked_here):
                                op = dve.tensor_scalar(qz[p][:, v, :], qs[p][:, :], mask[:, v:v + 1], None, ALU.mult)
                            op.then_inc(masked_dve, 1)
                        if not a["proj"] and at.batch(0, back=1):
                            b, p = at.batch(0, back=1)
                            cols = ds(b * TOK, TOK)
                            dve.wait_ge(valued, SLACK + NI * (b + 1))
                            dve.tensor_tensor(hidden[:, cols], O[:, 0:TOK], hidden[:, cols], ALU.add).then_inc(o_copied, 1)
                        if at.item(3):
                            u, x = at.item(3)
                            n = place(x)[2]
                            dve.wait_ge(scored, u + 1)
                            if pos:
                                loads = u // 4 + 1 if at.i is None else at.i * (per_turn // 4) + (at.s + 3) // 4 + 1
                                dve.wait_ge(shifted_in[x % 4], 16 * loads)
                                dve.tensor_tensor(score[x % 2][0:n, :, :].rearrange("p (a v) n -> p a (v n)", a=nb), s_view(x, n),
                                                  shifted[x % 4][0:n, :, :].rearrange("p (a v) n -> p a (v n)", a=nb),
                                                  ALU.add).then_inc(pos_added, 1)
                                dve.wait_ge(pos_added, SLACK + u + 1)
                                dve.tensor_reduce(top[x % 2][0:n, :], score[x % 2][0:n, :, :], AX.X, ALU.max,
                                                  negate=True).then_inc(maxed, 1)
                            else:
                                dve.tensor_reduce(top[x % 2][0:n, :].rearrange("p (a v) -> p a v", a=nb),
                                                  s_view(x, n).rearrange("p a (v n) -> p a v n", v=2), AX.X, ALU.max,
                                                  negate=True).then_inc(maxed, 1)
                        if at.item(2):
                            u, x = at.item(2)
                            n = place(x)[2]
                            dve.wait_ge(exped, SLACK + u + 1)
                            dve.reciprocal(inv[x % 2][0:n, :], total[x % 2][0:n, :]).then_inc(inverted, 1)
                            dve.wait_ge(inverted, u + 1)
                            dve.tensor_tensor(prob[x % 2][0:n, :, :], prob[x % 2][0:n, :, :],
                                              inv[x % 2][0:n, :].unsqueeze(2).to_broadcast([n, NV, TOK]),
                                              ALU.mult).then_inc(normalised, 1)
                        if at.item(1):
                            u, x = at.item(1)
                            n = place(x)[2]
                            dve.wait_ge(turned, SLACK + u + 1)
                            dve.wait_ge(valued, SLACK + u - 1)
                            dve.tensor_copy(probT[x % 2][1][0:QN[1], :, 0:n],
                                            T[0:QN[1], 1, 0:NV * 94].rearrange("p (v n) -> p v n", n=94)[:, :, 0:n]).then_inc(turned_v, 1)
                        if at.batch(V_AHEAD):
                            b, p = at.batch(V_AHEAD)
                            dve.wait_ge(v_ready, b + 1)
                            for t in range(2):
                                out = vz[p][t][0:QN[t], :].rearrange("p (v c) -> p v c", c=128 + dh)[:, :, 0:dh]
                                op = dve.tensor_tensor(out, V[0:QN[t], 128 * t:128 * t + 128].rearrange("p (v c) -> p v c", c=dh),
                                                       self.w(L + "bv")[0:QN[t], :].rearrange("p (v c) -> p v c", c=dh), ALU.add)
                            op.then_inc(v_placed, 1)
                        if a["proj"] and at.batch(2, back=2):
                            b, p = at.batch(2, back=2)
                            cols = ds(b * TOK, TOK)
                            dve.wait_ge(projected, b + 1)
                            dve.scalar_tensor_tensor(hidden[:, cols], M[:, 0:TOK], self.w(L + "bo"), hidden[:, cols],
                                                     ALU.add, ALU.add).then_inc(added_in, 1)

                    run(dve, step)

                @block.scalar
                def _(act):
                    def step(at):
                        if at.batch(4):
                            b, p = at.batch(4)
                            act.wait_ge(qk_ready, b + 1)
                            act.activation(qs[p][:, :], M[:, 0:TOK], ACT.Identity, bias=bias[:, 0:1])
                            act.activation(ks[p][:, :], M[:, TOK:2 * TOK], ACT.Identity,
                                           bias=self.w(L + "bk")).then_inc(qk_copied, 1)
                        if a["proj"] and at.batch(0, back=1):
                            b, p = at.batch(0, back=1)
                            act.wait_ge(valued, SLACK + NI * (b + 1))
                            act.activation(o_s[p][:, :], O[:, 0:TOK], ACT.Copy).then_inc(o_copied, 1)
                        if at.item(1):
                            u, x = at.item(1)
                            n = place(x)[2]
                            act.wait_ge(turned, SLACK + u + 1)
                            act.wait_ge(valued, SLACK + u - 1)
                            act.activation(probT[x % 2][0][0:QN[0], :, 0:n],
                                           T[0:QN[0], 0, 0:NV * 94].rearrange("p (v n) -> p v n", n=94)[:, :, 0:n],
                                           ACT.Copy).then_inc(turned_a, 1)
                        if at.item(3):
                            u, x = at.item(3)
                            n = place(x)[2]
                            act.wait_ge(maxed, u + 1)
                            act.wait_ge(turned, SLACK + u - 1)
                            for v in range(NV):
                                src = score[x % 2][0:n, v, :] if pos else S[x % 2][0:n, v // 2, (v % 2) * TOK:(v % 2) * TOK + TOK]
                                op = act.activation(prob[x % 2][0:n, v, :], src, ACT.Exp, bias=top[x % 2][0:n, v:v + 1],
                                                    accum_out=total[x % 2][0:n, v:v + 1])
                            op.then_inc(exped, 1)

                    run(act, step)

    def gate(self, L, xn, parts_T, weights_T):
        f = FFN[L]
        E = f["E"]
        nc = self.nc
        with ExitStack() as ctx:
            sem = self.sems("gate")
            tag = f"g{L}"
            sb = lambda name, shape, dt=F32: ctx.enter_context(nc.sbuf_tensor(tag + name, shape, dt))
            LG = ctx.enter_context(nc.psum_tensor(tag + "LG", [128, 2 * PIECE], F32))
            TB = ctx.enter_context(nc.psum_tensor(tag + "TB", [96, 2, 2 * PIECE], BF16))
            TF = ctx.enter_context(nc.psum_tensor(tag + "TF", [32, 4, PIECE], F32))
            R = 2 * GTILES
            val, work, hot1, hot2, w = (sb(n, [GT, R, E]) for n in ("val", "work", "hot1", "hot2", "w"))
            m1, m2, r, ex, rd = (sb(n, [GT, R]) for n in ("m1", "m2", "r", "ex", "rd"))
            parts = sb("parts", [GT, GTILES, 3, 32], BF16)
            wpad = sb("wpad", [GT, GTILES, 32])
            identb = sb("identb", [128, 128], BF16)
            logits, step, exped, turned, copied, cleared = (sem(n) for n in ("logits", "step", "exped", "turned", "copied", "cleared"))
            wide = lambda t: t[:, :].unsqueeze(2).to_broadcast([GT, R, E])
            rank = self.w(f"rank{E}")[0:GT, :].unsqueeze(1).to_broadcast([GT, R, E])
            bias = self.w(L + "br")[0:GT, 0:E].unsqueeze(1).to_broadcast([GT, R, E])
            count = [0]
            fu = f["softmax_first"]

            with nc.Block() as block:
                self.phases.clear_before(block)

                @block.gpsimd
                def _(pool):
                    if E == 8:
                        pool.memset(parts[:, :, :, :], 0.0).then_inc(cleared, 1)
                        pool.memset(wpad[:, :, :], 0.0).then_inc(cleared, 1)
                    pool.tensor_copy(identb[:, :], self.w("ident")).then_inc(cleared, 1)

                @block.tensor
                def _(pe):
                    for t in range(GTILES):
                        mm = pe.matmul(LG[0:GT, 2 * E * t:2 * E * t + 2 * E], xn[:, GT * t:GT * t + GT], self.w(L + "wr"),
                                       start=True, stop=True)
                    mm.then_inc(logits, 1)
                    pe.wait_ge(copied, 1)
                    pe.wait_ge(cleared, 3 if E == 8 else 1)
                    for t in range(GTILES):
                        mm = pe.transpose(TB[0:96, t // 9, (t % 9) * GT:(t % 9) * GT + GT],
                                          parts[:, t, :, :].rearrange("p s r -> p (s r)"), identb[0:GT, 0:GT])
                    mm.then_inc(turned, 1)
                    for t in range(GTILES):
                        mm = pe.transpose(TF[0:32, t // 5, (t % 5) * GT:(t % 5) * GT + GT], wpad[:, t, :],
                                          self.w("ident")[0:GT, 0:GT])
                    mm.then_inc(turned, 1)

                @block.scalar
                def _(act):
                    act.wait_ge(exped, 1)
                    if fu:
                        act.activation(work[:, :, :], val[:, :, :], ACT.Exp).then_inc(exped, 1)
                    else:
                        act.activation(ex[:, :], ex[:, :], ACT.Exp).then_inc(exped, 1)
                    act.wait_ge(turned, 2)
                    for k in range(4):
                        n = min(5, GTILES - 5 * k) * GT
                        act.activation(weights_T[:, 5 * GT * k:5 * GT * k + n], TF[0:32, k, 0:n], ACT.Copy).then_inc(copied, 1)

                @block.vector
                def _(dve):
                    def done(ins):
                        count[0] += 1
                        ins.then_inc(step, 1)
                        dve.wait_ge(step, count[0])

                    dve.wait_ge(logits, 1)
                    done(dve.tensor_tensor(val[:, :, :], LG[0:GT, 0:R * E].rearrange("p (r e) -> p r e", e=E), bias, ALU.add))
                    if L == "L1":
                        done(dve.tensor_tensor(val[:, :, :], val[:, :, :],
                                               self.w(L + "br")[0:GT, E:2 * E].unsqueeze(1).to_broadcast([GT, R, E]), ALU.add))
                    if fu:
                        done(dve.tensor_reduce(m1[:, :], val[:, :, :], AX.X, ALU.max))
                        dve.tensor_tensor(val[:, :, :], val[:, :, :], wide(m1), ALU.subtract).then_inc(exped, 1)
                        dve.wait_ge(exped, 2)
                        done(dve.tensor_reduce(r[:, :], work[:, :, :], AX.X, ALU.add))
                        done(dve.reciprocal(rd[:, :], r[:, :]))
                        done(dve.tensor_tensor(val[:, :, :], work[:, :, :], wide(rd), ALU.mult))

                    def choose(top, hot):
                        done(dve.tensor_reduce(top[:, :], val[:, :, :], AX.X, ALU.max))
                        done(dve.tensor_tensor(work[:, :, :], val[:, :, :], wide(top), ALU.is_equal))
                        done(dve.tensor_tensor(work[:, :, :], work[:, :, :], rank, ALU.mult))
                        done(dve.tensor_reduce(r[:, :], work[:, :, :], AX.X, ALU.max))
                        done(dve.tensor_tensor(hot[:, :, :], work[:, :, :], wide(r), ALU.is_equal))

                    choose(m1, hot1)
                    done(dve.scalar_tensor_tensor(val[:, :, :], hot1[:, :, :], -1e30, val[:, :, :], ALU.mult, ALU.add))
                    choose(m2, hot2)
                    if fu:
                        done(dve.tensor_tensor(ex[:, :], m1[:, :], m2[:, :], ALU.add))
                        done(dve.reciprocal(rd[:, :], ex[:, :]))
                        done(dve.tensor_tensor(m1[:, :], m1[:, :], rd[:, :], ALU.mult))
                        done(dve.tensor_tensor(m2[:, :], m2[:, :], rd[:, :], ALU.mult))
                    else:
                        dve.tensor_tensor(ex[:, :], m2[:, :], m1[:, :], ALU.subtract).then_inc(exped, 1)
                        dve.wait_ge(exped, 2)
                        done(dve.tensor_scalar(r[:, :], ex[:, :], 1.0, None, ALU.add))
                        done(dve.reciprocal(m1[:, :], r[:, :]))
                        done(dve.tensor_tensor(m2[:, :], ex[:, :], m1[:, :], ALU.mult))
                    done(dve.tensor_tensor(hot1[:, :, :], hot1[:, :, :], wide(m1), ALU.mult))
                    done(dve.tensor_tensor(hot2[:, :, :], hot2[:, :, :], wide(m2), ALU.mult))
                    done(dve.tensor_tensor(w[:, :, :], hot1[:, :, :], hot2[:, :, :], ALU.add))
                    dve.wait_ge(cleared, 3 if E == 8 else 1)
                    flat = w[:, :, :].rearrange("p (t h) e -> p t (h e)", h=2)
                    rest = hot1[:, :, :].rearrange("p (t h) e -> p t (h e)", h=2)
                    part = lambda s: parts[:, :, s, 0:2 * E]
                    done(dve.tensor_copy(part(0), flat))
                    done(dve.tensor_tensor(rest, flat, part(0), ALU.subtract))
                    done(dve.tensor_copy(part(1), rest))
                    done(dve.tensor_tensor(part(2), rest, part(1), ALU.subtract))
                    dve.tensor_copy(wpad[:, :, 0:2 * E], flat).then_inc(copied, 1)
                    dve.wait_ge(turned, 1)
                    for k in range(2):
                        n = (9, GTILES - 9)[k] * GT
                        dve.tensor_copy(parts_T[:, 9 * GT * k:9 * GT * k + n], TB[0:96, k, 0:n]).then_inc(copied, 1)

    def experts(self, L, xn, parts_T, weights_T, dst, base):
        f = FFN[L]
        E, per_expert, shared = f["E"], f["blocks"], f["shared"]
        NB = E * per_expert + shared
        blocks = [(None, k, E * per_expert + k) for k in range(shared)]
        blocks += [(e, k, e * per_expert + k) for e in range(E) for k in range(per_expert)]
        nc = self.nc
        func = {"Gelu": ACT.Gelu, "Relu": ACT.Relu}[f["act"]]
        loaded = self.ffn_loaded[L]
        selector = self.selectors[E]
        with ExitStack() as ctx:
            sem = self.sems("moe")
            tag = f"m{L}"
            ps = lambda name, *shape: ctx.enter_context(nc.psum_tensor(tag + name, [128, *shape], F32))
            sb = lambda name, *shape: ctx.enter_context(nc.sbuf_tensor(tag + name, [128, *shape], F32))
            hid = [ps(f"hid{k}", 2, PIECE) for k in range(2)]
            out_e = [ps(f"out{k}", PIECE) for k in range(2)]
            weight, plain = ps("weight", PIECE), ps("plain", PIECE)
            g = [sb(f"g{k}", 2, CHUNK) for k in range(2)]
            weight_in = [sb(f"weight_in{k}", CHUNK) for k in range(2)]
            product = [sb(f"product{k}", CHUNK) for k in range(2)]
            hidden_ready, activated, multiplied = sem("hidden_ready"), sem("activated"), sem("multiplied")
            plain_ready, plain_taken = sem("plain_ready"), sem("plain_taken")
            weight_ready, weight_copied, weighed, summed = (
                sem(n) for n in ("weight_ready", "weight_copied", "weighed", "summed"))
            cols = lambda c: ds(c * CHUNK, CHUNK)
            rows = lambda h: slice(64 * h, 64 * h + 64)

            with nc.Block() as block:
                self.phases.clear_before(block)

                @block.tensor
                def _(pe):
                    def up(c, u):
                        n = blocks[u][2]
                        if not (isinstance(c, int) and c * NB + u < 2):
                            pe.wait_ge(activated, c * NB + u - 1)
                        for h in range(2):
                            pe.matmul(hid[u % 2][:, h, 0:CHUNK], self.w(L + "w1", (h * NB + n) * 128, 128),
                                      xn[:, cols(c)], start=True, stop=True).then_inc(hidden_ready, 1)

                    def down(c, u):
                        e, k, n = blocks[u]
                        pe.wait_ge(activated, c * NB + u + 1)
                        if e is None:
                            target, start, stop = plain, False, u == shared - 1
                        else:
                            target, start, stop = out_e[e % 2], k == 0, k == per_expert - 1
                            if start:
                                pe.wait_ge(weighed, SLACK + c * E + e - 1)
                                pe.wait_ge(weight_copied, SLACK + c * E + e)
                                pe.matmul(weight[:, 0:CHUNK], selector[:, 128 * e:128 * e + 128], parts_T[:, cols(c)],
                                          start=True, stop=True).then_inc(weight_ready, 1)
                        for h in range(2):
                            pe.matmul(target[rows(h), 0:CHUNK], self.w(L + "w2", n * 64, 64), g[u % 2][:, h, :],
                                      start=start, stop=stop).then_inc(multiplied, 1)

                    def chunk(c, last):
                        pe.wait_ge(plain_taken, SLACK + c)
                        pe.matmul(plain[:, 0:CHUNK], self.w(L + "b2")[0:32, :], weights_T[:, cols(c)],
                                  start=True, stop=not shared).then_inc(plain_ready, 1)
                        for u in range(NB):
                            down(c, u)
                            if u + 2 < NB:
                                up(c, u + 2)
                            elif not last:
                                up(c + 1, u + 2 - NB)

                    pe.wait_ge(loaded, 16)
                    up(0, 0)
                    up(0, 1)
                    with pe.Fori(0, CHUNKS - 1) as c:
                        chunk(c, False)
                    chunk(CHUNKS - 1, True)

                @block.scalar
                def _(act):
                    act.wait_ge(loaded, 16)
                    with act.Fori(0, CHUNKS) as c:
                        for u in range(NB):
                            e, k, n = blocks[u]
                            act.wait_ge(hidden_ready, 2 * (c * NB + u + 1))
                            act.wait_ge(multiplied, SLACK + 2 * (c * NB + u - 1))
                            act.activation(g[u % 2][:, :, :], hid[u % 2][:, :, 0:CHUNK], func,
                                           bias=self.w(L + "b1", n, 1)).then_inc(activated, 1)
                            if e is not None and k == 0:
                                act.wait_ge(weight_ready, c * E + e + 1)
                                act.wait_ge(weighed, SLACK + c * E + e - 1)
                                act.activation(weight_in[e % 2][:, :], weight[:, 0:CHUNK], ACT.Copy).then_inc(weight_copied, 1)

                @block.vector
                def _(dve):
                    def add_product(c, e):
                        dve.wait_ge(weighed, SLACK + c * E + e + 1)
                        dve.wait_ge(summed, SLACK + c * E + e)
                        dve.tensor_tensor(dst[:, cols(c)], product[e % 2][:, :], dst[:, cols(c)], ALU.add).then_inc(summed, 1)

                    with dve.Fori(0, CHUNKS) as c:
                        dve.wait_ge(plain_ready, c + 1)
                        if shared:
                            dve.wait_ge(multiplied, SLACK + 2 * (c * NB + shared))
                            op = dve.scalar_tensor_tensor(dst[:, cols(c)], plain[:, 0:CHUNK], self.w("L2b2s"), base[:, cols(c)],
                                                          ALU.add, ALU.add)
                        else:
                            op = dve.tensor_tensor(dst[:, cols(c)], plain[:, 0:CHUNK], base[:, cols(c)], ALU.add)
                        op.then_inc(plain_taken, 1)
                        for e in range(E):
                            dve.wait_ge(multiplied, SLACK + 2 * (c * NB + shared + (e + 1) * per_expert))
                            dve.wait_ge(weight_copied, SLACK + c * E + e + 1)
                            if e == 0:
                                dve.wait_ge(plain_taken, SLACK + c + 1)
                            dve.wait_ge(summed, SLACK + c * E + e - 1)
                            dve.tensor_tensor(product[e % 2][:, :], out_e[e % 2][:, 0:CHUNK], weight_in[e % 2][:, :],
                                              ALU.mult).then_inc(weighed, 1)
                            if e > 0:
                                add_product(c, e - 1)
                        add_product(c, E - 1)

                @block.gpsimd
                def _(pool):
                    for free in (plain_taken, weighed, summed, multiplied, weight_copied):
                        pool.sem_inc(free, SLACK)

    def add(self, dst, a, b):
        with self.nc.Block() as block:
            added = self.sems("add")("added")
            self.phases.clear_before(block)

            @block.vector
            def _(dve):
                dve.tensor_tensor(dst[:, :], a[:, :], b[:, :], ALU.add).then_inc(added, 1)


def post(nc, phases, hidden, weights_in):
    with ExitStack() as ctx:
        sb = lambda name, shape, dt=F32: ctx.enter_context(nc.sbuf_tensor(name, shape, dt))
        W = sb("post_weights", [128, PC.n])
        selectors = {E: sb(f"expert_selector{E}", [96, E * 128], BF16) for E in (8, 16)}
        xn, x2 = sb("xn", [128, COLS]), sb("x2", [128, COLS])
        parts_T = sb("parts_T", [96, COLS], BF16)
        weights_T = sb("weights_T", [32, COLS])
        loaded = ctx.enter_context(nc.semaphore("post_loaded"))
        selected = ctx.enter_context(nc.semaphore("post_selected"))
        ffn_loaded = {L: ctx.enter_context(nc.semaphore(f"ffn_loaded_{L}")) for L in FFN}

        def load(sp, k, sem):
            a, b = PC.loads[k]
            sp.dma_start(W[:, a:b], weights_in[:, a:b]).then_inc(sem, 16)

        with nc.Block() as block:
            @block.sync
            def _(sp):
                load(sp, 0, loaded)
                for k, L in enumerate(FFN):
                    load(sp, k + 1, ffn_loaded[L])
                sp.wait_ge(loaded, 16)
        P = Post(nc, phases, W, hidden, (loaded, 16))
        P.selectors, P.ffn_loaded = selectors, ffn_loaded

        def make_selectors(pool):
            expert_selector(pool, selectors[8], 8, selected, 0)
            expert_selector(pool, selectors[16], 16, selected, 7)

        for L in ("L0", "L1", "L2", "L3"):
            P.norm(hidden, xn, alongside=make_selectors if L == "L0" else None)
            if L == "L2":
                P.norm(xn, xn, ("a2_gamma", "a2_beta"))
            P.attention(L, xn)
            P.norm(hidden, xn)
            if L == "L0":
                P.norm(xn, xn, ("f0_gamma", "f0_beta"))
            P.gate(L, xn, parts_T, weights_T)
            if L == "L3":
                P.experts(L, xn, parts_T, weights_T, x2, xn)
                P.norm(x2, x2, ("f3_gamma", "f3_beta"))
                P.add(hidden, hidden, x2)
            else:
                P.experts(L, xn, parts_T, weights_T, hidden, hidden)


def build(nc, x_in, ssm_w, post_w, out):
    phases = Phases(nc)
    with ExitStack() as ctx:
        sb = lambda name, shape, dt: ctx.enter_context(nc.sbuf_tensor(name, shape, dt))
        hidden = sb("hidden", [128, COLS], F32)
        inputs_loaded = ctx.enter_context(nc.semaphore("inputs_loaded"))
        rest_loaded = ctx.enter_context(nc.semaphore("rest_loaded"))
        with ExitStack() as ssm:
            ssb = lambda name, shape, dt: ssm.enter_context(nc.sbuf_tensor(name, shape, dt))
            weights = ssb("ssm_weights", [128, SSM_W], F32)
            selector = ssb("selector", [96, 16 * 128], BF16)
            a_neg = ssb("a_neg", [128, SSM_LAYERS * PAIRS], F32)
            xa = ssb("xa", [128, HALF * SEQ], F32)
            xb = ssb("xb", [128, HALF * LENS[1]], F32)
            a_done = ctx.enter_context(nc.semaphore("a_done"))
            selected = ctx.enter_context(nc.semaphore("selected"))
            with nc.Block() as block:

                @block.sync
                def _(sp):
                    sp.dma_start(weights[:, :], ssm_w).then_inc(inputs_loaded, 16)
                    sp.dma_start(xa[:, 0:FIRST_COLS], x_in[:, 0:FIRST_COLS]).then_inc(inputs_loaded, 16)
                    sp.dma_start(xa[:, FIRST_COLS:], x_in[:, FIRST_COLS:]).then_inc(rest_loaded, 16)
                    sp.wait_ge(inputs_loaded, INPUT_DMAS)

                @block.gpsimd
                def _(pool):
                    selector_of(pool, selector, 64, selected)

                @block.scalar
                def _(act):
                    act.wait_ge(inputs_loaded, INPUT_DMAS)
                    for i in range(SSM_LAYERS):
                        act.activation(a_neg[:, PAIRS * i:PAIRS * (i + 1)],
                                       weights[:, i * SSM_COLS + SSM_A:i * SSM_COLS + SSM_A + PAIRS], ACT.Exp).then_inc(a_done, 1)

                @block.vector
                def _(dve):
                    dve.wait_ge(a_done, SSM_LAYERS)
                    dve.tensor_scalar(a_neg[:, :], a_neg[:, :], -1.0, None, ALU.mult).then_inc(a_done, 1)

            x = [xa, xb, xa]
            for layer in range(SSM_LAYERS):
                L = LENS[layer]
                seqs = max(1, SEQ // L)
                width = seqs * L
                split_dram = nc.dram_tensor(f"split{layer}", (HALF // seqs, 2, 96, 2, 2, width), BF16, kind="Internal").ap()
                with (nc.sbuf_tensor(f"b_rep{layer}", [128, 2 * HALF * L], F32) as b_rep,
                      nc.sbuf_tensor(f"c_rep{layer}", [128, 2 * HALF * L], F32) as c_rep):
                    ssm_prep(nc, phases, inputs_loaded, rest_loaded, layer, L, x[layer], weights, b_rep, c_rep, split_dram)
                    y = hidden if layer == SSM_LAYERS - 1 else x[layer]
                    ssm_scan(nc, phases, inputs_loaded, layer, L, x[layer], y, weights, selector, a_neg, b_rep, c_rep,
                             split_dram)
                if layer < SSM_LAYERS - 1:
                    mean_of_pairs(nc, phases, layer, L, y, x[layer + 1])
        post(nc, phases, hidden, post_w)
        with ExitStack() as c2, nc.Block() as block:
            done = c2.enter_context(nc.semaphore("out_done"))

            @block.sync
            def _(sp):
                sp.dma_start(out, hidden[:, :]).then_inc(done, 16)
                sp.wait_ge(done, 16)


def ssm_layout(inp):
    import numpy as np
    f = np.float32
    x = np.asarray(inp["x"]).reshape(2, HALF, SEQ, D).transpose(0, 3, 1, 2).reshape(128, HALF * SEQ)
    w = np.zeros((128, SSM_W), f)
    A_log, Dp, Wdbc, Wdt, bdt = (np.asarray(inp["L0_tok_" + n]) for n in ("A_log", "D", "W_dbc", "W_dt", "b_dt"))
    for i in range(SSM_LAYERS):
        o = i * SSM_COLS
        for h in range(2):
            r = slice(64 * h, 64 * h + 64)
            w[r, o + 64 * h:o + 64 * h + 64] = Wdbc[i, 0][:, None]
            for c in range(2):
                w[r, o + SSM_WB + 128 * h + 64 * c:o + SSM_WB + 128 * h + 64 * c + 64] = Wdbc[i, 1:65].T
                w[r, o + SSM_WC + 128 * h + 64 * c:o + SSM_WC + 128 * h + 64 * c + 64] = Wdbc[i, 65:129].T
            w[r, o + SSM_VEC] = Wdt[i, :, 0]
            w[r, o + SSM_VEC + 1] = bdt[i]
            w[r, o + SSM_VEC + 2] = Dp[i]
            w[r, o + SSM_A:o + SSM_A + PAIRS] = A_log[i, h::2, :].T
        w[0:64, YSEL + 62] = 1
        w[64:128, YSEL + 63] = 1
    return {"x_in": np.ascontiguousarray(x), "ssm_w": w}


def post_layout(inp):
    import numpy as np
    f = np.float32
    W = np.zeros((128, PC.n), f)
    g = {k: np.asarray(v) for k, v in inp.items()}

    def at(name):
        o, n = PC.at[name]
        return W[:, o:o + n]

    def diag(name, m):
        at(name)[0:64, 0:64] = m
        at(name)[64:128, 64:128] = m

    def col(name, v):
        at(name)[0:64, 0] = v
        at(name)[64:128, 0] = v

    diag("mean", np.full((64, 64), 1 / 64, f))
    at("ident")[:] = np.eye(128, dtype=f)
    for e in (8, 16):
        at(f"rank{e}")[:] = e - np.arange(e, dtype=f)
    col("f0_gamma", g["L0_ffn_gamma"]); col("f0_beta", g["L0_ffn_beta"])
    col("a2_gamma", g["L2_attn_ln_gamma"]); col("a2_beta", g["L2_attn_ln_beta"])
    col("f3_gamma", g["L3_ffn_gamma"]); col("f3_beta", g["L3_ffn_beta"])
    wqkv, bqkv = g["L0_attn_W_qkv"], g["L0_attn_b_qkv"]
    att = {"L0": [wqkv[0:64].T, wqkv[64:128].T, wqkv[128:192].T, bqkv[0:64], bqkv[64:128], bqkv[128:192]],
           "L1": [g["L1_attn_Wq"].T, g["L1_attn_Wk"].T, g["L1_attn_Wv"].T, g["L1_attn_bq"], g["L1_attn_bk"], g["L1_attn_bv"]],
           "L2": [g["L2_attn_Wq"], g["L2_attn_Wk"], g["L2_attn_Wv"], g["L2_attn_bq"], g["L2_attn_bk"], g["L2_attn_bv"]],
           "L3": [g["L3_attn_Wq"].T, g["L3_attn_Wk"].T, g["L3_attn_Wv"].T, None, None, None]}
    scale = {"L0": 0.25, "L1": 1.0, "L2": 0.125, "L3": 0.125}
    for L, (wq, wk, wv, bq, bk, bv) in att.items():
        diag(L + "wq", wq); diag(L + "wk", wk); diag(L + "wv", wv)
        if bq is not None:
            col(L + "bq", bq); col(L + "bk", bk)
            at(L + "bv")[:, 0:64] = bv; at(L + "bv")[:, 64:128] = bv
        H = ATTN[L]["heads"]
        for v in range(2 * H):
            dh = 64 // H
            at(L + "mask")[v * dh:(v + 1) * dh, v] = scale[L]
    diag("L0wo", g["L0_attn_W_proj"].T); col("L0bo", g["L0_attn_b_proj"])
    diag("L2wo", g["L2_attn_Wout"]); col("L2bo", g["L2_attn_bout"])
    diag("L2wpos", g["L2_attn_Wpos"])
    pos = np.arange(TOK, dtype=f)[:, None]
    div = np.exp(np.arange(0, D, 2, dtype=f) * f(-np.log(10000.0) / D)).astype(f)
    pe = np.zeros((TOK, D), f)
    pe[:, 0::2] = np.sin(pos * div)
    pe[:, 1::2] = np.cos(pos * div)
    at("L2pe")[0:64] = pe.T; at("L2pe")[64:128] = pe.T
    col("L2u", g["L2_attn_u_bias"].reshape(64)); col("L2v", g["L2_attn_v_bias"].reshape(64))
    at("L1scale")[:, 0] = g["L1_attn_scale"][0]
    col("L2b2s", g["L2_ffn_b2s"])
    ffn = {"L0": ("L0_ffn_W1", "L0_ffn_b1", "L0_ffn_W2", "L0_ffn_b2", "L0_ffn_Wr"),
           "L1": ("L1_ffn_W1", "L1_ffn_b1", "L1_ffn_W2", "L1_ffn_b2", "L1_ffn_Wg"),
           "L2": ("L2_ffn_W1p", "L2_ffn_b1p", "L2_ffn_W2p", "L2_ffn_b2p", "L2_ffn_Wr"),
           "L3": ("L3_ffn_w1", "L3_ffn_b1", "L3_ffn_w2", "L3_ffn_b2", "L3_ffn_gate_w")}
    for L, names in ffn.items():
        W1, b1, W2, b2, wr = (g[n] for n in names)
        E, nbk = FFN[L]["E"], FFN[L]["blocks"]
        nblk = E * nbk + FFN[L]["shared"]
        o1, o2 = PC.at[L + "w1"][0], PC.at[L + "w2"][0]
        srcs = [(W1[e][:, k * 128:(k + 1) * 128], b1[e][k * 128:(k + 1) * 128], W2[e][k * 128:(k + 1) * 128]) for e in range(E) for k in range(nbk)]
        if L == "L2":
            srcs += [(g["L2_ffn_W1s"][:, k * 128:(k + 1) * 128], g["L2_ffn_b1s"][k * 128:(k + 1) * 128], g["L2_ffn_W2s"][k * 128:(k + 1) * 128]) for k in range(2)]
        for n, (a, b, c) in enumerate(srcs):
            W[0:64, o1 + n * 128:o1 + n * 128 + 128] = a
            W[64:128, o1 + (nblk + n) * 128:o1 + (nblk + n) * 128 + 128] = a
            at(L + "b1")[:, n] = b
            W[:, o2 + n * 64:o2 + n * 64 + 64] = c
        at(L + "b2")[0:E, 0:64] = b2
        at(L + "b2")[E:2 * E, 64:128] = b2
        at(L + "wr")[0:64, 0:E] = wr
        at(L + "wr")[64:128, E:2 * E] = wr
    at("L0br")[:, 0:8] = g["L0_ffn_br"]; at("L0br")[:, 8:16] = g["L0_ffn_br"]
    at("L1br")[:, 0:8] = g["L1_ffn_bg"]; at("L1br")[:, 8:16] = g["L1_ffn_bias"]
    at("L3br")[:, 0:16] = g["L3_ffn_gate_b"]
    return {"post_w": W}


def kernel(**inputs):
    import numpy as np
    import concourse.bacc as bacc
    from concourse.bass_utils import run_bass_kernel_spmd
    nc = bacc.Bacc("TRN2", target_bir_lowering=False, num_devices=1)
    arrays = {**ssm_layout(inputs), **post_layout(inputs)}
    aps = {n: nc.dram_tensor(n, a.shape, mybir.dt.from_np(a.dtype), kind="ExternalInput").ap() for n, a in arrays.items()}
    out = nc.dram_tensor("out", (128, COLS), F32, kind="ExternalOutput").ap()
    build(nc, aps["x_in"], aps["ssm_w"], aps["post_w"], out)
    r = run_bass_kernel_spmd(nc, [arrays], core_ids=[0])
    y = r.results[0]["out"]
    return np.ascontiguousarray(y.reshape(2, D, HALF, TOK).transpose(0, 2, 3, 1)).reshape(BATCH, TOK, D)
```
